# Optimizing a Trainium2 kernel written in Bass

```python
import numpy as np
import jax
import jax.numpy as jnp

def _softmax(x, axis=-1):
    return jax.nn.softmax(x, axis=axis)

def _gelu(x):
    return jax.nn.gelu(x, approximate=True)

def _silu(x):
    return jax.nn.silu(x)

def _sigmoid(x):
    return jax.nn.sigmoid(x)

def _layernorm(x, axis=-1, eps=1e-05):
    m = jnp.mean(x, axis=axis, keepdims=True)
    v = jnp.var(x, axis=axis, keepdims=True)
    return (x - m) / jnp.sqrt(v + eps)

def _scatter_add(tgt, idx, src, axis=0):
    return tgt.at[idx].add(src)

def _segment_sum(src, seg, n):
    return jax.ops.segment_sum(src, seg, n)
kernel_name = 'mk_flamingo_gated_d4_seqx_r4_6bbbd5'

def setup_inputs(seed: int=0):
    np.random.seed(seed)
    _w = jnp.asarray

    def _rec_inputs():
        import jax
        import jax.numpy as jnp
        _rk = jax.random.key(seed)
        x = -0.0002928 + 1 * jax.random.normal(jax.random.fold_in(_rk, 1), (8, 256, 256), jnp.float32)
        _lenS = 256 - jax.random.randint(jax.random.fold_in(_rk, 7), (8,), 0, max(1, 256 // 4) + 1, jnp.int32)
        _lenS2 = 77 - jax.random.randint(jax.random.fold_in(_rk, 8), (8,), 0, max(1, 77 // 4) + 1, jnp.int32)
        _ctx_1024P = jax.random.normal(jax.random.fold_in(_rk, 11), (8, 16, 256), jnp.float32)
        _ctx_1024c = jax.random.dirichlet(jax.random.fold_in(_rk, 511), 0.3 * jnp.ones((16,), jnp.float32), (8, 77))
        _ctx_1024t = jnp.einsum('bsk,bkd->bsd', _ctx_1024c, _ctx_1024P)
        _ctx_1024t = _ctx_1024t * jax.lax.rsqrt(jnp.mean(jnp.square(_ctx_1024t)) + 1e-12) * 0.953939
        ctx_1024 = -1.39393e-06 + 0.999914 * (_ctx_1024t + 0.3 * jax.random.normal(jax.random.fold_in(_rk, 611), (8, 77, 256), jnp.float32))
        _validS = jnp.arange(256)[None, :] < _lenS[:, None]
        _validS2 = jnp.arange(77)[None, :] < _lenS2[:, None]
        _causal = jnp.tril(jnp.ones((256, 256), dtype=bool))
        mask_BxSxS2_bf1 = jnp.ones((8, 256, 77), dtype=bool)
        _g = jax.random.normal(jax.random.fold_in(_rk, 9001), (2, 4), jnp.float32)
        _g = jnp.sign(_g) * jnp.maximum(jnp.abs(_g), 1.0) + (_g == 0) * 1.0
        g_xattn = _g[0]
        g_ffn = _g[1]
        return (x, ctx_1024, mask_BxSxS2_bf1, g_xattn, g_ffn)
    x, ctx_1024, mask_BxSxS2_bf1, g_xattn, g_ffn = _rec_inputs()

    def _L0_xattn_setup():
        import jax, jax.numpy as jnp
        import numpy as np
        D_MODEL = 256
        NUM_HEADS = 16
        D_K = D_MODEL // NUM_HEADS

        def _split_heads(x, B):
            return x.reshape(B, -1, NUM_HEADS, D_K).transpose(0, 2, 1, 3)
        key = jax.random.key(seed)
        ks = jax.random.split(key, 11)
        B, S = (2, 512)
        s = 1.0 / np.sqrt(D_MODEL)
        inp = {'Q': jax.random.normal(ks[0], (B, S, D_MODEL), jnp.float32), 'K': jax.random.normal(ks[1], (B, S, D_MODEL), jnp.float32), 'V': jax.random.normal(ks[2], (B, S, D_MODEL), jnp.float32), 'Wq': jax.random.normal(ks[3], (D_MODEL, D_MODEL), jnp.float32) * s, 'bq': jnp.zeros((D_MODEL,), jnp.float32), 'Wk': jax.random.normal(ks[4], (D_MODEL, D_MODEL), jnp.float32) * s, 'bk': jnp.zeros((D_MODEL,), jnp.float32), 'Wv': jax.random.normal(ks[5], (D_MODEL, D_MODEL), jnp.float32) * s, 'bv': jnp.zeros((D_MODEL,), jnp.float32), 'Wo': jax.random.normal(ks[6], (D_MODEL, D_MODEL), jnp.float32) * s, 'bo': jnp.zeros((D_MODEL,), jnp.float32)}
        return inp
    _L0_xattn_all = _L0_xattn_setup()
    _L0_xattn_in = {k: v for k, v in _L0_xattn_all.items() if k in ('Wq', 'bq', 'Wk', 'bk', 'Wv', 'bv', 'Wo', 'bo')}
    del _L0_xattn_all

    def _L0_ffn_setup():
        import jax, jax.numpy as jnp
        import numpy as np
        D = 256
        H = 512
        E = 8
        TOP_K = 2
        N_SHARED = 1
        B, S = (2, 256)
        key = jax.random.key(seed)
        ks = jax.random.split(key, 12)
        sc = 0.02
        return {'hidden': jax.random.normal(ks[0], (B, S, D), jnp.float32), 'router_w': jax.random.normal(ks[1], (D, E), jnp.float32) * sc, 'router_b': jnp.zeros((E,), jnp.float32), 'sw1': jax.random.normal(ks[2], (D, H), jnp.float32) * sc, 'sb1': jnp.zeros((H,), jnp.float32), 'sw2': jax.random.normal(ks[3], (H, D), jnp.float32) * sc, 'sb2': jnp.zeros((D,), jnp.float32), 'rw1': jax.random.normal(ks[4], (E, D, H), jnp.float32) * sc, 'rb1': jnp.zeros((E, H), jnp.float32), 'rw2': jax.random.normal(ks[5], (E, H, D), jnp.float32) * sc, 'rb2': jnp.zeros((E, D), jnp.float32)}
    _L0_ffn_all = _L0_ffn_setup()
    _L0_ffn_in = {k: v for k, v in _L0_ffn_all.items() if k in ('router_w', 'router_b', 'sw1', 'sb1', 'sw2', 'sb2', 'rw1', 'rb1', 'rw2', 'rb2')}
    del _L0_ffn_all

    def _L1_xattn_setup():
        import jax, jax.numpy as jnp
        import numpy as np
        DIM = 256
        HEADS = 16
        HEAD_DIM = 64
        INNER = HEADS * HEAD_DIM
        SCALE = 8.0
        LN_EPS = 1e-05
        NORM_EPS = 1e-12

        def layer_norm(x, g, b):
            m = jnp.mean(x, axis=-1, keepdims=True)
            v = jnp.mean((x - m) ** 2, axis=-1, keepdims=True)
            return (x - m) * jax.lax.rsqrt(v + LN_EPS) * g + b

        def l2_normalize(x):
            n = jnp.sqrt(jnp.sum(x * x, axis=-1, keepdims=True))
            return x / jnp.maximum(n, NORM_EPS)
        key = jax.random.key(seed)
        ks = jax.random.split(key, 8)
        B, N, T = (4, 1024, 64)
        s = 0.02
        return {'x': jax.random.normal(ks[0], (B, N, DIM), jnp.float32), 'context': jax.random.normal(ks[1], (B, T, DIM), jnp.float32), 'Wq': jax.random.normal(ks[2], (DIM, INNER), jnp.float32) * s, 'Wkv': jax.random.normal(ks[3], (DIM, 2 * INNER), jnp.float32) * s, 'Wo': jax.random.normal(ks[4], (INNER, DIM), jnp.float32) * s, 'null_kv': jax.random.normal(ks[5], (2, HEAD_DIM), jnp.float32), 'q_scale': jnp.ones((HEAD_DIM,), jnp.float32), 'k_scale': jnp.ones((HEAD_DIM,), jnp.float32), 'ln_in_g': jnp.ones((DIM,), jnp.float32), 'ln_in_b': jnp.zeros((DIM,), jnp.float32), 'ln_ctx_g': jnp.ones((DIM,), jnp.float32), 'ln_ctx_b': jnp.zeros((DIM,), jnp.float32), 'ln_out_g': jnp.ones((DIM,), jnp.float32), 'ln_out_b': jnp.zeros((DIM,), jnp.float32)}
    _L1_xattn_all = _L1_xattn_setup()
    _L1_xattn_in = {k: v for k, v in _L1_xattn_all.items() if k in ('Wq', 'Wkv', 'Wo', 'null_kv', 'q_scale', 'k_scale', 'ln_in_g', 'ln_in_b', 'ln_ctx_g', 'ln_ctx_b', 'ln_out_g', 'ln_out_b')}
    del _L1_xattn_all

    def _L1_ffn_setup():
        import jax, jax.numpy as jnp
        import numpy as np
        K = 2
        key = jax.random.key(seed)
        ks = jax.random.split(key, 7)
        B, S, D, E = (2, 512, 256, 8)
        H = 4 * D
        sd = 1.0 / np.sqrt(D)
        sh = 1.0 / np.sqrt(H)
        return {'x': jax.random.normal(ks[0], (B, S, D), jnp.float32), 'Wr': jax.random.normal(ks[1], (D, E), jnp.float32) * sd, 'br': jax.random.normal(ks[2], (E,), jnp.float32) * sd, 'W1': jax.random.normal(ks[3], (E, D, H), jnp.float32) * sd, 'b1': jax.random.normal(ks[4], (E, H), jnp.float32) * sd, 'W2': jax.random.normal(ks[5], (E, H, D), jnp.float32) * sh, 'b2': jax.random.normal(ks[6], (E, D), jnp.float32) * sh}
    _L1_ffn_all = _L1_ffn_setup()
    _L1_ffn_in = {k: v for k, v in _L1_ffn_all.items() if k in ('Wr', 'br', 'W1', 'b1', 'W2', 'b2')}
    del _L1_ffn_all

    def _L2_xattn_setup():
        import jax, jax.numpy as jnp
        import numpy as np
        NUM_HEAD = 16
        HEAD_DIM = 64
        QUERY_DIM = 256
        INNER = NUM_HEAD * HEAD_DIM
        key = jax.random.key(seed)
        ks = jax.random.split(key, 12)
        B, S = (4, 512)
        query = jax.random.normal(ks[0], (B, S, QUERY_DIM), dtype=jnp.float32)
        context = jax.random.normal(ks[1], (B, S, QUERY_DIM), dtype=jnp.float32)
        mask = jnp.ones((B, S, S), dtype=bool)
        s = 0.02
        Wq = jax.random.normal(ks[2], (QUERY_DIM, INNER), dtype=jnp.float32) * s
        bq = jnp.zeros((INNER,), dtype=jnp.float32)
        Wk = jax.random.normal(ks[3], (QUERY_DIM, INNER), dtype=jnp.float32) * s
        bk = jnp.zeros((INNER,), dtype=jnp.float32)
        Wv = jax.random.normal(ks[4], (QUERY_DIM, INNER), dtype=jnp.float32) * s
        bv = jnp.zeros((INNER,), dtype=jnp.float32)
        Wo = jax.random.normal(ks[5], (INNER, QUERY_DIM), dtype=jnp.float32) * s
        bo = jnp.zeros((QUERY_DIM,), dtype=jnp.float32)
        return {'query': query, 'context': context, 'mask': mask, 'Wq': Wq, 'bq': bq, 'Wk': Wk, 'bk': bk, 'Wv': Wv, 'bv': bv, 'Wo': Wo, 'bo': bo}
    _L2_xattn_all = _L2_xattn_setup()
    _L2_xattn_in = {k: v for k, v in _L2_xattn_all.items() if k in ('Wq', 'bq', 'Wk', 'bk', 'Wv', 'bv', 'Wo', 'bo')}
    del _L2_xattn_all

    def _L2_ffn_setup():
        import jax, jax.numpy as jnp
        import numpy as np
        B, S, D, F, E, R = (4, 512, 256, 1024, 8, 4)
        key = jax.random.key(seed)
        ks = jax.random.split(key, 8)
        s_in = 1.0 / np.sqrt(D)
        s_ff = 1.0 / np.sqrt(F)
        return {'hidden_states': jax.random.normal(ks[0], (B, S, D), jnp.float32), 'gate_W': jax.random.normal(ks[1], (E, D), jnp.float32) * s_in, 'gate_b': jnp.zeros((E,), jnp.float32), 'wi_W': jax.random.normal(ks[2], (F, D), jnp.float32) * s_in, 'wi_b': jnp.zeros((F,), jnp.float32), 'wo_W': jax.random.normal(ks[3], (D, F), jnp.float32) * s_ff, 'wo_b': jnp.zeros((D,), jnp.float32), 'lora_A': jax.random.normal(ks[4], (E, R, D), jnp.float32) * s_in, 'lora_B': jax.random.normal(ks[5], (E, F, R), jnp.float32) * 0.02}
    _L2_ffn_all = _L2_ffn_setup()
    _L2_ffn_in = {k: v for k, v in _L2_ffn_all.items() if k in ('gate_W', 'gate_b', 'wi_W', 'wi_b', 'wo_W', 'wo_b', 'lora_A', 'lora_B')}
    del _L2_ffn_all

    def _L3_xattn_setup():
        import jax, jax.numpy as jnp
        import numpy as np
        EMBED_DIM = 256
        NUM_HEADS = 16
        HEAD_DIM = EMBED_DIM // NUM_HEADS
        WINDOW = 128
        B, S_Q, S_K = (2, 512, 512)

        def apply_rope(x):
            Dh = x.shape[-1]
            half = Dh // 2
            pos = jnp.arange(x.shape[2], dtype=jnp.float32)
            inv_freq = 1.0 / 10000.0 ** (jnp.arange(0, half, dtype=jnp.float32) / half)
            ang = pos[:, None] * inv_freq[None, :]
            cos = jnp.cos(ang)[None, None, :, :].astype(x.dtype)
            sin = jnp.sin(ang)[None, None, :, :].astype(x.dtype)
            x1, x2 = (x[..., :half], x[..., half:])
            return jnp.concatenate([x1 * cos - x2 * sin, x1 * sin + x2 * cos], axis=-1)
        key = jax.random.key(seed)
        ks = jax.random.split(key, 11)
        scale = 1.0 / np.sqrt(EMBED_DIM)
        inp = {'query': jax.random.normal(ks[0], (B, S_Q, EMBED_DIM), jnp.float32), 'key': jax.random.normal(ks[1], (B, S_K, EMBED_DIM), jnp.float32), 'value': jax.random.normal(ks[2], (B, S_K, EMBED_DIM), jnp.float32), 'Wq': jax.random.normal(ks[3], (EMBED_DIM, EMBED_DIM), jnp.float32) * scale, 'bq': jnp.zeros((EMBED_DIM,), jnp.float32), 'Wk': jax.random.normal(ks[4], (EMBED_DIM, EMBED_DIM), jnp.float32) * scale, 'bk': jnp.zeros((EMBED_DIM,), jnp.float32), 'Wv': jax.random.normal(ks[5], (EMBED_DIM, EMBED_DIM), jnp.float32) * scale, 'bv': jnp.zeros((EMBED_DIM,), jnp.float32), 'Wo': jax.random.normal(ks[6], (EMBED_DIM, EMBED_DIM), jnp.float32) * scale, 'bo': jnp.zeros((EMBED_DIM,), jnp.float32)}
        return inp
    _L3_xattn_all = _L3_xattn_setup()
    _L3_xattn_in = {k: v for k, v in _L3_xattn_all.items() if k in ('Wq', 'bq', 'Wk', 'bk', 'Wv', 'bv', 'Wo', 'bo')}
    del _L3_xattn_all

    def _L3_ffn_setup():
        import jax, jax.numpy as jnp
        import numpy as np
        DIM = 256
        INTER = 256
        N_EXPERTS = 8
        TOPK = 2
        N_SHARED = 2
        key = jax.random.key(seed)
        ks = jax.random.split(key, 10)
        s = 0.02
        return {'x': jax.random.normal(ks[0], (4, 512, DIM), dtype=jnp.float32), 'gate_w': jax.random.normal(ks[1], (N_EXPERTS, DIM), dtype=jnp.float32) * s, 'gate_bias': jax.random.normal(ks[2], (N_EXPERTS,), dtype=jnp.float32) * s, 'w1': jax.random.normal(ks[3], (N_EXPERTS, INTER, DIM), dtype=jnp.float32) * s, 'w3': jax.random.normal(ks[4], (N_EXPERTS, INTER, DIM), dtype=jnp.float32) * s, 'w2': jax.random.normal(ks[5], (N_EXPERTS, DIM, INTER), dtype=jnp.float32) * s, 'sw1': jax.random.normal(ks[6], (N_SHARED * INTER, DIM), dtype=jnp.float32) * s, 'sw3': jax.random.normal(ks[7], (N_SHARED * INTER, DIM), dtype=jnp.float32) * s, 'sw2': jax.random.normal(ks[8], (DIM, N_SHARED * INTER), dtype=jnp.float32) * s}
    _L3_ffn_all = _L3_ffn_setup()
    _L3_ffn_in = {k: v for k, v in _L3_ffn_all.items() if k in ('gate_w', 'gate_bias', 'w1', 'w3', 'w2', 'sw1', 'sw3', 'sw2')}
    del _L3_ffn_all
    return {'x': x, 'ctx_1024': ctx_1024, 'mask_BxSxS2_bf1': mask_BxSxS2_bf1, 'g_xattn': g_xattn, 'g_ffn': g_ffn, 'L0_xattn_Wq': _L0_xattn_in['Wq'], 'L0_xattn_bq': _L0_xattn_in['bq'], 'L0_xattn_Wk': _L0_xattn_in['Wk'], 'L0_xattn_bk': _L0_xattn_in['bk'], 'L0_xattn_Wv': _L0_xattn_in['Wv'], 'L0_xattn_bv': _L0_xattn_in['bv'], 'L0_xattn_Wo': _L0_xattn_in['Wo'], 'L0_xattn_bo': _L0_xattn_in['bo'], 'L0_ffn_router_w': _L0_ffn_in['router_w'], 'L0_ffn_router_b': _L0_ffn_in['router_b'], 'L0_ffn_sw1': _L0_ffn_in['sw1'], 'L0_ffn_sb1': _L0_ffn_in['sb1'], 'L0_ffn_sw2': _L0_ffn_in['sw2'], 'L0_ffn_sb2': _L0_ffn_in['sb2'], 'L0_ffn_rw1': _L0_ffn_in['rw1'], 'L0_ffn_rb1': _L0_ffn_in['rb1'], 'L0_ffn_rw2': _L0_ffn_in['rw2'], 'L0_ffn_rb2': _L0_ffn_in['rb2'], 'L1_xattn_Wq': _L1_xattn_in['Wq'], 'L1_xattn_Wkv': _L1_xattn_in['Wkv'], 'L1_xattn_Wo': _L1_xattn_in['Wo'], 'L1_xattn_null_kv': _L1_xattn_in['null_kv'], 'L1_xattn_q_scale': _L1_xattn_in['q_scale'], 'L1_xattn_k_scale': _L1_xattn_in['k_scale'], 'L1_xattn_ln_in_g': _L1_xattn_in['ln_in_g'], 'L1_xattn_ln_in_b': _L1_xattn_in['ln_in_b'], 'L1_xattn_ln_ctx_g': _L1_xattn_in['ln_ctx_g'], 'L1_xattn_ln_ctx_b': _L1_xattn_in['ln_ctx_b'], 'L1_xattn_ln_out_g': _L1_xattn_in['ln_out_g'], 'L1_xattn_ln_out_b': _L1_xattn_in['ln_out_b'], 'L1_ffn_Wr': _L1_ffn_in['Wr'], 'L1_ffn_br': _L1_ffn_in['br'], 'L1_ffn_W1': _L1_ffn_in['W1'], 'L1_ffn_b1': _L1_ffn_in['b1'], 'L1_ffn_W2': _L1_ffn_in['W2'], 'L1_ffn_b2': _L1_ffn_in['b2'], 'L2_xattn_Wq': _L2_xattn_in['Wq'], 'L2_xattn_bq': _L2_xattn_in['bq'], 'L2_xattn_Wk': _L2_xattn_in['Wk'], 'L2_xattn_bk': _L2_xattn_in['bk'], 'L2_xattn_Wv': _L2_xattn_in['Wv'], 'L2_xattn_bv': _L2_xattn_in['bv'], 'L2_xattn_Wo': _L2_xattn_in['Wo'], 'L2_xattn_bo': _L2_xattn_in['bo'], 'L2_ffn_gate_W': _L2_ffn_in['gate_W'], 'L2_ffn_gate_b': _L2_ffn_in['gate_b'], 'L2_ffn_wi_W': _L2_ffn_in['wi_W'], 'L2_ffn_wi_b': _L2_ffn_in['wi_b'], 'L2_ffn_wo_W': _L2_ffn_in['wo_W'], 'L2_ffn_wo_b': _L2_ffn_in['wo_b'], 'L2_ffn_lora_A': _L2_ffn_in['lora_A'], 'L2_ffn_lora_B': _L2_ffn_in['lora_B'], 'L3_xattn_Wq': _L3_xattn_in['Wq'], 'L3_xattn_bq': _L3_xattn_in['bq'], 'L3_xattn_Wk': _L3_xattn_in['Wk'], 'L3_xattn_bk': _L3_xattn_in['bk'], 'L3_xattn_Wv': _L3_xattn_in['Wv'], 'L3_xattn_bv': _L3_xattn_in['bv'], 'L3_xattn_Wo': _L3_xattn_in['Wo'], 'L3_xattn_bo': _L3_xattn_in['bo'], 'L3_ffn_gate_w': _L3_ffn_in['gate_w'], 'L3_ffn_gate_bias': _L3_ffn_in['gate_bias'], 'L3_ffn_w1': _L3_ffn_in['w1'], 'L3_ffn_w3': _L3_ffn_in['w3'], 'L3_ffn_w2': _L3_ffn_in['w2'], 'L3_ffn_sw1': _L3_ffn_in['sw1'], 'L3_ffn_sw3': _L3_ffn_in['sw3'], 'L3_ffn_sw2': _L3_ffn_in['sw2']}

def reference(x, ctx_1024, mask_BxSxS2_bf1, g_xattn, g_ffn, L0_xattn_Wq, L0_xattn_bq, L0_xattn_Wk, L0_xattn_bk, L0_xattn_Wv, L0_xattn_bv, L0_xattn_Wo, L0_xattn_bo, L0_ffn_router_w, L0_ffn_router_b, L0_ffn_sw1, L0_ffn_sb1, L0_ffn_sw2, L0_ffn_sb2, L0_ffn_rw1, L0_ffn_rb1, L0_ffn_rw2, L0_ffn_rb2, L1_xattn_Wq, L1_xattn_Wkv, L1_xattn_Wo, L1_xattn_null_kv, L1_xattn_q_scale, L1_xattn_k_scale, L1_xattn_ln_in_g, L1_xattn_ln_in_b, L1_xattn_ln_ctx_g, L1_xattn_ln_ctx_b, L1_xattn_ln_out_g, L1_xattn_ln_out_b, L1_ffn_Wr, L1_ffn_br, L1_ffn_W1, L1_ffn_b1, L1_ffn_W2, L1_ffn_b2, L2_xattn_Wq, L2_xattn_bq, L2_xattn_Wk, L2_xattn_bk, L2_xattn_Wv, L2_xattn_bv, L2_xattn_Wo, L2_xattn_bo, L2_ffn_gate_W, L2_ffn_gate_b, L2_ffn_wi_W, L2_ffn_wi_b, L2_ffn_wo_W, L2_ffn_wo_b, L2_ffn_lora_A, L2_ffn_lora_B, L3_xattn_Wq, L3_xattn_bq, L3_xattn_Wk, L3_xattn_bk, L3_xattn_Wv, L3_xattn_bv, L3_xattn_Wo, L3_xattn_bo, L3_ffn_gate_w, L3_ffn_gate_bias, L3_ffn_w1, L3_ffn_w3, L3_ffn_w2, L3_ffn_sw1, L3_ffn_sw3, L3_ffn_sw2):
    import jax
    import jax.numpy as jnp

    def _L0_xattn_ref(Q, K, V, Wq, bq, Wk, bk, Wv, bv, Wo, bo):
        import jax, jax.numpy as jnp
        import numpy as np
        D_MODEL = 256
        NUM_HEADS = 16
        D_K = D_MODEL // NUM_HEADS

        def _split_heads(x, B):
            return x.reshape(B, -1, NUM_HEADS, D_K).transpose(0, 2, 1, 3)
        B, S, _ = Q.shape
        q = _split_heads(Q @ Wq.T + bq, B)
        k = _split_heads(K @ Wk.T + bk, B)
        v = _split_heads(V @ Wv.T + bv, B)
        scale = 1.0 / jnp.sqrt(jnp.asarray(D_K, q.dtype))
        scores = jnp.einsum('bhqd,bhkd->bhqk', q, k) * scale
        attn = jax.nn.softmax(scores, axis=-1)
        ctx = jnp.einsum('bhqk,bhkd->bhqd', attn, v)
        ctx = ctx.transpose(0, 2, 1, 3).reshape(B, S, D_MODEL)
        out = ctx @ Wo.T + bo
        return out

    def _L0_ffn_ref(hidden, router_w, router_b, sw1, sb1, sw2, sb2, rw1, rb1, rw2, rb2):
        import jax, jax.numpy as jnp
        import numpy as np
        D = 256
        H = 512
        E = 8
        TOP_K = 2
        N_SHARED = 1
        B, S = (2, 256)
        b, s, d = hidden.shape
        T = b * s
        flat = hidden.reshape(T, d)
        router_logits = flat @ router_w + router_b
        router_probs = jax.nn.softmax(router_logits, axis=-1)
        topk_probs, topk_idx = jax.lax.top_k(router_probs, TOP_K)
        weights = jnp.zeros_like(router_probs).at[jnp.arange(T)[:, None], topk_idx].add(topk_probs)
        sh = jax.nn.gelu(flat @ sw1 + sb1, approximate=False)
        shared_out = (sh @ sw2 + sb2) / N_SHARED
        h1 = jax.nn.gelu(jnp.einsum('td,edh->teh', flat, rw1) + rb1[None], approximate=False)
        expert_out = jnp.einsum('teh,ehd->ted', h1, rw2) + rb2[None]
        mixed = jnp.einsum('ted,te->td', expert_out, weights)
        return (shared_out + mixed).reshape(b, s, d)

    def _L1_xattn_ref(x, context, Wq, Wkv, Wo, null_kv, q_scale, k_scale, ln_in_g, ln_in_b, ln_ctx_g, ln_ctx_b, ln_out_g, ln_out_b):
        import jax, jax.numpy as jnp
        import numpy as np
        DIM = 256
        HEADS = 16
        HEAD_DIM = 64
        INNER = HEADS * HEAD_DIM
        SCALE = 8.0
        LN_EPS = 1e-05
        NORM_EPS = 1e-12

        def layer_norm(x, g, b):
            m = jnp.mean(x, axis=-1, keepdims=True)
            v = jnp.mean((x - m) ** 2, axis=-1, keepdims=True)
            return (x - m) * jax.lax.rsqrt(v + LN_EPS) * g + b

        def l2_normalize(x):
            n = jnp.sqrt(jnp.sum(x * x, axis=-1, keepdims=True))
            return x / jnp.maximum(n, NORM_EPS)
        B, N, _ = x.shape
        T = context.shape[1]
        xn = layer_norm(x, ln_in_g, ln_in_b)
        cn = layer_norm(context, ln_ctx_g, ln_ctx_b)
        q = xn @ Wq
        kv = cn @ Wkv
        k, v = jnp.split(kv, 2, axis=-1)

        def split_heads(t):
            b, s, _ = t.shape
            return t.reshape(b, s, HEADS, HEAD_DIM).transpose(0, 2, 1, 3)
        q, k, v = (split_heads(q), split_heads(k), split_heads(v))
        nk = jnp.broadcast_to(null_kv[0], (B, HEADS, 1, HEAD_DIM))
        nv = jnp.broadcast_to(null_kv[1], (B, HEADS, 1, HEAD_DIM))
        k = jnp.concatenate([k, nk], axis=2)
        v = jnp.concatenate([v, nv], axis=2)
        q = l2_normalize(q) * q_scale
        k = l2_normalize(k) * k_scale
        scores = jnp.einsum('bhid,bhkd->bhik', q, k) * SCALE
        attn = jax.nn.softmax(scores, axis=-1)
        out = jnp.einsum('bhik,bhkd->bhid', attn, v)
        out = out.transpose(0, 2, 1, 3).reshape(B, N, INNER)
        out = out @ Wo
        return layer_norm(out, ln_out_g, ln_out_b)

    def _L1_ffn_ref(x, Wr, br, W1, b1, W2, b2):
        import jax, jax.numpy as jnp
        import numpy as np
        K = 2
        E = Wr.shape[-1]
        scores = jnp.einsum('bsd,de->bse', x, Wr) + br
        _, topk_idx = jax.lax.top_k(scores, K)
        indicator = jax.nn.one_hot(topk_idx, E, dtype=scores.dtype).sum(-2)
        neg_inf = jnp.asarray(-jnp.inf, scores.dtype)
        weights = jax.nn.softmax(jnp.where(indicator > 0, scores, neg_inf), axis=-1)
        out = jnp.zeros_like(x)
        for i in range(E):
            xi = x * indicator[..., i:i + 1]
            h = jax.nn.relu(jnp.einsum('bsd,dh->bsh', xi, W1[i]) + b1[i])
            yi = jnp.einsum('bsh,hd->bsd', h, W2[i]) + b2[i]
            out = out + yi * weights[..., i:i + 1]
        return out

    def _L2_xattn_ref(query, context, mask, Wq, bq, Wk, bk, Wv, bv, Wo, bo):
        import jax, jax.numpy as jnp
        import numpy as np
        NUM_HEAD = 16
        HEAD_DIM = 64
        QUERY_DIM = 256
        INNER = NUM_HEAD * HEAD_DIM
        B, q_len, _ = query.shape
        c_len = context.shape[1]
        q = (query @ Wq + bq).reshape(B, q_len, NUM_HEAD, HEAD_DIM)
        k = (context @ Wk + bk).reshape(B, c_len, NUM_HEAD, HEAD_DIM)
        v = (context @ Wv + bv).reshape(B, c_len, NUM_HEAD, HEAD_DIM)
        energy = jnp.einsum('bqhd,bkhd->bhqk', q, k) / HEAD_DIM ** 0.5
        energy = jnp.where(mask[:, None, :, :], energy, -1000000000.0)
        attention = jax.nn.softmax(energy, axis=-1)
        out = jnp.einsum('bhqc,bchd->bqhd', attention, v).reshape(B, q_len, INNER)
        return out @ Wo + bo

    def _L2_ffn_ref(hidden_states, gate_W, gate_b, wi_W, wi_b, wo_W, wo_b, lora_A, lora_B):
        import jax, jax.numpy as jnp
        import numpy as np
        B, S, D, F, E, R = (4, 512, 256, 1024, 8, 4)
        x = hidden_states
        logits = jnp.einsum('bsd,ed->bse', x, gate_W) + gate_b
        top1 = jnp.argmax(jax.nn.softmax(logits, axis=-1), axis=-1)
        base = jnp.einsum('bsd,fd->bsf', x, wi_W) + wi_b
        out = jnp.zeros_like(x)
        for i in range(lora_A.shape[0]):
            lora = jnp.einsum('bsr,fr->bsf', jnp.einsum('bsd,rd->bsr', x, lora_A[i]), lora_B[i])
            inter = jax.nn.relu(base + lora)
            expert_out = jnp.einsum('bsf,df->bsd', inter, wo_W) + wo_b
            mask = (top1 == i).astype(x.dtype)[..., None]
            out = out + mask * expert_out
        return out

    def _L3_xattn_ref(query, key, value, Wq, bq, Wk, bk, Wv, bv, Wo, bo):
        import jax, jax.numpy as jnp
        import numpy as np
        EMBED_DIM = 256
        NUM_HEADS = 16
        HEAD_DIM = EMBED_DIM // NUM_HEADS
        WINDOW = 128
        B, S_Q, S_K = (2, 512, 512)

        def apply_rope(x):
            Dh = x.shape[-1]
            half = Dh // 2
            pos = jnp.arange(x.shape[2], dtype=jnp.float32)
            inv_freq = 1.0 / 10000.0 ** (jnp.arange(0, half, dtype=jnp.float32) / half)
            ang = pos[:, None] * inv_freq[None, :]
            cos = jnp.cos(ang)[None, None, :, :].astype(x.dtype)
            sin = jnp.sin(ang)[None, None, :, :].astype(x.dtype)
            x1, x2 = (x[..., :half], x[..., half:])
            return jnp.concatenate([x1 * cos - x2 * sin, x1 * sin + x2 * cos], axis=-1)
        Bq, Sq, D = query.shape
        Sk = key.shape[1]
        H, Dh = (NUM_HEADS, HEAD_DIM)

        def proj(x, W, b):
            return (x @ W.T + b).reshape(x.shape[0], x.shape[1], H, Dh).transpose(0, 2, 1, 3)
        q = apply_rope(proj(query, Wq, bq))
        k = apply_rope(proj(key, Wk, bk))
        v = proj(value, Wv, bv)
        q = q * Dh ** (-0.5)
        scores = jnp.einsum('bhqd,bhkd->bhqk', q, k)
        q_idx = jnp.arange(Sq)[:, None]
        kv_idx = jnp.arange(Sk)[None, :]
        rel = kv_idx - q_idx
        mask = (rel > 0) | (rel < -WINDOW)
        mask4 = mask[None, None, :, :]
        neg = jnp.finfo(scores.dtype).min
        scores = jnp.where(mask4, neg, scores)
        probs = jax.nn.softmax(scores, axis=-1)
        all_masked = jnp.all(mask4, axis=-1, keepdims=True)
        probs = jnp.where(all_masked, jnp.zeros((), probs.dtype), probs)
        out = jnp.einsum('bhqk,bhkd->bhqd', probs, v)
        out = out.transpose(0, 2, 1, 3).reshape(Bq, Sq, D)
        return out @ Wo.T + bo

    def _L3_ffn_ref(x, gate_w, gate_bias, w1, w3, w2, sw1, sw3, sw2):
        import jax, jax.numpy as jnp
        import numpy as np
        DIM = 256
        INTER = 256
        N_EXPERTS = 8
        TOPK = 2
        N_SHARED = 2
        shape = x.shape
        xt = x.reshape(-1, shape[-1])
        scores = jax.nn.softmax((xt @ gate_w.T).astype(jnp.float32), axis=-1)
        _, idx = jax.lax.top_k(scores + gate_bias, TOPK)
        weights = jnp.take_along_axis(scores, idx, axis=1).astype(x.dtype)
        y = jnp.zeros_like(xt)
        for e in range(N_EXPERTS):
            gate_e = jnp.sum(jnp.where(idx == e, weights, 0.0), axis=1)
            h = jax.nn.silu(xt @ w1[e].T) * (xt @ w3[e].T)
            y = y + gate_e[:, None] * (h @ w2[e].T)
        z = jax.nn.silu(xt @ sw1.T) * (xt @ sw3.T) @ sw2.T
        return (y + z).reshape(shape)
    x = x + jnp.tanh(g_xattn[0]) * _L0_xattn_ref(_layernorm(x, axis=-1), ctx_1024, ctx_1024, L0_xattn_Wq, L0_xattn_bq, L0_xattn_Wk, L0_xattn_bk, L0_xattn_Wv, L0_xattn_bv, L0_xattn_Wo, L0_xattn_bo)
    x = x + jnp.tanh(g_ffn[0]) * _L0_ffn_ref(_layernorm(x, axis=-1), L0_ffn_router_w, L0_ffn_router_b, L0_ffn_sw1, L0_ffn_sb1, L0_ffn_sw2, L0_ffn_sb2, L0_ffn_rw1, L0_ffn_rb1, L0_ffn_rw2, L0_ffn_rb2)
    x = x + jnp.tanh(g_xattn[1]) * _L1_xattn_ref(_layernorm(x, axis=-1), ctx_1024, L1_xattn_Wq, L1_xattn_Wkv, L1_xattn_Wo, L1_xattn_null_kv, L1_xattn_q_scale, L1_xattn_k_scale, L1_xattn_ln_in_g, L1_xattn_ln_in_b, L1_xattn_ln_ctx_g, L1_xattn_ln_ctx_b, L1_xattn_ln_out_g, L1_xattn_ln_out_b)
    x = x + jnp.tanh(g_ffn[1]) * _L1_ffn_ref(_layernorm(x, axis=-1), L1_ffn_Wr, L1_ffn_br, L1_ffn_W1, L1_ffn_b1, L1_ffn_W2, L1_ffn_b2)
    x = x + jnp.tanh(g_xattn[2]) * _L2_xattn_ref(_layernorm(x, axis=-1), ctx_1024, mask_BxSxS2_bf1, L2_xattn_Wq, L2_xattn_bq, L2_xattn_Wk, L2_xattn_bk, L2_xattn_Wv, L2_xattn_bv, L2_xattn_Wo, L2_xattn_bo)
    x = x + jnp.tanh(g_ffn[2]) * _L2_ffn_ref(_layernorm(x, axis=-1), L2_ffn_gate_W, L2_ffn_gate_b, L2_ffn_wi_W, L2_ffn_wi_b, L2_ffn_wo_W, L2_ffn_wo_b, L2_ffn_lora_A, L2_ffn_lora_B)
    x = x + jnp.tanh(g_xattn[3]) * _L3_xattn_ref(_layernorm(x, axis=-1), ctx_1024, ctx_1024, L3_xattn_Wq, L3_xattn_bq, L3_xattn_Wk, L3_xattn_bk, L3_xattn_Wv, L3_xattn_bv, L3_xattn_Wo, L3_xattn_bo)
    x = x + jnp.tanh(g_ffn[3]) * _L3_ffn_ref(_layernorm(x, axis=-1), L3_ffn_gate_w, L3_ffn_gate_bias, L3_ffn_w1, L3_ffn_w3, L3_ffn_w2, L3_ffn_sw1, L3_ffn_sw3, L3_ffn_sw2)
    return x

_drawn_inputs = setup_inputs


def setup_inputs(seed=0):
    import zlib

    import numpy as np

    out = dict(_drawn_inputs(seed))
    spreads = {'L0_xattn_bq': (0.0, 0.1),
     'L0_xattn_bk': (0.0, 2.0),
     'L0_xattn_bv': (0.0, 0.1),
     'L0_xattn_bo': (0.0, 0.1),
     'L0_ffn_router_b': (0.0, 0.393),
     'L0_ffn_sb1': (0.0, 0.1),
     'L0_ffn_sb2': (0.0, 0.1),
     'L0_ffn_rb1': (0.0, 0.793),
     'L0_ffn_rb2': (0.0, 0.1),
     'L1_xattn_q_scale': (1.0, 0.2),
     'L1_xattn_k_scale': (1.0, 0.2),
     'L1_xattn_ln_in_g': (1.0, 0.2),
     'L1_xattn_ln_in_b': (0.0, 0.1),
     'L1_xattn_ln_ctx_g': (1.0, 0.2),
     'L1_xattn_ln_ctx_b': (0.0, 0.1),
     'L1_xattn_ln_out_g': (1.0, 0.2),
     'L1_xattn_ln_out_b': (0.0, 0.1),
     'L2_xattn_bq': (0.0, 0.8),
     'L2_xattn_bk': (0.0, 2.0),
     'L2_xattn_bv': (0.0, 0.1),
     'L2_xattn_bo': (0.0, 0.1),
     'L2_ffn_gate_b': (0.0, 0.8),
     'L2_ffn_wi_b': (0.0, 0.1),
     'L2_ffn_wo_b': (0.0, 0.1),
     'L3_xattn_bq': (0.0, 0.763),
     'L3_xattn_bk': (0.0, 0.8),
     'L3_xattn_bv': (0.0, 0.1),
     'L3_xattn_bo': (0.0, 0.1)}
    factors = {'g_ffn': 35.872,
     'L1_ffn_b1': 2.861,
     'L1_ffn_b2': 3.953,
     'L2_xattn_Wq': 8.0,
     'L2_xattn_Wk': 8.0,
     'L2_ffn_gate_W': 4.438,
     'L2_ffn_lora_A': 4.282,
     'L2_ffn_lora_B': 4.374,
     'L3_ffn_gate_w': 8.0,
     'L3_ffn_gate_bias': 8.0,
     'L3_ffn_w1': 8.0,
     'L3_ffn_w3': 8.0,
     'L3_ffn_w2': 8.0,
     'L3_ffn_sw1': 4.506,
     'L3_ffn_sw3': 4.496,
     'L3_ffn_sw2': 4.486}
    for name, (base, spread) in spreads.items():
        noise = np.random.default_rng([zlib.crc32(name.encode()), seed]).standard_normal(out[name].shape)
        drawn = base * np.exp(spread * noise) if base else spread * noise
        out[name] = jnp.asarray(drawn.astype(out[name].dtype))
    for name, factor in factors.items():
        out[name] = (out[name] * factor).astype(out[name].dtype)
    return out
```

```python
from contextlib import ExitStack

import concourse.bass as bass
import numpy as np
from concourse import mybir

F32 = mybir.dt.float32
F32R = mybir.dt.float32r
U8 = mybir.dt.uint8
ACT = mybir.ActivationFunctionType
ALU = mybir.AluOpType
AX = mybir.AxisListType

P = 128
NBATCH = 8
SEQ = 256
D = 256
DC = D // P
TOKENS = NBATCH * SEQ
TILES = TOKENS // P
TPB = SEQ // P
CTX = 77
HEADS = 16
GROUP = 4
GROUPS = HEADS // GROUP
EPS = 1e-5
BANK = 512
UNIT = 512
CHUNK = 512
CHUNKS = TOKENS // CHUNK
HUGE = 3.0e38
MASKED = -1.0e30
L2_FILL = -1.0e9

ATTN = [
    dict(name="a0", hd=16, keys=CTX, scale=0.25, rope=False, l2norm=False, mask=None),
    dict(name="a1", hd=64, keys=CTX + 1, scale=8.0, rope=False, l2norm=True, mask=None),
    dict(name="a2", hd=64, keys=CTX, scale=0.125, rope=False, l2norm=False, mask="given"),
    dict(name="a3", hd=16, keys=CTX, scale=0.25, rope=True, l2norm=False, mask="window"),
]
FFN = [
    dict(name="f0", units=9, per_expert=1, experts=8, gates=9, bias_rows=9, lora=0, act="gelu"),
    dict(name="f1", units=16, per_expert=2, experts=8, gates=8, bias_rows=8, lora=0, act="relu"),
    dict(name="f2", units=2, per_expert=2, experts=8, gates=1, bias_rows=1, lora=4, act="relu"),
    dict(name="f3", units=10, per_expert=1, experts=8, gates=10, bias_rows=0, lora=0, act="silu"),
]


class Tally:

    def __init__(self, sem, per=0, base=0):
        self.sem, self.per, self.base, self.k, self.i = sem, per, base, 0, 0

    def round(self, i):
        self.i, self.k = i, 0

    def add(self, ins):
        ins.then_inc(self.sem, 1)
        self.k += 1

    def value(self):
        return self.i * self.per + (self.base + self.k)


class Step:

    def __init__(self, engine, sem, per=0, base=0):
        self.engine, self.t = engine, Tally(sem, per, base)

    def round(self, i):
        self.t.round(i)

    def did(self, ins):
        self.t.add(ins)

    def then(self, ins):
        self.t.add(ins)
        self.engine.wait_ge(self.t.sem, self.t.value())

    def filled(self):
        self.t.base, self.t.k = self.t.base + self.t.k, 0

    def check(self):
        assert self.t.k == self.t.per, (self.t.k, self.t.per)


def build(nc, dram, out, stages):
    with ExitStack() as whole:

        in_use = []

        def sem(name):
            in_use.append(nc.alloc_semaphore(name=name))
            return in_use[-1]

        def clear_semaphores():
            nc.clear_and_free_semaphores(in_use)
            nc.all_engine_barrier()
            in_use.clear()

        def resident(name, shape, dt=F32):
            return whole.enter_context(nc.sbuf_tensor(name, shape, dt))

        psum = whole.enter_context(nc.psum_tensor("psum", [P, 8, BANK], F32))
        x = resident("residual", [P, TILES, D])
        ident = resident("identity", [P, P])
        half = resident("half", [P, TILES])
        zero = resident("zero", [P, 1])
        half32 = resident("half32", [P, TPB * HEADS])
        ctxT = resident("ctx_features", [P, DC, NBATCH * CTX])
        g_all = resident("g_all", [P, 8])
        tg = resident("tg", [P, 8])
        rank = resident("ranks", [P, TILES, 8])
        stats = resident("stats", [P, TILES, 6])
        mv = resident("mv", [P, TILES, 2])
        var = resident("var", [P, TILES])
        rstd = resident("rstd", [P, TILES])

        env = dict(nc=nc, dram=dram, sem=sem, psum=psum, x=x, ident=ident, half=half, zero=zero, half32=half32, ctxT=ctxT, tg=tg,
                   rank=rank, stats=stats, mv=mv, var=var, rstd=rstd)
        setup(env, g_all)
        for kind, n in stages:
            with ExitStack() as scope:
                if kind == "a":
                    attention_layer(env, scope, n)
                else:
                    ffn_layer(env, scope, n)
            clear_semaphores()
        store(env, out)


def setup(env, g_all):
    nc, dram, x = env["nc"], env["dram"], env["x"]
    loaded, gates_loaded, made, tanhed = (env["sem"](n) for n in ("loaded", "gates_loaded", "made", "tanhed"))
    with nc.Block() as block:
        @block.sync
        def _(sp):
            sp.dma_start(x[:], dram["x"].rearrange("b (h p) d -> p (b h) d", p=P)).then_inc(loaded, 16)
            sp.dma_start(env["ctxT"][:], dram["ctxT"]).then_inc(loaded, 16)
            sp.dma_start(env["ident"][:], dram["ident"]).then_inc(loaded, 16)
            sp.dma_start(env["rank"][:], dram["rank"]).then_inc(loaded, 16)
            sp.wait_ge(loaded, 64)

        @block.scalar
        def _(act):
            act.dma_start(g_all[:, 0:4], dram["g_xattn"].partition_broadcast(P)).then_inc(gates_loaded, 16)
            act.dma_start(g_all[:, 4:8], dram["g_ffn"].partition_broadcast(P)).then_inc(gates_loaded, 16)
            act.wait_ge(gates_loaded, 32)
            nc.scalar.activation(env["tg"][:], g_all[:], ACT.Tanh).then_inc(tanhed, 1)

        @block.gpsimd
        def _(pool):
            nc.gpsimd.memset(env["half"][:], -0.5).then_inc(made, 1)
            nc.gpsimd.memset(env["half32"][:], -0.5).then_inc(made, 1)
            nc.gpsimd.memset(env["zero"][:], 0.0).then_inc(made, 1)


def store(env, out):
    stored = env["sem"]("stored")
    with env["nc"].Block() as block:
        @block.sync
        def _(sp):
            sp.dma_start(out.rearrange("b (h p) d -> p (b h) d", p=P), env["x"][:]).then_inc(stored, 16)
            sp.wait_ge(stored, 16)


def emit_statistics(env, dve, source, stats_done, var_done, rows=P, tiles=TILES):
    nc = env["nc"]
    stats, mv, var = env["stats"], env["mv"], env["var"]
    with dve.Fori(0, tiles) as t:
        nc.vector.bn_stats(stats[0:rows, t, :], source[0:rows, t, :]).then_inc(stats_done, 1)
    dve.wait_ge(stats_done, tiles)
    for t in range(tiles):
        last = nc.vector.bn_aggr(mv[0:rows, t, :], stats[0:rows, t, :])
    last.then_inc(stats_done, 1)
    dve.wait_ge(stats_done, tiles + 1)
    nc.vector.tensor_scalar(var[0:rows, 0:tiles], mv[0:rows, 0:tiles, 1], EPS, None, ALU.add).then_inc(var_done, 1)


def ffn_layer(env, scope, n):
    cfg = FFN[n]
    nc = env["nc"]

    def sb(name, shape, dt=F32):
        return scope.enter_context(nc.sbuf_tensor(f"{cfg['name']}_{name}", shape, dt))

    t = dict(
        xh=sb("xh", [P, DC, TOKENS], F32R), xl=sb("xl", [P, DC, TOKENS], F32R),
        gates=sb("gates", [P, TILES, cfg["gates"]]),
    )
    if cfg["lora"]:
        t["uh"] = sb("uh", [32, TOKENS], F32R)
        t["ul"] = sb("ul", [32, TOKENS], F32R)
    with ExitStack() as inner:
        route(env, inner, n, t)
    with ExitStack() as inner:
        experts(env, inner, n, t)


def route(env, scope, n, t):
    cfg = FFN[n]
    nc, dram, psum, x, ident = env["nc"], env["dram"], env["psum"], env["x"], env["ident"]
    mv, var, rstd, tg, rank = env["mv"], env["var"], env["rstd"], env["tg"], env["rank"]
    name, E, NG, NB = cfg["name"], cfg["experts"], cfg["gates"], cfg["bias_rows"]
    NR = E * (1 + cfg["lora"])
    gate = tg[:, 4 + n:5 + n]
    xh, xl, gates = t["xh"], t["xl"], t["gates"]

    def sb(nm, shape, dt=F32):
        return scope.enter_context(nc.sbuf_tensor(f"{name}_{nm}_sb", shape, dt))

    wr = sb("wr", [P, DC, NR])
    rb = sb("rb", [P, E])
    xn = sb("xn", [P, TPB, D])
    stage = sb("stage", [P, DC, SEQ])
    logits = sb("logits", [P, TILES, E])
    a, b, c, oh1, oh2 = (sb(nm, [P, TILES, E]) for nm in ("ra", "rexp", "rc", "oh1", "oh2"))
    m1, m2 = sb("m1", [P, TILES]), sb("m2", [P, TILES])
    if NB:
        b2 = sb("b2", [NB, D])
        gT = sb("gT", [NB, TOKENS])
    if cfg["lora"]:
        um = sb("um", [P, TILES, 32])
        ust = sb("ust", [32, TOKENS])
    sems = {k: env["sem"](f"{name}_{k}") for k in (
        "consts", "stats1", "chain", "var_done", "rstd_done", "normed", "turned", "staged", "high",
        "low", "routed", "shifted", "exped", "gates_done", "gates_turned", "gates_copied", "bias_mm",
        "bias_added", "u_turned", "u_staged", "u_high")}
    xT_ps = psum[:, 0, :].rearrange("p (c s) -> p c s", c=DC)
    rt_ps = psum[:, 1:3, :].rearrange("p k (t r) -> p (k t) r", r=64)

    with nc.Block() as block:
        @block.sync
        def _(sp):
            sp.dma_start(wr[:], dram[f"{name}_wr"]).then_inc(sems["consts"], 16)
            sp.dma_start(rb[:], dram[f"{name}_rb"].partition_broadcast(P)).then_inc(sems["consts"], 16)
            if NB:
                sp.dma_start(b2[:], dram[f"{name}_b2"]).then_inc(sems["consts"], 16)
            sp.wait_ge(sems["consts"], 32 + 16 * bool(NB))

        @block.gpsimd
        def _(pool):
            pool.wait_ge(sems["var_done"], 1)
            nc.gpsimd.tensor_tensor(rstd[:], var[:], env["half"][:], ALU.pow).then_inc(sems["rstd_done"], 1)

        @block.vector
        def _(dve):
            step = Step(dve, sems["chain"])
            emit_statistics(env, dve, x, sems["stats1"], sems["var_done"])
            dve.wait_ge(sems["rstd_done"], 1)
            with dve.Fori(0, NBATCH) as bi:
                dve.wait_ge(sems["turned"], bi)
                for h in range(TPB):
                    tile = bi * TPB + h
                    nc.vector.tensor_scalar(xn[:, h, :], x[:, tile, :], mv[:, tile, 0:1], rstd[:, bass.ds(tile, 1)],
                                            ALU.subtract, ALU.mult).then_inc(sems["normed"], 1)
                dve.wait_ge(sems["high"], bi + 1)
                nc.vector.tensor_tensor(xl[:, :, bass.ds(bi * SEQ, SEQ)], stage[:],
                                        xh[:, :, bass.ds(bi * SEQ, SEQ)].bitcast(F32),
                                        ALU.subtract).then_inc(sems["low"], 1)
            dve.wait_ge(sems["routed"], NBATCH)
            dve.wait_ge(sems["consts"], 32 + 16 * bool(NB))
            wide = [P, TILES, E]

            def over(v):
                return v.unsqueeze(2).to_broadcast(wide)

            if n == 3:
                step.then(nc.vector.tensor_copy(logits[:], rt_ps[:, :, 0:E]))
            else:
                step.then(nc.vector.tensor_tensor(logits[:], rt_ps[:, :, 0:E],
                                                  rb[:].unsqueeze(1).to_broadcast(wide), ALU.add))

            def softmax_rows(dst):
                step.then(nc.vector.tensor_reduce(m1[:], logits[:], AX.X, ALU.max))
                nc.vector.tensor_tensor(a[:], logits[:], over(m1[:]), ALU.subtract).then_inc(sems["shifted"], 1)
                dve.wait_ge(sems["exped"], 1)
                step.then(nc.vector.tensor_reduce(m2[:], b[:], AX.X, ALU.add))
                step.then(nc.vector.reciprocal(m2[:], m2[:]))
                step.then(nc.vector.tensor_tensor(dst[:], b[:], over(m2[:]), ALU.mult))

            def first_largest(dst, values):
                step.then(nc.vector.tensor_reduce(m1[:], values[:], AX.X, ALU.max))
                step.then(nc.vector.tensor_tensor(dst[:], values[:], over(m1[:]), ALU.is_equal))
                step.then(nc.vector.tensor_tensor(dst[:], dst[:], rank[:], ALU.mult))
                step.then(nc.vector.tensor_reduce(m2[:], dst[:], AX.X, ALU.max))
                step.then(nc.vector.tensor_tensor(dst[:], dst[:], over(m2[:]), ALU.is_equal))

            def second_largest(values, spare):
                step.then(nc.vector.scalar_tensor_tensor(spare[:], oh1[:], -HUGE, values[:], ALU.mult, ALU.add))
                first_largest(oh2, spare)
                step.then(nc.vector.tensor_tensor(oh1[:], oh1[:], oh2[:], ALU.add))

            def set_gates(weights):
                return nc.vector.tensor_scalar(gates[:, :, 0:E], weights[:], gate, None, ALU.mult)

            def set_plain_gates(first):
                return nc.vector.tensor_scalar(gates[:, :, first:NG], rank[:, :, 0:NG - first], 0.0, gate,
                                               ALU.mult, ALU.add)

            if n in (0, 3):
                softmax_rows(c)
                if n == 3:
                    step.then(nc.vector.tensor_tensor(b[:], c[:], rb[:].unsqueeze(1).to_broadcast(wide), ALU.add))
                    first_largest(oh1, b)
                    second_largest(b, a)
                else:
                    first_largest(oh1, c)
                    second_largest(c, a)
                step.then(nc.vector.tensor_tensor(a[:], c[:], oh1[:], ALU.mult))
                set_gates(a)
                last = set_plain_gates(E)
            elif n == 1:
                first_largest(oh1, logits)
                second_largest(logits, a)
                step.then(nc.vector.tensor_reduce(m1[:], logits[:], AX.X, ALU.max))
                nc.vector.tensor_tensor(a[:], logits[:], over(m1[:]), ALU.subtract).then_inc(sems["shifted"], 1)
                dve.wait_ge(sems["exped"], 1)
                step.then(nc.vector.tensor_tensor(c[:], b[:], oh1[:], ALU.mult))
                step.then(nc.vector.tensor_reduce(m2[:], c[:], AX.X, ALU.add))
                step.then(nc.vector.reciprocal(m2[:], m2[:]))
                step.then(nc.vector.tensor_tensor(a[:], c[:], over(m2[:]), ALU.mult))
                last = set_gates(a)
            else:
                softmax_rows(c)
                first_largest(oh1, c)
                set_plain_gates(0)
                with_r = [P, TILES, E, cfg["lora"]]
                last = nc.vector.tensor_tensor(
                    um[:].rearrange("p t (e r) -> p t e r", r=cfg["lora"]),
                    rt_ps[:, :, E:NR].rearrange("p t (e r) -> p t e r", r=cfg["lora"]),
                    oh1[:].unsqueeze(3).to_broadcast(with_r), ALU.mult)
            last.then_inc(sems["gates_done"], 1)
            for k in range(TILES // 2 if NB else 0):
                dve.wait_ge(sems["bias_mm"], k + 1)
                nc.vector.tensor_tensor(x[:, 2 * k:2 * k + 2, :], x[:, 2 * k:2 * k + 2, :],
                                        psum[:, 4 + k % 4, :].rearrange("p (t d) -> p t d", t=2),
                                        ALU.add).then_inc(sems["bias_added"], 1)
            if cfg["lora"]:
                for k in range(4):
                    dve.wait_ge(sems["u_high"], k + 1)
                    nc.vector.tensor_tensor(t["ul"][:, k * 512:(k + 1) * 512], ust[:, k * 512:(k + 1) * 512],
                                            t["uh"][:, k * 512:(k + 1) * 512].bitcast(F32),
                                            ALU.subtract).then_inc(sems["u_staged"], 1)

        @block.scalar
        def _(act):
            with act.Fori(0, NBATCH) as bi:
                act.wait_ge(sems["turned"], bi + 1)
                act.wait_ge(sems["low"], bi)
                act.wait_ge(sems["routed"], bi)
                nc.scalar.activation(stage[:], xT_ps, ACT.Copy).then_inc(sems["staged"], 1)
                nc.scalar.activation(xh[:, :, bass.ds(bi * SEQ, SEQ)], xT_ps, ACT.Copy).then_inc(sems["high"], 1)
            act.wait_ge(sems["shifted"], 1)
            nc.scalar.activation(b[:], a[:], ACT.Exp).then_inc(sems["exped"], 1)
            for k in range(4 if NB else 0):
                act.wait_ge(sems["gates_turned"], k + 1)
                nc.scalar.activation(gT[:, k * 512:(k + 1) * 512], psum[0:NB, 3, :], ACT.Copy).then_inc(
                    sems["gates_copied"], 1)
            for k in range(4 if cfg["lora"] else 0):
                act.wait_ge(sems["u_turned"], k + 1)
                nc.scalar.activation(ust[:, k * 512:(k + 1) * 512], psum[0:32, 3, :], ACT.Copy)
                nc.scalar.activation(t["uh"][:, k * 512:(k + 1) * 512], psum[0:32, 3, :], ACT.Copy).then_inc(
                    sems["u_high"], 1)

        @block.tensor
        def _(pe):
            pe.wait_ge(sems["consts"], 32 + 16 * bool(NB))
            with pe.Fori(0, NBATCH) as bi:
                pe.wait_ge(sems["normed"], TPB * bi + TPB)
                pe.wait_ge(sems["high"], bi)
                for c_ in range(DC):
                    for h in range(TPB):
                        last = nc.tensor.transpose(xT_ps[:, c_, h * P:(h + 1) * P],
                                                   xn[:, h, c_ * P:(c_ + 1) * P], ident[:])
                last.then_inc(sems["turned"], 1)
                pe.wait_ge(sems["staged"], bi + 1)
                for h in range(TPB):
                    for c_ in range(DC):
                        last = nc.tensor.matmul(rt_ps[:, bi * TPB + h, 0:NR], stage[:, c_, h * P:(h + 1) * P],
                                                wr[:, c_, :], start=(c_ == 0), stop=(c_ == DC - 1))
                last.then_inc(sems["routed"], 1)
            if NB or cfg["lora"]:
                pe.wait_ge(sems["gates_done"], 1)
            for k in range(4 if NB else 0):
                if k:
                    pe.wait_ge(sems["gates_copied"], k)
                for q in range(4):
                    last = nc.tensor.transpose(psum[0:NB, 3, q * P:(q + 1) * P],
                                               gates[:, 4 * k + q, 0:NB], ident[:])
                last.then_inc(sems["gates_turned"], 1)
            for k in range(TILES // 2 if NB else 0):
                pe.wait_ge(sems["gates_copied"], min(k // 2 + 1, 4))
                if k >= 4:
                    pe.wait_ge(sems["bias_added"], k - 3)
                for q in range(2):
                    tt = 2 * k + q
                    last = nc.tensor.matmul(psum[:, 4 + k % 4, q * D:(q + 1) * D], gT[:, tt * P:(tt + 1) * P],
                                            b2[:], start=True, stop=True)
                last.then_inc(sems["bias_mm"], 1)
            for k in range(4 if cfg["lora"] else 0):
                pe.wait_ge(sems["gates_copied"], 4)
                if k:
                    pe.wait_ge(sems["u_high"], k)
                for q in range(4):
                    last = nc.tensor.transpose(psum[0:32, 3, q * P:(q + 1) * P], um[:, 4 * k + q, :], ident[:])
                last.then_inc(sems["u_turned"], 1)


def experts(env, scope, n, t):
    cfg = FFN[n]
    nc, dram, psum, x = env["nc"], env["dram"], env["psum"], env["x"]
    name, U = cfg["name"], cfg["units"]
    silu = cfg["act"] == "silu"
    HB = UNIT // P
    HC = HB // 2 if silu else HB
    xh, xl, gates = t["xh"], t["xl"], t["gates"]
    func = {"gelu": ACT.Gelu, "relu": ACT.Relu, "silu": ACT.Silu}[cfg["act"]]
    pairs, odd = divmod(U, 2)
    looped = pairs - (0 if odd else 1)

    def sb(nm, shape, dt=F32):
        return scope.enter_context(nc.sbuf_tensor(f"{name}_{nm}_sb", shape, dt))

    zero = env["zero"][:]
    w1raw = [sb(f"w1raw{s}", [P, DC, UNIT]) for s in range(2)]
    w2raw = [sb(f"w2raw{s}", [P, HC, D]) for s in range(2)]
    w1h = [sb(f"w1h{s}", [P, DC, UNIT], F32R) for s in range(2)]
    w1l = [sb(f"w1l{s}", [P, DC, UNIT], F32R) for s in range(2)]
    w2h = [sb(f"w2h{s}", [P, HC, D], F32R) for s in range(2)]
    w2l = [sb(f"w2l{s}", [P, HC, D], F32R) for s in range(2)]
    h32 = sb("h32", [P, HC, CHUNK])
    hh = sb("hh", [P, 2, HC, CHUNK], F32R)
    hl = sb("hl", [P, 2, HC, CHUNK], F32R)
    b1 = None if silu else sb("b1", [P, U, HB])
    b1u = None if silu else sb("b1u", [P, 2, HB])
    s32 = sb("s32", [P, HC, CHUNK]) if silu else None
    if cfg["lora"]:
        lb = sb("lb", [32, U, UNIT])
        lbh, lbl = sb("lbh", [32, U, UNIT], F32R), sb("lbl", [32, U, UNIT], F32R)
    sems = {k: env["sem"](f"{name}x_{k}") for k in (
        "bias_in", "raw_in0", "raw_in1", "split_high", "split", "hidden", "gated", "multiplied",
        "activated", "lowered", "product", "added", "lora_split", "bias_set")}
    SPLIT0 = 2
    HID0 = HC if silu else HB
    LOW0 = HC
    PROD0 = 4 * CHUNKS
    ADD0 = 4
    hid_ps = [psum[:, m, :] for m in range(HB)]
    y_ps = [psum[:, 4 + q, 0:D] for q in range(4)]

    def run(engine, body):
        if looped:
            with engine.Fori(0, looped) as i:
                body(i, 0, False)
                body(i, 1, False)
        body(looped, 0, bool(odd))
        if not odd:
            body(looped, 1, True)

    def run_ahead(engine, first, second):
        def body(i, s, last):
            for c in range(CHUNKS):
                if c < CHUNKS - 1:
                    first(i, s, c + 1)
                elif not last:
                    first(i + s, 1 - s, 0)
                second(i, s, c)

        first(0, 0, 0)
        run(engine, body)

    with nc.Block() as block:
        @block.sync
        def _(sp):
            if b1 is not None:
                sp.dma_start(b1[:], dram[f"{name}_b1"]).then_inc(sems["bias_in"], 16)
            if cfg["lora"]:
                sp.dma_start(lb[:], dram[f"{name}_lb"]).then_inc(sems["bias_in"], 16)

            def body(i, s, last):
                u = i * 2 + s
                sp.wait_ge(sems["split"], u * 2)
                sp.dma_start(w1raw[s][:], dram[f"{name}_w1"][u]).then_inc(sems[f"raw_in{s}"], 16)
                sp.dma_start(w2raw[s][:], dram[f"{name}_w2"][u]).then_inc(sems[f"raw_in{s}"], 16)

            run(sp, body)

        @block.gpsimd
        def _(pool):
            pool.sem_inc(sems["split"], SPLIT0)
            if cfg["lora"]:
                pool.wait_ge(sems["bias_in"], 32)
                nc.gpsimd.tensor_copy(lbh[:], lb[:]).then_inc(sems["lora_split"], 1)
                pool.wait_ge(sems["lora_split"], 1)
                nc.gpsimd.tensor_tensor(lbl[:], lb[:], lbh[:].bitcast(F32), ALU.subtract).then_inc(
                    sems["lora_split"], 1)

            def body(i, s, last):
                u = i * 2 + s
                pool.wait_ge(sems[f"raw_in{s}"], i * 32 + 32)
                pool.wait_ge(sems["product"], u * 4 * CHUNKS)
                nc.gpsimd.tensor_tensor(w1h[s][:], w1raw[s][:], zero.unsqueeze(2).to_broadcast([P, DC, UNIT]),
                                        ALU.add).then_inc(sems["split_high"], 1)
                nc.gpsimd.tensor_tensor(w2h[s][:], w2raw[s][:], zero.unsqueeze(2).to_broadcast([P, HC, D]),
                                        ALU.add).then_inc(sems["split_high"], 1)
                pool.wait_ge(sems["split_high"], u * 2 + 2)
                nc.gpsimd.tensor_tensor(w1l[s][:], w1raw[s][:], w1h[s][:].bitcast(F32),
                                        ALU.subtract).then_inc(sems["split"], 1)
                nc.gpsimd.tensor_tensor(w2l[s][:], w2raw[s][:], w2h[s][:].bitcast(F32),
                                        ALU.subtract).then_inc(sems["split"], 1)

            run(pool, body)

        @block.tensor
        def _(pe):
            pe.sem_inc(sems["product"], PROD0)
            if cfg["lora"]:
                pe.wait_ge(sems["lora_split"], 2)

            def first(i, s, c):
                u = i * 2 + s
                g = u * CHUNKS + c
                if c == 0:
                    pe.wait_ge(sems["split"], u * 2 + 2 + SPLIT0)
                tok = slice(c * CHUNK, (c + 1) * CHUNK)
                for m in range(HB):
                    if not silu:
                        pe.wait_ge(sems["activated"], g * HB + m + 1)
                    else:
                        pe.wait_ge(sems["gated" if m < HC else "multiplied"], g * HC + m % HC + 1)
                    cols = slice(m * P, (m + 1) * P)
                    terms = [(w[s][:, k, cols], v[:, k, tok]) for k in range(DC)
                             for w, v in ((w1h, xh), (w1h, xl), (w1l, xh))]
                    if cfg["lora"]:
                        terms += [(w[:, u, cols], v[:, tok]) for w, v in
                                  ((lbh, t["uh"]), (lbh, t["ul"]), (lbl, t["uh"]))]
                    for j, (w, v) in enumerate(terms):
                        last = nc.tensor.matmul(hid_ps[m], w, v, start=(j == 0), stop=(j == len(terms) - 1))
                    last.then_inc(sems["hidden"], 1)

            def second(i, s, c):
                g = (i * 2 + s) * CHUNKS + c
                pe.wait_ge(sems["lowered"], g * HC + HC + LOW0)
                for q in range(4):
                    pe.wait_ge(sems["added"], g * 4 + q + 1)
                    tok = slice(q * P, (q + 1) * P)
                    terms = [(v[:, c % 2, k, tok], w[s][:, k, :]) for k in range(HC)
                             for v, w in ((hh, w2h), (hh, w2l), (hl, w2h))]
                    for j, (v, w) in enumerate(terms):
                        last = nc.tensor.matmul(y_ps[q], v, w, start=(j == 0), stop=(j == len(terms) - 1))
                    last.then_inc(sems["product"], 1)

            run_ahead(pe, first, second)

        @block.scalar
        def _(act):
            act.sem_inc(sems["gated" if silu else "activated"], HID0)
            if b1 is not None:
                act.wait_ge(sems["bias_in"], 16 + 16 * bool(cfg["lora"]))

            def plain(i, s, last):
                u = i * 2 + s
                nc.scalar.activation(b1u[:, s, :], b1[:, u, :], ACT.Copy).then_inc(sems["bias_set"], 1)
                for c in range(CHUNKS):
                    g = u * CHUNKS + c
                    if c == 0:
                        act.wait_ge(sems["bias_set"], u + 1)
                    act.wait_ge(sems["product"], g * 4 + 4 + PROD0 - 8)
                    for m in range(HB):
                        act.wait_ge(sems["hidden"], g * HB + m + 1)
                        act.wait_ge(sems["lowered"], g * HC + m + 1)
                        bias = b1u[:, s, m:m + 1]
                        nc.scalar.activation(h32[:, m, :], hid_ps[m], func, bias=bias)
                        nc.scalar.activation(hh[:, c % 2, m, :], hid_ps[m], func, bias=bias).then_inc(
                            sems["activated"], 1)

            def with_product(i, s, last):
                u = i * 2 + s
                for c in range(CHUNKS):
                    g = u * CHUNKS + c
                    act.wait_ge(sems["product"], g * 4 + 4 + PROD0 - 8)
                    for m in range(HC):
                        act.wait_ge(sems["hidden"], g * HB + m + 1)
                        act.wait_ge(sems["multiplied"], g * HC + m + 1)
                        nc.scalar.activation(s32[:, m, :], hid_ps[m], func).then_inc(sems["gated"], 1)
                    for m in range(HC):
                        act.wait_ge(sems["multiplied"], g * HC + m + 1 + HID0)
                        nc.scalar.activation(hh[:, c % 2, m, :], h32[:, m, :], ACT.Copy).then_inc(
                            sems["activated"], 1)

            run(act, with_product if silu else plain)

        @block.vector
        def _(dve):
            dve.sem_inc(sems["lowered"], LOW0)
            dve.sem_inc(sems["added"], ADD0)
            if silu:
                dve.sem_inc(sems["multiplied"], HID0)

            def first(i, s, c):
                g = (i * 2 + s) * CHUNKS + c
                if silu:
                    for m in range(HC):
                        dve.wait_ge(sems["gated"], g * HC + m + 1 + HID0)
                        dve.wait_ge(sems["hidden"], g * HB + HC + m + 1)
                        dve.wait_ge(sems["lowered"], g * HC + m + 1)
                        nc.vector.tensor_tensor(h32[:, m, :], s32[:, m, :], hid_ps[HC + m], ALU.mult).then_inc(
                            sems["multiplied"], 1)
                for m in range(HC):
                    dve.wait_ge(sems["activated"], g * HC + m + 1 + (0 if silu else HID0))
                    nc.vector.tensor_tensor(hl[:, c % 2, m, :], h32[:, m, :], hh[:, c % 2, m, :].bitcast(F32),
                                            ALU.subtract).then_inc(sems["lowered"], 1)

            def second(i, s, c):
                u = i * 2 + s
                g = u * CHUNKS + c
                column = (i if cfg["per_expert"] == 2 else u)
                for q in range(4):
                    tile = c * 4 + q
                    dve.wait_ge(sems["product"], g * 4 + q + 1 + PROD0)
                    nc.vector.scalar_tensor_tensor(x[:, tile, :], y_ps[q], gates[:, tile, bass.ds(column, 1)],
                                                   x[:, tile, :], ALU.mult, ALU.add).then_inc(sems["added"], 1)

            run_ahead(dve, first, second)


def attention_layer(env, scope, n):
    cfg = ATTN[n]
    nc = env["nc"]
    name, hd, keys = cfg["name"], cfg["hd"], cfg["keys"]
    inner = HEADS * hd
    NC = inner // P
    per_chunk = P // hd

    def sb(nm, shape, dt=F32):
        return scope.enter_context(nc.sbuf_tensor(f"{name}_{nm}_sb", shape, dt))

    t = dict(
        inner=inner, NC=NC, per_chunk=per_chunk,
        xT=sb("xT", [P, DC, TOKENS]),
        keysT=sb("keysT", [P, NC, NBATCH, per_chunk, keys]),
        values=sb("values", [keys, NBATCH, HEADS, hd + 1]),
    )
    if cfg["mask"] == "given":
        t["mask_mul"] = sb("mask_mul", [P, TILES, CTX])
        t["mask_add"] = sb("mask_add", [P, TILES, CTX])
    if cfg["l2norm"]:
        t["gain"] = sb("gain", [P, D])
    with ExitStack() as part:
        normalise(env, part, n, t)
    with ExitStack() as part:
        keys_and_values(env, part, n, t)
    with ExitStack() as part:
        attend(env, part, n, t)


def normalise(env, scope, n, t):
    cfg = ATTN[n]
    nc, dram, psum, x, ident = env["nc"], env["dram"], env["psum"], env["x"], env["ident"]
    mv, var, rstd = env["mv"], env["var"], env["rstd"]
    name, twice, xT = cfg["name"], cfg["l2norm"], t["xT"]

    def sb(nm, shape, dt=F32):
        return scope.enter_context(nc.sbuf_tensor(f"{name}_{nm}_sb", shape, dt))

    xn = sb("xn", [P, TPB, D])
    if twice:
        once = sb("once", [P, TILES, D])
        ln = sb("ln", [P, 2, DC])
    sems = {k: env["sem"](f"{name}n_{k}") for k in (
        "ln_in", "stats1", "stats2", "var_done", "rstd_done", "applied", "normed", "turned", "copied")}
    turn_ps = psum[:, 0, :].rearrange("p (c s) -> p c s", c=DC)

    with nc.Block() as block:
        if twice:
            @block.sync
            def _(sp):
                sp.dma_start(ln[:], dram[f"{name}_ln_in"]).then_inc(sems["ln_in"], 16)

        @block.gpsimd
        def _(pool):
            for k in range(2 if twice else 1):
                pool.wait_ge(sems["var_done"], k + 1)
                nc.gpsimd.tensor_tensor(rstd[:], var[:], env["half"][:], ALU.pow).then_inc(sems["rstd_done"], 1)

        @block.vector
        def _(dve):
            emit_statistics(env, dve, x, sems["stats1"], sems["var_done"])
            dve.wait_ge(sems["rstd_done"], 1)
            source = x
            if twice:
                with dve.Fori(0, TILES) as tile:
                    nc.vector.tensor_scalar(once[:, tile, :], x[:, tile, :], mv[:, tile, 0:1], rstd[:, bass.ds(tile, 1)],
                                            ALU.subtract, ALU.mult).then_inc(sems["applied"], 1)
                dve.wait_ge(sems["applied"], TILES)
                emit_statistics(env, dve, once, sems["stats2"], sems["var_done"])
                dve.wait_ge(sems["rstd_done"], 2)
                dve.wait_ge(sems["ln_in"], 16)
                source = once

            with dve.Fori(0, NBATCH) as bi:
                for h in range(TPB):
                    tile = bi * TPB + h
                    if h == 0:
                        dve.wait_ge(sems["turned"], bi)
                    nc.vector.tensor_scalar(xn[:, h, :], source[:, tile, :], mv[:, tile, 0:1],
                                            rstd[:, bass.ds(tile, 1)], ALU.subtract, ALU.mult).then_inc(
                                                sems["normed"], 1)
                dve.wait_ge(sems["turned"], bi + 1)
                for c in range(DC):
                    dst = xT[:, c, bass.ds(bi * SEQ, SEQ)]
                    if twice:
                        ins = nc.vector.tensor_scalar(dst, turn_ps[:, c, :], ln[:, 0, c:c + 1], ln[:, 1, c:c + 1],
                                                      ALU.mult, ALU.add)
                    else:
                        ins = nc.vector.tensor_scalar(dst, turn_ps[:, c, :], 1.0, None, ALU.mult)
                ins.then_inc(sems["copied"], 1)

        @block.tensor
        def _(pe):
            with pe.Fori(0, NBATCH) as bi:
                pe.wait_ge(sems["copied"], bi)
                pe.wait_ge(sems["normed"], bi * TPB + TPB)
                for c in range(DC):
                    for h in range(TPB):
                        last = nc.tensor.transpose(turn_ps[:, c, h * P:(h + 1) * P],
                                                   xn[:, h, c * P:(c + 1) * P], ident[:])
                last.then_inc(sems["turned"], 1)


def keys_and_values(env, scope, n, t):
    cfg = ATTN[n]
    nc, dram, psum, x, ident = env["nc"], env["dram"], env["psum"], env["x"], env["ident"]
    ctxT, tg = env["ctxT"], env["tg"]
    name, hd, keys, inner, NC, per_chunk = cfg["name"], cfg["hd"], cfg["keys"], t["inner"], t["NC"], t["per_chunk"]
    keysT, values = t["keysT"], t["values"]
    own = cfg["l2norm"]
    gate = tg[:, n:n + 1]
    HALF = NBATCH // 2 * CTX

    def sb(nm, shape, dt=F32):
        return scope.enter_context(nc.sbuf_tensor(f"{name}_{nm}_sb", shape, dt))

    wk = sb("wk", [P, DC, inner])
    wv = sb("wv", [P, DC, inner])
    loads = [(wk[:], dram[f"{name}_wk"]), (wv[:], dram[f"{name}_wv"])]
    if own:
        ctx = sb("ctx", [CTX, NBATCH, D])
        ctxn = sb("ctxn", [CTX, NBATCH, D])
        ctxnT = sb("ctxnT", [P, DC, NBATCH * CTX])
        ln = sb("ln2", [P, 2, DC])
        out_rows = sb("out_rows", [P, 2, D])
        ksc = sb("ksc", [keys, hd])
        ktm = [sb(f"ktm{i}", [keys, HEADS, hd]) for i in range(2)]
        kn = [sb(f"kn{i}", [keys, HEADS, hd]) for i in range(2)]
        square = sb("square", [keys, HEADS, hd])
        ss = [sb(f"ss{i}", [keys, HEADS]) for i in range(2)]
        rn = [sb(f"rnk{i}", [keys, HEADS]) for i in range(2)]
        nkeys = NBATCH
        loads += [(ctx[:], dram["ctx"]), (ln[:], dram[f"{name}_ln_ctx"]),
                  (out_rows[:], dram[f"{name}_ln_out"].partition_broadcast(P)),
                  (ksc[:], dram[f"{name}_k_scale"].partition_broadcast(keys)),
                  (ktm[0][CTX:keys, :, :], dram[f"{name}_null"][0:1, 0]),
                  (ktm[1][CTX:keys, :, :], dram[f"{name}_null"][0:1, 0]),
                  (values[CTX:keys, :, :, 0:hd], dram[f"{name}_null_v"])]
        source = ctxnT
    else:
        bk = sb("bk", [P, NC])
        bv = sb("bv", [CTX, inner])
        bo = sb("bo", [P, D])
        loads += [(bk[:], dram[f"{name}_bk"]), (bv[:], dram[f"{name}_bv"].partition_broadcast(CTX)),
                  (bo[:], dram[f"{name}_bo"].partition_broadcast(P))]
        source = ctxT
    if hd == 16:
        kT = sb("kT", [P, NC, NBATCH * CTX])
        own_rows = sb("own_rows", [P, per_chunk])
        loads += [(own_rows[:], dram["own_rows"])]
    if cfg["rope"]:
        wkr = sb("wkr", [P, DC, inner])
        bkr = sb("bkr", [P, NC])
        kr = sb("kr", [P, NC, NBATCH * CTX])
        cos, sin = sb("cos", [P, CTX]), sb("sin", [P, CTX])
        loads += [(wkr[:], dram[f"{name}_wkr"]), (bkr[:], dram[f"{name}_bkr"]),
                  (cos[:], dram["cos"][:, 0:CTX]), (sin[:], dram["sin"][:, 0:CTX])]
    if cfg["mask"] == "given":
        mask8 = sb("mask8", [P, TILES, CTX], U8)
        loads += [(mask8[:], dram["mask"])]
    added_row = sb("added_row", [P, D])
    sems = {k: env["sem"](f"{name}k_{k}") for k in (
        "loaded", "chain", "pool_chain", "k_ready", "k_out", "v_ready", "v_out", "gated_row", "shaped",
        "stats", "var_done", "rstd_done", "ctx_turned", "ctx_out", "squared", "inverted", "normed",
        "kn_turned", "kn_out")}
    k_list = [] if own else [(w, c, half) for w in ((wk, wkr) if cfg["rope"] else (wk,))
                             for c in range(NC) for half in range(2)]
    v_list = [(b, part) for b in range(NBATCH) for part in range(max(1, inner // BANK))]
    VN = min(inner, BANK)
    v_bank = lambda j: psum[0:CTX, 4 + j % 4, 0:VN]
    k_bank = lambda j: psum[:, j % 4, 0:HALF]

    with nc.Block() as block:
        @block.sync
        def _(sp):
            for dst, src in loads:
                sp.dma_start(dst, src).then_inc(sems["loaded"], 16)

        @block.gpsimd
        def _(pool):
            step = Step(pool, sems["pool_chain"])
            if per_chunk == 2:
                step.then(nc.gpsimd.memset(keysT[0:hd, :, :, 1, :], 0.0))
                step.then(nc.gpsimd.memset(keysT[hd:P, :, :, 0, :], 0.0))
            step.then(nc.gpsimd.memset(values[:, :, :, hd:hd + 1], 1.0))
            if own:
                pool.wait_ge(sems["var_done"], 1)
                nc.gpsimd.tensor_tensor(env["rstd"][0:CTX, 0:NBATCH], env["var"][0:CTX, 0:NBATCH],
                                        env["half"][0:CTX, 0:NBATCH], ALU.pow).then_inc(sems["rstd_done"], 1)
                for b in range(NBATCH):
                    pool.wait_ge(sems["squared"], b + 1)
                    nc.gpsimd.tensor_tensor(rn[b % 2][:], ss[b % 2][:], env["half"][0:keys, 0:HEADS],
                                            ALU.pow).then_inc(sems["inverted"], 1)
            pool.wait_ge(sems["gated_row"], 1)
            nc.gpsimd.tensor_tensor(x[:], x[:], added_row[:].unsqueeze(1).to_broadcast([P, TILES, D]),
                                    ALU.add).then_inc(sems["pool_chain"], 1)

        @block.tensor
        def _(pe):
            pe.wait_ge(sems["loaded"], 16 * len(loads))
            if own:
                pe.wait_ge(sems["normed"], 1)
                for j in range(4):
                    for q in range(4):
                        b = 4 * (j % 2) + q
                        last = nc.tensor.transpose(psum[:, j, q * CTX:(q + 1) * CTX],
                                                   ctxn[:, b, (j // 2) * P:(j // 2 + 1) * P], ident[0:CTX, 0:CTX])
                    last.then_inc(sems["ctx_turned"], 1)
                pe.wait_ge(sems["ctx_out"], 4)
            for j, (w, c, half) in enumerate(k_list):
                if j >= 4:
                    pe.wait_ge(sems["k_out"], j - 3)
                for k in range(DC):
                    last = nc.tensor.matmul(k_bank(j), w[:, k, c * P:(c + 1) * P],
                                            source[:, k, half * HALF:(half + 1) * HALF],
                                            start=(k == 0), stop=(k == DC - 1))
                last.then_inc(sems["k_ready"], 1)
            for j, (b, part) in enumerate(v_list):
                if j >= 4:
                    pe.wait_ge(sems["v_out"], j - 3)
                for k in range(DC):
                    last = nc.tensor.matmul(v_bank(j), source[:, k, b * CTX:(b + 1) * CTX],
                                            wv[:, k, part * VN:(part + 1) * VN], start=(k == 0), stop=(k == DC - 1))
                last.then_inc(sems["v_ready"], 1)
            if own:
                def project(b):
                    if b:
                        pe.wait_ge(sems["k_out"], b)
                    for part in range(2):
                        for k in range(DC):
                            last = nc.tensor.matmul(psum[0:CTX, part, :], source[:, k, b * CTX:(b + 1) * CTX],
                                                    wk[:, k, part * BANK:(part + 1) * BANK],
                                                    start=(k == 0), stop=(k == DC - 1))
                    last.then_inc(sems["k_ready"], 1)

                project(0)
                for b in range(NBATCH):
                    if b + 1 < NBATCH:
                        project(b + 1)
                    pe.wait_ge(sems["normed"], b + 2)
                    if b:
                        pe.wait_ge(sems["kn_out"], b)
                    for c in range(NC):
                        last = nc.tensor.transpose(psum[:, 2 + c // 4, (c % 4) * keys:(c % 4 + 1) * keys],
                                                   kn[b % 2][:, 2 * c:2 * c + 2, :].rearrange("p h d -> p (h d)"),
                                                   ident[0:keys, 0:keys])
                    last.then_inc(sems["kn_turned"], 1)

        @block.scalar
        def _(act):
            act.wait_ge(sems["loaded"], 16 * len(loads))
            if own:
                for j in range(4):
                    act.wait_ge(sems["ctx_turned"], j + 1)
                    nc.scalar.activation(ctxnT[:, j // 2, (j % 2) * HALF:(j % 2 + 1) * HALF], psum[:, j, 0:HALF],
                                         ACT.Identity, scale=ln[:, 0, j // 2:j // 2 + 1],
                                         bias=ln[:, 1, j // 2:j // 2 + 1]).then_inc(sems["ctx_out"], 1)
            for j, (w, c, half) in enumerate(k_list):
                act.wait_ge(sems["k_ready"], j + 1)
                bias = bk if w is wk else bkr
                if hd == 16:
                    dst = kT if w is wk else kr
                    nc.scalar.activation(dst[:, c, half * HALF:(half + 1) * HALF], k_bank(j), ACT.Identity,
                                         bias=bias[:, c:c + 1]).then_inc(sems["k_out"], 1)
                else:
                    for s in range(2):
                        rows = slice(s * hd, (s + 1) * hd)
                        last = nc.scalar.activation(
                            keysT[rows, c, half * 4:half * 4 + 4, s, :],
                            psum[rows, j % 4, 0:HALF].rearrange("p (b k) -> p b k", k=CTX), ACT.Identity,
                            bias=bias[rows, c:c + 1])
                    last.then_inc(sems["k_out"], 1)
            if own:
                for b in range(NBATCH):
                    act.wait_ge(sems["k_ready"], b + 1)
                    if b >= 2:
                        act.wait_ge(sems["normed"], b)
                    nc.scalar.activation(ktm[b % 2][0:CTX, :, :].rearrange("p h d -> p (h d)").rearrange(
                        "p (a c) -> p a c", a=2), psum[0:CTX, 0:2, :], ACT.Copy).then_inc(sems["k_out"], 1)

        @block.vector
        def _(dve):
            step = Step(dve, sems["chain"])
            dve.wait_ge(sems["loaded"], 16 * len(loads))
            if own:
                emit_statistics(env, dve, ctx, sems["stats"], sems["var_done"], CTX, NBATCH)
                step.then(nc.vector.tensor_scalar(added_row[:], out_rows[:, 1, :], gate, None, ALU.mult))
                nc.vector.tensor_scalar(t["gain"][:], out_rows[:, 0, :], gate, None, ALU.mult).then_inc(
                    sems["gated_row"], 1)
                dve.wait_ge(sems["rstd_done"], 1)
                for b in range(NBATCH):
                    last = nc.vector.tensor_scalar(ctxn[:, b, :], ctx[:, b, :], env["mv"][0:CTX, b, 0:1],
                                                   env["rstd"][0:CTX, b:b + 1], ALU.subtract, ALU.mult)
                last.then_inc(sems["normed"], 1)
            else:
                nc.vector.tensor_scalar(added_row[:], bo[:], gate, None, ALU.mult).then_inc(sems["gated_row"], 1)
            if cfg["mask"] == "given":
                step.then(nc.vector.tensor_copy(t["mask_mul"][:], mask8[:]))
                step.did(nc.vector.tensor_scalar(t["mask_add"][:], t["mask_mul"][:], -1.0, -L2_FILL / cfg["scale"],
                                                 ALU.add, ALU.mult))
            if not own:
                for j, (b, part) in enumerate(v_list):
                    dve.wait_ge(sems["v_ready"], j + 1)
                    heads = slice(part * (VN // hd), (part + 1) * (VN // hd))
                    nc.vector.tensor_tensor(values[0:CTX, b, heads, 0:hd],
                                            v_bank(j).rearrange("p (h d) -> p h d", d=hd),
                                            bv[:, part * VN:(part + 1) * VN].rearrange("p (h d) -> p h d", d=hd),
                                            ALU.add).then_inc(sems["v_out"], 1)
            else:
                for j, (b, part) in enumerate(v_list):
                    dve.wait_ge(sems["v_ready"], j + 1)
                    heads = slice(part * (VN // hd), (part + 1) * (VN // hd))
                    nc.vector.tensor_copy(values[0:CTX, b, heads, 0:hd],
                                          v_bank(j).rearrange("p (h d) -> p h d", d=hd)).then_inc(sems["v_out"], 1)

                def squares(b):
                    dve.wait_ge(sems["k_out"], b + 1)
                    step.then(nc.vector.tensor_tensor(square[:], ktm[b % 2][:], ktm[b % 2][:], ALU.mult))
                    step.then(nc.vector.tensor_reduce(ss[b % 2][:], square[:], AX.X, ALU.add))
                    nc.vector.tensor_scalar(ss[b % 2][:], ss[b % 2][:], 1e-24, None, ALU.max).then_inc(
                        sems["squared"], 1)

                def spread(b):
                    dve.wait_ge(sems["kn_turned"], b + 1)
                    for part in range(2):
                        for s in range(2):
                            rows = slice(s * hd, (s + 1) * hd)
                            last = nc.vector.tensor_copy(
                                keysT[rows, part * 4:part * 4 + 4, b, s, :],
                                psum[rows, 2 + part, 0:4 * keys].rearrange("p (c k) -> p c k", k=keys))
                    last.then_inc(sems["kn_out"], 1)

                squares(0)
                for b in range(NBATCH):
                    if b + 1 < NBATCH:
                        squares(b + 1)
                    dve.wait_ge(sems["inverted"], b + 1)
                    if b >= 2:
                        dve.wait_ge(sems["kn_turned"], b - 1)
                    step.then(nc.vector.tensor_tensor(kn[b % 2][:], ktm[b % 2][:],
                                                      rn[b % 2][:].unsqueeze(2).to_broadcast([keys, HEADS, hd]),
                                                      ALU.mult))
                    nc.vector.tensor_tensor(kn[b % 2][:], kn[b % 2][:],
                                            ksc[:].unsqueeze(1).to_broadcast([keys, HEADS, hd]),
                                            ALU.mult).then_inc(sems["normed"], 1)
                    if b:
                        spread(b - 1)
                spread(NBATCH - 1)
            if hd == 16:
                dve.wait_ge(sems["k_out"], len(k_list))
                if cfg["rope"]:
                    wide = [P, NC * NBATCH, CTX]
                    for v, table in ((kT, cos), (kr, sin)):
                        v3 = v[:].rearrange("p c (b k) -> p (c b) k", k=CTX)
                        step.then(nc.vector.tensor_tensor(v3, v3, table[:].unsqueeze(1).to_broadcast(wide), ALU.mult))
                    step.then(nc.vector.tensor_tensor(kT[:], kT[:], kr[:], ALU.add))
                for c in range(NC):
                    for h in range(per_chunk):
                        last = nc.vector.tensor_scalar(keysT[:, c, :, h, :],
                                                       kT[:, c, :].rearrange("p (b k) -> p b k", k=CTX),
                                                       own_rows[:, h:h + 1], None, ALU.mult)
                last.then_inc(sems["shaped"], 1)


def attend(env, scope, n, t):
    cfg = ATTN[n]
    nc, dram, psum, x, ident, tg = env["nc"], env["dram"], env["psum"], env["x"], env["ident"], env["tg"]
    name, hd, keys, inner, NC = cfg["name"], cfg["hd"], cfg["keys"], t["inner"], t["NC"]
    xT, keysT, values = t["xT"], t["keysT"], t["values"]
    rope, own, mask = cfg["rope"], cfg["l2norm"], cfg["mask"]
    gate = tg[:, n:n + 1]
    STEPS = TPB * GROUPS
    wide = [P, GROUP, keys]

    def sb(nm, shape, dt=F32):
        return scope.enter_context(nc.sbuf_tensor(f"{name}_{nm}_sb", shape, dt))

    wq = sb("wq", [P, DC, inner])
    wo = sb("wo", [P, NC, D])
    qT = sb("qT", [P, NC, SEQ])
    shifted = [sb(f"shifted{i}", wide) for i in range(2)]
    probs = [sb(f"probs{i}", wide) for i in range(2)]
    probsT = [sb(f"probsT{i}", [keys, GROUP * P]) for i in range(2)]
    top = [sb(f"top{i}", [P, GROUP]) for i in range(2)]
    inv = [sb(f"inv{i}", [P, GROUP]) for i in range(2)]
    att = [sb(f"att{i}", [P, HEADS, hd]) for i in range(TPB)]
    attT = [sb(f"attT{i}", [P, NC, P]) for i in range(TPB)]
    loads = [(wq[:], dram[f"{name}_wq"]), (wo[:], dram[f"{name}_wo"])]
    if own:
        q_scale = sb("q_scale", [P, 1])
        of_head = sb("of_head", [P, 2])
        q2 = sb("q2", [P, NC, SEQ])
        qss, qrn = sb("qss", [P, TPB, HEADS]), sb("qrn", [P, TPB, HEADS])
        y_all = sb("y_all", [P, TILES, D])
        loads += [(q_scale[:], dram[f"{name}_q_scale"]), (of_head[:], dram["of_head"])]
    else:
        bq = sb("bq", [P, NC])
        loads += [(bq[:], dram[f"{name}_bq"])]
    if rope:
        wqr, bqr = sb("wqr", [P, DC, inner]), sb("bqr", [P, NC])
        q_raw, qr = sb("q_raw", [P, NC, SEQ]), sb("qr", [P, NC, SEQ])
        cos, sin = sb("cosq", [P, SEQ]), sb("sinq", [P, SEQ])
        loads += [(wqr[:], dram[f"{name}_wqr"]), (bqr[:], dram[f"{name}_bqr"]), (cos[:], dram["cos"]),
                  (sin[:], dram["sin"])]
    if mask == "window":
        window, seen = sb("window", [P, TPB, CTX]), sb("seen", [P, TPB])
        loads += [(window[:], dram["window"]), (seen[:], dram["seen"])]
    sems = {k: env["sem"](f"{name}l_{k}") for k in (
        "loaded", "q_ready", "q_out", "q_done", "sq_ready", "sq_out", "q_inverted", "scored", "s_free",
        "shift", "probs", "turned", "pt_out", "summed", "normed", "att_turned", "y_ready", "left", "chain",
        "stats", "var_done", "rstd_done", "applied", "gained")}

    SCORES, EXPS, TURN, SUMS = 6, 5, 4, 3
    NQ = (2 if rope else 1) * max(1, NC // 2)
    AT = max(1, NC // 4)
    QPS = 2
    Q_SLOTS = [range(q, min(q + QPS, NQ)) for q in range(0, NQ, QPS)]
    SQ_SLOT = len(Q_SLOTS)
    TURN_SLOT, OUT_SLOT = (2, 6), (3, 7)

    uses = [("q_out", j + 1) for j in range(NQ)] + ([("sq_out", 1)] if own else [])
    LEFT = TPB * (AT + 1)
    first_left = len(uses)
    uses += [("left", j + 1) for j in range(LEFT)]
    spare = lambda use: psum[:, 6 + use % 2, :]

    def count(b, o, per, k):
        if isinstance(b, int):
            return max((b + o) * per + k, 0)
        assert o * per + k >= 0
        return b * per + (o * per + k)

    def at_spare(pe, b, o, use, last):
        kind = uses[use - 2][0] if use >= 2 else None
        if kind == "left" and uses[use][0] == "left":
            pe.wait_ge(sems["left"], count(b, o, LEFT, uses[use - 2][1]))
        elif use < 2 or (last and uses[use][0] == "left"):
            pe.wait_ge(sems["left"], count(b, 0, LEFT, 0))
            pe.wait_ge(sems["q_out"], count(b, 0, NQ, NQ if o or last else 0))
            if own:
                pe.wait_ge(sems["sq_out"], count(b, 0, 1, 1 if o or last else 0))
        else:
            per = NQ if kind == "q_out" else 1
            ahead = 1 if uses[use][0] == "left" else o
            pe.wait_ge(sems[kind], count(b, ahead, per, uses[use - 2][1]))
        return spare(use)

    def stream(engine, prepare, slot, step=None):
        prepare(0, 0)
        for s in range(-SCORES, 0):
            slot(0, s, False)
        if step:
            step.filled()
        with engine.Fori(0, NBATCH - 1) as bi:
            if step:
                step.round(bi)
            for s in range(STEPS):
                slot(bi, s, False)
            if step:
                step.check()
        if step:
            step.round(NBATCH - 1)
        for s in range(STEPS):
            slot(NBATCH - 1, s, True)

    def item(fn, b, s, lead, last):
        g = s + lead
        if 0 <= g < STEPS:
            fn(b, 0, g)
        elif g >= STEPS and not last:
            fn(b, 1, g - STEPS)

    with nc.Block() as block:
        @block.sync
        def _(sp):
            for dst, src in loads:
                sp.dma_start(dst, src).then_inc(sems["loaded"], 16)

        @block.tensor
        def _(pe):
            def queries(b, o, j):
                w = wqr if rope and j >= NQ // 2 else wq
                bank = at_spare(pe, b, o, j, False)
                for s in range(2):
                    c = (2 * j + s) % NC
                    for k in range(DC):
                        last = nc.tensor.matmul(bank[:, s * SEQ:(s + 1) * SEQ], w[:, k, c * P:(c + 1) * P],
                                                xT[:, k, bass.ds((b + o) * SEQ, SEQ)],
                                                start=(k == 0), stop=(k == DC - 1))
                last.then_inc(sems["q_ready"], 1)

            def query_squares(b, o):
                pe.wait_ge(sems["q_out"], count(b, o, NQ, NQ))
                bank = at_spare(pe, b, o, NQ, False)
                for tile in range(TPB):
                    for c in range(NC):
                        col = tile * HEADS + 2 * c
                        last = nc.tensor.matmul(bank[:, col:col + 2], q2[:, c, tile * P:(tile + 1) * P],
                                                of_head[:], start=True, stop=True)
                last.then_inc(sems["sq_ready"], 1)

            def scores(b, o, g):
                tile, quad = divmod(g, GROUPS)
                if g < GROUPS:
                    if rope:
                        pe.wait_ge(sems["q_done"], count(b, o, 2, quad // 2 + 1))
                    else:
                        pe.wait_ge(sems["q_out"], count(b, o, NQ, min(quad + 1, NQ)))
                pe.wait_ge(sems["s_free" if own or mask else "shift"], count(b, o, STEPS, g - 1))
                rows = slice(tile * P, (tile + 1) * P)
                if hd == 16:
                    first = (quad % 2) * GROUP
                    last = nc.tensor.matmul(psum[:, g % 2, 0:GROUP * keys], qT[:, quad // 2, rows],
                                            keysT[:, quad // 2, b + o, first:first + GROUP, :], start=True, stop=True)
                else:
                    for s in range(2):
                        c = 2 * quad + s
                        last = nc.tensor.matmul(psum[:, g % 2, s * 2 * keys:(s + 1) * 2 * keys], qT[:, c, rows],
                                                keysT[:, c, b + o, :, :], start=True, stop=True)
                last.then_inc(sems["scored"], 1)

            def turn(b, o, g):
                pe.wait_ge(sems["probs"], count(b, o, STEPS, g + 1))
                pe.wait_ge(sems["pt_out"], count(b, o, STEPS, g - 1))
                for h in range(GROUP):
                    last = nc.tensor.transpose(psum[0:keys, 2 + g % 2, h * P:(h + 1) * P],
                                               probs[g % 2][:, h, :], ident[:])
                last.then_inc(sems["turned"], 1)

            def sums(b, o, g):
                quad = g % GROUPS
                pe.wait_ge(sems["pt_out"], count(b, o, STEPS, g + 1))
                pe.wait_ge(sems["normed"], count(b, o, STEPS, g - 1))
                for h in range(GROUP):
                    last = nc.tensor.matmul(psum[:, 4 + g % 2, h * (hd + 1):(h + 1) * (hd + 1)],
                                            probsT[g % 2][:, h * P:(h + 1) * P],
                                            values[:, b + o, quad * GROUP + h, :], start=True, stop=True)
                last.then_inc(sems["summed"], 1)

            def turn_sums(b, tile, end):
                pe.wait_ge(sems["normed"], count(b, 0, STEPS, (tile + 1) * GROUPS))
                for j in range(AT):
                    bank = at_spare(pe, b, 0, first_left + tile * (AT + 1) + j, end)
                    per = NC // AT
                    for q in range(per):
                        c = j * per + q
                        last = nc.tensor.transpose(
                            bank[:, q * P:(q + 1) * P],
                            att[tile][:].rearrange("p h d -> p (h d)")[:, c * P:(c + 1) * P], ident[:])
                    last.then_inc(sems["att_turned"], 1)

            def output(b, tile, end):
                pe.wait_ge(sems["left"], count(b, 0, LEFT, tile * (AT + 1) + AT))
                bank = at_spare(pe, b, 0, first_left + tile * (AT + 1) + AT, end)
                for c in range(NC):
                    last = nc.tensor.matmul(bank[:, 0:D], attT[tile][:, c, :], wo[:, c, :],
                                            start=(c == 0), stop=(c == NC - 1))
                last.then_inc(sems["y_ready"], 1)

            def prepare(b, o):
                for j in range(NQ):
                    queries(b, o, j)
                if own:
                    query_squares(b, o)

            def slot(b, s, end):
                item(scores, b, s, SCORES, end)
                if 0 <= s < len(Q_SLOTS) and not end:
                    for j in Q_SLOTS[s]:
                        queries(b, 1, j)
                if own and s == SQ_SLOT and not end:
                    query_squares(b, 1)
                item(turn, b, s, TURN, end)
                item(sums, b, s, SUMS, end)
                for tile in range(TPB):
                    if s == TURN_SLOT[tile]:
                        turn_sums(b, tile, end)
                    if s == OUT_SLOT[tile]:
                        output(b, tile, end)

            pe.wait_ge(sems["loaded"], 16 * len(loads))
            stream(pe, prepare, slot)

        @block.scalar
        def _(act):
            def queries_out(b, o, j):
                act.wait_ge(sems["q_ready"], count(b, o, NQ, j + 1))
                if own:
                    act.wait_ge(sems["scored"], count(b, o, STEPS, j + 1 - GROUPS))
                    both = spare(j).rearrange("p (c s) -> p c s", c=2)
                    nc.scalar.activation(q2[:, 2 * j:2 * j + 2, :], both, ACT.Square)
                    nc.scalar.activation(qT[:, 2 * j:2 * j + 2, :], both, ACT.Copy,
                                         scale=q_scale[:]).then_inc(sems["q_out"], 1)
                    return
                if rope:
                    act.wait_ge(sems["q_done"], count(b, o, 2, 0))
                for s in range(2):
                    c = (2 * j + s) % NC
                    if not rope:
                        read = GROUPS // NC * (s + 1) if hd == 16 else j + 1
                        act.wait_ge(sems["scored"], count(b, o, STEPS, read - GROUPS))
                    turned = rope and j >= NQ // 2
                    dst = (qr if turned else q_raw) if rope else qT
                    last = nc.scalar.activation(dst[:, c, :], spare(j)[:, s * SEQ:(s + 1) * SEQ], ACT.Identity,
                                                bias=(bqr if turned else bq)[:, c:c + 1])
                last.then_inc(sems["q_out"], 1)

            def exps(b, o, g):
                act.wait_ge(sems["shift"], count(b, o, STEPS, g + 1))
                act.wait_ge(sems["turned"], count(b, o, STEPS, g - 1))
                nc.scalar.activation(probs[g % 2][:], shifted[g % 2][:], ACT.Exp,
                                     scale=cfg["scale"]).then_inc(sems["probs"], 1)

            def turned_out(b, o, g):
                act.wait_ge(sems["turned"], count(b, o, STEPS, g + 1))
                act.wait_ge(sems["summed"], count(b, o, STEPS, g - 1))
                nc.scalar.activation(probsT[g % 2][:], psum[0:keys, 2 + g % 2, :], ACT.Copy).then_inc(
                    sems["pt_out"], 1)

            def prepare(b, o):
                for j in range(NQ):
                    queries_out(b, o, j)

            def slot(b, s, end):
                item(exps, b, s, EXPS, end)
                if 0 <= s < len(Q_SLOTS) and not end:
                    for j in Q_SLOTS[s]:
                        queries_out(b, 1, j)
                item(turned_out, b, s, TURN, end)

            act.wait_ge(sems["loaded"], 16 * len(loads))
            stream(act, prepare, slot)

        if own:
            @block.gpsimd
            def _(pool):
                with pool.Fori(0, NBATCH) as bi:
                    pool.wait_ge(sems["sq_out"], bi + 1)
                    nc.gpsimd.tensor_tensor(qrn[:].rearrange("p t h -> p (t h)"), qss[:].rearrange("p t h -> p (t h)"),
                                            env["half32"][:], ALU.pow).then_inc(sems["q_inverted"], 1)
                pool.wait_ge(sems["var_done"], 1)
                nc.gpsimd.tensor_tensor(env["rstd"][:], env["var"][:], env["half"][:], ALU.pow).then_inc(
                    sems["rstd_done"], 1)

        @block.vector
        def _(dve):
            step = Step(dve, sems["chain"], per=STEPS * (3 if mask else 2) + (2 if rope else 0))
            dve.wait_ge(sems["loaded"], 16 * len(loads))

            def soft(b, o, g):
                tile, quad = divmod(g, GROUPS)
                s3 = psum[:, g % 2, 0:GROUP * keys].rearrange("p (h k) -> p h k", k=keys)
                dst, mx = shifted[g % 2], top[g % 2]
                if own and g == 0:
                    dve.wait_ge(sems["q_inverted"], count(b, o, 1, 1))
                dve.wait_ge(sems["scored"], count(b, o, STEPS, g + 1))
                dve.wait_ge(sems["probs"], count(b, o, STEPS, g - 1))
                source = dst[:]
                if own:
                    ins = nc.vector.tensor_tensor(
                        dst[:], s3, qrn[:, tile, quad * GROUP:(quad + 1) * GROUP].unsqueeze(2).to_broadcast(wide),
                        ALU.mult)
                elif mask == "given":
                    row = t["mask_mul"][:, bass.ds((b + o) * TPB + tile, 1), :].to_broadcast(wide)
                    ins = nc.vector.tensor_tensor(dst[:], s3, row, ALU.mult)
                elif mask == "window":
                    ins = nc.vector.tensor_tensor(dst[:], s3, window[:, tile, :].unsqueeze(1).to_broadcast(wide),
                                                  ALU.add)
                else:
                    ins, source = None, s3
                if ins is not None:
                    ins.then_inc(sems["s_free"], 1)
                    dve.wait_ge(sems["s_free"], count(b, o, STEPS, g + 1))
                if mask == "given":
                    row = t["mask_add"][:, bass.ds((b + o) * TPB + tile, 1), :].to_broadcast(wide)
                    step.then(nc.vector.tensor_tensor(dst[:], dst[:], row, ALU.add))
                step.then(nc.vector.tensor_reduce(mx[:], source, AX.X, ALU.max))
                nc.vector.tensor_tensor(dst[:], source, mx[:].unsqueeze(2).to_broadcast(wide),
                                        ALU.subtract).then_inc(sems["shift"], 1)

            def norm(b, o, g):
                tile, quad = divmod(g, GROUPS)
                dve.wait_ge(sems["summed"], count(b, o, STEPS, g + 1))
                if quad == 0:
                    dve.wait_ge(sems["att_turned"], count(b, o, TPB * AT, (tile + 1 - TPB) * AT))
                o3 = psum[:, 4 + g % 2, 0:GROUP * (hd + 1)].rearrange("p (h d) -> p h d", d=hd + 1)
                step.then(nc.vector.reciprocal(inv[g % 2][:], o3[:, :, hd]))
                if mask == "window":
                    step.then(nc.vector.tensor_scalar(inv[g % 2][:], inv[g % 2][:], seen[:, tile:tile + 1], None,
                                                      ALU.mult))
                nc.vector.tensor_tensor(att[tile][:, quad * GROUP:(quad + 1) * GROUP, :], o3[:, :, 0:hd],
                                        inv[g % 2][:].unsqueeze(2).to_broadcast([P, GROUP, hd]),
                                        ALU.mult).then_inc(sems["normed"], 1)

            def copy_turned(b, tile):
                per = NC // AT
                for j in range(AT):
                    dve.wait_ge(sems["att_turned"], count(b, 0, TPB * AT, tile * AT + j + 1))
                    nc.vector.tensor_copy(attT[tile][:, j * per:(j + 1) * per, :],
                                          spare(first_left + tile * (AT + 1) + j)[:, 0:per * P].rearrange(
                                              "p (c s) -> p c s", s=P)).then_inc(sems["left"], 1)

            def add_output(b, tile):
                dve.wait_ge(sems["y_ready"], count(b, 0, TPB, tile + 1))
                y = spare(first_left + tile * (AT + 1) + AT)[:, 0:D]
                where = bass.ds(b * TPB + tile, 1)
                if own:
                    nc.vector.tensor_scalar(y_all[:, where, :], y.unsqueeze(1), 1.0, None, ALU.mult).then_inc(
                        sems["left"], 1)
                else:
                    nc.vector.scalar_tensor_tensor(x[:, where, :], y.unsqueeze(1), gate, x[:, where, :],
                                                   ALU.mult, ALU.add).then_inc(sems["left"], 1)

            def turn_positions(b, o):
                table = lambda v: v[:].unsqueeze(1).to_broadcast([P, NC, SEQ])
                dve.wait_ge(sems["q_out"], count(b, o, NQ, NQ))
                step.did(nc.vector.tensor_tensor(q_raw[:], q_raw[:], table(cos), ALU.mult))
                step.then(nc.vector.tensor_tensor(qr[:], qr[:], table(sin), ALU.mult))
                for c in range(NC):
                    dve.wait_ge(sems["scored"], count(b, o, STEPS, GROUPS // NC * (c + 1) - GROUPS))
                    nc.vector.tensor_tensor(qT[:, c, :], q_raw[:, c, :], qr[:, c, :], ALU.add).then_inc(
                        sems["q_done"], 1)

            def sum_squares(b, o):
                dve.wait_ge(sems["sq_ready"], count(b, o, 1, 1))
                nc.vector.tensor_scalar(qss[:].rearrange("p t h -> p (t h)"), spare(NQ)[:, 0:TPB * HEADS], 1e-24,
                                        None, ALU.max).then_inc(sems["sq_out"], 1)

            def prepare(b, o):
                if rope:
                    turn_positions(b, o)
                if own:
                    sum_squares(b, o)

            def slot(b, s, end):
                if own and s == SQ_SLOT and not end:
                    sum_squares(b, 1)
                item(soft, b, s, SCORES, end)
                if rope and s == 0 and not end:
                    turn_positions(b, 1)
                item(norm, b, s, SUMS, end)
                for tile in range(TPB):
                    if s == TURN_SLOT[tile]:
                        copy_turned(b, tile)
                    if s == OUT_SLOT[tile]:
                        add_output(b, tile)

            stream(dve, prepare, slot, step)
            if own:
                dve.wait_ge(sems["left"], NBATCH * LEFT)
                emit_statistics(env, dve, y_all, sems["stats"], sems["var_done"])
                dve.wait_ge(sems["rstd_done"], 1)
                for tile in range(TILES):
                    nc.vector.tensor_scalar(y_all[:, tile, :], y_all[:, tile, :], env["mv"][:, tile, 0:1],
                                            env["rstd"][:, tile:tile + 1], ALU.subtract, ALU.mult).then_inc(
                                                sems["applied"], 1)
                dve.wait_ge(sems["applied"], TILES)
                nc.vector.tensor_tensor(y_all[:], y_all[:], t["gain"][:].unsqueeze(1).to_broadcast([P, TILES, D]),
                                        ALU.mult).then_inc(sems["gained"], 1)
                dve.wait_ge(sems["gained"], 1)
                nc.vector.tensor_tensor(x[:], x[:], y_all[:], ALU.add).then_inc(sems["gained"], 1)


def _chunks(w):
    r, c = w.shape
    return np.ascontiguousarray(w.reshape(r // P, P, c).transpose(1, 0, 2))


def _units(w1, w2, b1=None):
    out = [np.stack([_chunks(w) for w in w1]), np.stack([_chunks(w) for w in w2])]
    if b1 is not None:
        out.append(np.ascontiguousarray(np.stack([b.reshape(UNIT // P, P).T for b in b1], axis=1)))
    return out


def layout(inputs):
    a = {k: np.asarray(v) for k, v in inputs.items()}
    out = {"x": a["x"], "g_xattn": a["g_xattn"], "g_ffn": a["g_ffn"]}
    ctx = a["ctx_1024"]
    out["ctxT"] = _chunks(np.ascontiguousarray(ctx.reshape(-1, D).T))
    out["ctx"] = np.ascontiguousarray(ctx.transpose(1, 0, 2))
    out["mask"] = np.ascontiguousarray(
        a["mask_BxSxS2_bf1"].view(np.uint8).reshape(TILES, P, CTX).transpose(1, 0, 2))
    out["ident"] = np.eye(P, dtype=np.float32)
    out["rank"] = np.ascontiguousarray(np.broadcast_to((8 - np.arange(8)).astype(np.float32), (P, TILES, 8)))
    w1 = [*a["L0_ffn_rw1"], a["L0_ffn_sw1"]]
    w2 = [*a["L0_ffn_rw2"], a["L0_ffn_sw2"]]
    out["f0_w1"], out["f0_w2"], out["f0_b1"] = _units(w1, w2, [*a["L0_ffn_rb1"], a["L0_ffn_sb1"]])
    out["f0_b2"] = np.concatenate([a["L0_ffn_rb2"], a["L0_ffn_sb2"][None]])
    out["f0_wr"], out["f0_rb"] = _chunks(a["L0_ffn_router_w"]), a["L0_ffn_router_b"]
    halves = [slice(0, UNIT), slice(UNIT, 2 * UNIT)]
    out["f1_w1"], out["f1_w2"], out["f1_b1"] = _units(
        [w[:, h] for w in a["L1_ffn_W1"] for h in halves], [w[h] for w in a["L1_ffn_W2"] for h in halves],
        [b[h] for b in a["L1_ffn_b1"] for h in halves])
    out["f1_b2"], out["f1_wr"], out["f1_rb"] = a["L1_ffn_b2"], _chunks(a["L1_ffn_Wr"]), a["L1_ffn_br"]
    wi, wo = a["L2_ffn_wi_W"].T, a["L2_ffn_wo_W"].T
    out["f2_w1"], out["f2_w2"], out["f2_b1"] = _units(
        [wi[:, h] for h in halves], [wo[h] for h in halves], [a["L2_ffn_wi_b"][h] for h in halves])
    out["f2_b2"], out["f2_rb"] = a["L2_ffn_wo_b"][None], a["L2_ffn_gate_b"]
    out["f2_wr"] = _chunks(np.concatenate([a["L2_ffn_gate_W"], a["L2_ffn_lora_A"].reshape(-1, D)]).T)
    lb = a["L2_ffn_lora_B"].transpose(0, 2, 1).reshape(32, 2, UNIT)
    out["f2_lb"] = np.ascontiguousarray(lb)
    w1 = [np.concatenate([p, q]).T for p, q in zip(a["L3_ffn_w1"], a["L3_ffn_w3"])]
    w2 = [w.T for w in a["L3_ffn_w2"]]
    for h in (slice(0, D), slice(D, 2 * D)):
        w1.append(np.concatenate([a["L3_ffn_sw1"][h], a["L3_ffn_sw3"][h]]).T)
        w2.append(a["L3_ffn_sw2"][:, h].T)
    out["f3_w1"], out["f3_w2"] = _units(w1, w2)
    out["f3_wr"], out["f3_rb"] = _chunks(a["L3_ffn_gate_w"].T), a["L3_ffn_gate_bias"]
    for n in range(4):
        c, pre = ATTN[n], f"L{n}_xattn_"
        w = {k: a[pre + k] for k in ("Wq", "Wk", "Wv", "Wo") if pre + k in a}
        if n == 1:
            w["Wk"], w["Wv"] = a[pre + "Wkv"][:, :HEADS * c["hd"]], a[pre + "Wkv"][:, HEADS * c["hd"]:]
        if n in (0, 3):
            w = {k: v.T for k, v in w.items()}
        for k, v in w.items():
            out[f"a{n}_w{k[1]}"] = _chunks(v)
        if n != 1:
            for k in ("bq", "bk"):
                out[f"a{n}_{k}"] = np.ascontiguousarray(a[pre + k].reshape(-1, P).T)
            out[f"a{n}_bv"], out[f"a{n}_bo"] = a[pre + "bv"], a[pre + "bo"]
    per_feature = lambda g, b: np.ascontiguousarray(np.stack([g, b]).reshape(2, DC, P).transpose(2, 0, 1))
    out["a1_ln_in"] = per_feature(a["L1_xattn_ln_in_g"], a["L1_xattn_ln_in_b"])
    out["a1_ln_ctx"] = per_feature(a["L1_xattn_ln_ctx_g"], a["L1_xattn_ln_ctx_b"])
    out["a1_ln_out"] = np.stack([a["L1_xattn_ln_out_g"], a["L1_xattn_ln_out_b"]])
    out["a1_k_scale"] = a["L1_xattn_k_scale"]
    out["a1_q_scale"] = np.ascontiguousarray(np.tile(a["L1_xattn_q_scale"], 2)[:, None])
    null = a["L1_xattn_null_kv"]
    out["a1_null"] = np.ascontiguousarray(np.broadcast_to(null[0], (1, 1, HEADS, 64)))
    out["a1_null_v"] = np.ascontiguousarray(np.broadcast_to(null[1], (1, NBATCH, HEADS, 64)))
    partner = (np.arange(D) // 16) * 16 + (np.arange(D) + 8) % 16
    for k in "qk":
        out[f"a3_w{k}r"] = _chunks(a[f"L3_xattn_W{k}"][partner].T)
        out[f"a3_b{k}r"] = np.ascontiguousarray(a[f"L3_xattn_b{k}"][partner].reshape(-1, P).T)
    f = np.arange(P)
    out["own_rows"] = (f[:, None] // 16 == np.arange(8)[None]).astype(np.float32)
    out["of_head"] = (f[:, None] // 64 == np.arange(2)[None]).astype(np.float32)
    freq = (1.0 / np.float32(10000.0) ** (np.arange(8, dtype=np.float32) / np.float32(8))).astype(np.float32)
    angle = np.arange(SEQ, dtype=np.float32)[None, :] * freq[f % 8][:, None]
    out["cos"] = np.cos(angle).astype(np.float32)
    out["sin"] = (np.sin(angle) * np.where(f % 16 < 8, -1.0, 1.0)[:, None]).astype(np.float32)
    tok, key = np.arange(SEQ).reshape(TPB, P).T[:, :, None], np.arange(CTX)[None, None]
    hidden = (key > tok) | (key < tok - 128)
    out["window"] = np.where(hidden, np.float32(MASKED), np.float32(0))
    out["seen"] = (~hidden.all(-1)).astype(np.float32)
    return {k: np.ascontiguousarray(v) for k, v in out.items()}


STAGES = [("a", 0), ("f", 0), ("a", 1), ("f", 1), ("a", 2), ("f", 2), ("a", 3), ("f", 3)]


def kernel(**inputs):
    import concourse.bacc as bacc
    from concourse.bass_utils import run_bass_kernel_spmd

    nc = bacc.Bacc("TRN2", target_bir_lowering=False, num_devices=1)
    arrays, dram = {}, {}
    for name, v in layout(inputs).items():
        arrays[f"in_{name}"] = v
        dram[name] = nc.dram_tensor(f"in_{name}", v.shape, mybir.dt.from_np(v.dtype), kind="ExternalInput").ap()
    out = nc.dram_tensor("out", (NBATCH, SEQ, D), F32, kind="ExternalOutput").ap()
    build(nc, dram, out, STAGES)
    return run_bass_kernel_spmd(nc, [arrays], core_ids=[0]).results[0]["out"]
```

```python
from contextlib import ExitStack

import concourse.bass as bass
import numpy as np
from concourse import mybir

F32 = mybir.dt.float32
F32R = mybir.dt.float32r
U8 = mybir.dt.uint8
ACT = mybir.ActivationFunctionType
ALU = mybir.AluOpType
AX = mybir.AxisListType

P = 128
NBATCH = 8
SEQ = 256
D = 256
DC = D // P
TOKENS = NBATCH * SEQ
TILES = TOKENS // P
TPB = SEQ // P
CTX = 77
HEADS = 16
GROUP = 4
GROUPS = HEADS // GROUP
EPS = 1e-5
BANK = 512
UNIT = 512
CHUNK = 512
CHUNKS = TOKENS // CHUNK
HUGE = 3.0e38
MASKED = -1.0e30
L2_FILL = -1.0e9

ATTN = [
    dict(name="a0", hd=16, keys=CTX, scale=0.25, rope=False, l2norm=False, mask=None),
    dict(name="a1", hd=64, keys=CTX + 1, scale=8.0, rope=False, l2norm=True, mask=None),
    dict(name="a2", hd=64, keys=CTX, scale=0.125, rope=False, l2norm=False, mask="given"),
    dict(name="a3", hd=16, keys=CTX, scale=0.25, rope=True, l2norm=False, mask="window"),
]
FFN = [
    dict(name="f0", units=9, per_expert=1, experts=8, gates=9, bias_rows=9, lora=0, act="gelu"),
    dict(name="f1", units=16, per_expert=2, experts=8, gates=8, bias_rows=8, lora=0, act="relu"),
    dict(name="f2", units=2, per_expert=2, experts=8, gates=1, bias_rows=1, lora=4, act="relu"),
    dict(name="f3", units=10, per_expert=1, experts=8, gates=10, bias_rows=0, lora=0, act="silu"),
]


class Tally:

    def __init__(self, sem, per=0, base=0):
        self.sem, self.per, self.base, self.k, self.i = sem, per, base, 0, 0

    def round(self, i):
        self.i, self.k = i, 0

    def add(self, ins):
        ins.then_inc(self.sem, 1)
        self.k += 1

    def value(self):
        return self.i * self.per + (self.base + self.k)


class Step:

    def __init__(self, engine, sem, per=0, base=0):
        self.engine, self.t = engine, Tally(sem, per, base)

    def round(self, i):
        self.t.round(i)

    def did(self, ins):
        self.t.add(ins)

    def then(self, ins):
        self.t.add(ins)
        self.engine.wait_ge(self.t.sem, self.t.value())

    def filled(self):
        self.t.base, self.t.k = self.t.base + self.t.k, 0

    def check(self):
        assert self.t.k == self.t.per, (self.t.k, self.t.per)


def build(nc, dram, out, stages):
    with ExitStack() as whole:

        in_use = []

        def sem(name):
            in_use.append(nc.alloc_semaphore(name=name))
            return in_use[-1]

        def clear_semaphores():
            nc.clear_and_free_semaphores(in_use)
            nc.all_engine_barrier()
            in_use.clear()

        def resident(name, shape, dt=F32):
            return whole.enter_context(nc.sbuf_tensor(name, shape, dt))

        psum = whole.enter_context(nc.psum_tensor("psum", [P, 8, BANK], F32))
        x = resident("residual", [P, TILES, D])
        ident = resident("identity", [P, P])
        half = resident("half", [P, TILES])
        zero = resident("zero", [P, 1])
        half32 = resident("half32", [P, TPB * HEADS])
        ctxT = resident("ctx_features", [P, DC, NBATCH * CTX])
        g_all = resident("g_all", [P, 8])
        tg = resident("tg", [P, 8])
        rank = resident("ranks", [P, TILES, 8])
        stats = resident("stats", [P, TILES, 6])
        mv = resident("mv", [P, TILES, 2])
        var = resident("var", [P, TILES])
        rstd = resident("rstd", [P, TILES])

        context_w = resident("context_w", [P, 4 * DC * D * 2])
        env = dict(nc=nc, context_w=context_w, dram=dram, sem=sem, psum=psum, x=x, ident=ident, half=half, zero=zero, half32=half32, ctxT=ctxT, tg=tg,
                   rank=rank, stats=stats, mv=mv, var=var, rstd=rstd)
        setup(env, g_all, stages[0][1] if stages[0][0] == "a" else None)
        for (kind, n), following in zip(stages, stages[1:] + [("", 0)]):
            with ExitStack() as scope:
                if kind == "a":
                    attention_layer(env, scope, n)
                else:
                    ffn_layer(env, scope, n, following[1] if following[0] == "a" else None)
            clear_semaphores()
        store(env, out)


def context_weights(env, n):
    inner = HEADS * ATTN[n]["hd"]
    names = ["wk", "wv"] + (["wkr"] if ATTN[n]["rope"] else [])
    return {w: env["context_w"][:, j * DC * inner:(j + 1) * DC * inner].rearrange("p (c i) -> p c i", c=DC)
            for j, w in enumerate(names)}


def context_weight_loads(env, n):
    return [(v, env["dram"][f"{ATTN[n]['name']}_{w}"]) for w, v in context_weights(env, n).items()]


def setup(env, g_all, first_attention):
    nc, dram, x = env["nc"], env["dram"], env["x"]
    loaded, gates_loaded, made, tanhed = (env["sem"](n) for n in ("loaded", "gates_loaded", "made", "tanhed"))
    with nc.Block() as block:
        @block.sync
        def _(sp):
            sp.dma_start(x[:], dram["x"].rearrange("b (h p) d -> p (b h) d", p=P)).then_inc(loaded, 16)
            sp.dma_start(env["ctxT"][:], dram["ctxT"]).then_inc(loaded, 16)
            sp.dma_start(env["ident"][:], dram["ident"]).then_inc(loaded, 16)
            sp.dma_start(env["rank"][:], dram["rank"]).then_inc(loaded, 16)
            ahead = [] if first_attention is None else context_weight_loads(env, first_attention)
            for dst, src in ahead:
                sp.dma_start(dst, src).then_inc(loaded, 16)
            sp.wait_ge(loaded, 16 * (4 + len(ahead)))

        @block.scalar
        def _(act):
            act.dma_start(g_all[:, 0:4], dram["g_xattn"].partition_broadcast(P)).then_inc(gates_loaded, 16)
            act.dma_start(g_all[:, 4:8], dram["g_ffn"].partition_broadcast(P)).then_inc(gates_loaded, 16)
            act.wait_ge(gates_loaded, 32)
            nc.scalar.activation(env["tg"][:], g_all[:], ACT.Tanh).then_inc(tanhed, 1)

        @block.gpsimd
        def _(pool):
            nc.gpsimd.memset(env["half"][:], -0.5).then_inc(made, 1)
            nc.gpsimd.memset(env["half32"][:], -0.5).then_inc(made, 1)
            nc.gpsimd.memset(env["zero"][:], 0.0).then_inc(made, 1)


def store(env, out):
    stored = env["sem"]("stored")
    with env["nc"].Block() as block:
        @block.sync
        def _(sp):
            sp.dma_start(out.rearrange("b (h p) d -> p (b h) d", p=P), env["x"][:]).then_inc(stored, 16)
            sp.wait_ge(stored, 16)


def emit_statistics(nc, dve, source, into, stats_done, var_done, rows=P, tiles=TILES):
    stats, mv, var = into["stats"], into["mv"], into["var"]
    for t in range(tiles):
        last = nc.vector.bn_stats(stats[0:rows, t, :], source[0:rows, t, :])
    last.then_inc(stats_done, 1)
    dve.wait_ge(stats_done, 1)
    for t in range(tiles):
        last = nc.vector.bn_aggr(mv[0:rows, t, :], stats[0:rows, t, :])
    last.then_inc(stats_done, 1)
    dve.wait_ge(stats_done, 2)
    nc.vector.tensor_scalar(var[0:rows, 0:tiles], mv[0:rows, 0:tiles, 1], EPS, None, ALU.add).then_inc(var_done, 1)


def ffn_layer(env, scope, n, following):
    cfg = FFN[n]
    nc = env["nc"]

    def sb(name, shape, dt=F32):
        return scope.enter_context(nc.sbuf_tensor(f"{cfg['name']}_{name}", shape, dt))

    t = dict(
        xh=sb("xh", [P, DC, TOKENS], F32R), xl=sb("xl", [P, DC, TOKENS], F32R),
        gates=sb("gates", [P, TILES, cfg["gates"]]),
    )
    if cfg["lora"]:
        t["uh"] = sb("uh", [32, TOKENS], F32R)
        t["ul"] = sb("ul", [32, TOKENS], F32R)
    r_sync, r_gpsimd, r_tensor, r_biases, r_scalar, r_vector = route(env, scope, n, t)
    e_sync, e_gpsimd, e_tensor, e_scalar, e_vector, credits = experts(env, scope, n, t)
    ahead = [] if following is None else context_weight_loads(env, following)
    ahead_in = env["sem"](f"{cfg['name']}_ahead_in")
    with nc.Block() as block:
        @block.sync
        def _(sp):
            r_sync(sp)
            e_sync(sp)
            for dst, src in ahead:
                sp.dma_start(dst, src).then_inc(ahead_in, 16)
            if ahead:
                sp.wait_ge(ahead_in, 16 * len(ahead))

        @block.gpsimd
        def _(pool):
            r_gpsimd(pool)
            e_gpsimd(pool)

        @block.tensor
        def _(pe):
            credits[0](pe)
            r_tensor(pe)
            e_tensor(pe, r_biases)

        @block.scalar
        def _(act):
            credits[1](act)
            r_scalar(act)
            e_scalar(act)

        @block.vector
        def _(dve):
            credits[2](dve)
            r_vector(dve)
            e_vector(dve)


def route(env, scope, n, t):
    cfg = FFN[n]
    nc, dram, psum, x, ident = env["nc"], env["dram"], env["psum"], env["x"], env["ident"]
    mv, var, rstd, tg, rank = env["mv"], env["var"], env["rstd"], env["tg"], env["rank"]
    name, E, NG, NB = cfg["name"], cfg["experts"], cfg["gates"], cfg["bias_rows"]
    NR = E * (1 + cfg["lora"])
    gate = tg[:, 4 + n:5 + n]
    xh, xl, gates = t["xh"], t["xl"], t["gates"]

    def sb(nm, shape, dt=F32):
        return scope.enter_context(nc.sbuf_tensor(f"{name}_{nm}_sb", shape, dt))

    wr = sb("wr", [P, DC, NR])
    rb = sb("rb", [P, E])
    xn = sb("xn", [P, 2, TPB, D])
    stage = sb("stage", [P, 2, DC, SEQ])
    logits = sb("logits", [P, TILES, E])
    a, b, c, oh1, oh2 = (sb(nm, [P, TILES, E]) for nm in ("ra", "rexp", "rc", "oh1", "oh2"))
    m1, m2 = sb("m1", [P, TILES]), sb("m2", [P, TILES])
    if NB:
        b2 = sb("b2", [NB, D])
        gT = sb("gT", [NB, 2, 512])
    if cfg["lora"]:
        um = sb("um", [P, TILES, 32])
        ust = sb("ust", [32, 2, 512])
    sems = {k: env["sem"](f"{name}_{k}") for k in (
        "consts", "stats1", "chain", "var_done", "rstd_done", "normed", "turned", "staged", "high",
        "low", "routed", "logits_read", "shifted", "exped", "gates_done", "gates_turned", "gates_copied", "bias_mm",
        "bias_added", "u_turned", "u_staged", "u_high")}
    xT_ps = lambda b: psum[:, 3 * (b % 2), :].rearrange("p (c s) -> p c s", c=DC)
    rt_ps = psum[:, 1:3, :].rearrange("p k (t r) -> p (k t) r", r=64)

    def sync(sp):
        sp.dma_start(wr[:], dram[f"{name}_wr"]).then_inc(sems["consts"], 16)
        sp.dma_start(rb[:], dram[f"{name}_rb"].partition_broadcast(P)).then_inc(sems["consts"], 16)
        if NB:
            sp.dma_start(b2[:], dram[f"{name}_b2"]).then_inc(sems["consts"], 16)
        sp.wait_ge(sems["consts"], 32 + 16 * bool(NB))

    def gpsimd(pool):
        pool.wait_ge(sems["var_done"], 1)
        nc.gpsimd.tensor_tensor(rstd[:], var[:], env["half"][:], ALU.pow).then_inc(sems["rstd_done"], 1)

    def vector(dve):
        step = Step(dve, sems["chain"])
        emit_statistics(nc, dve, x, env, sems["stats1"], sems["var_done"])
        dve.wait_ge(sems["rstd_done"], 1)
        for b_ in range(NBATCH + 1):
            if b_ < NBATCH:
                if b_ >= 2:
                    dve.wait_ge(sems["turned"], b_ - 1)
                for h in range(TPB):
                    tile = b_ * TPB + h
                    last = nc.vector.tensor_scalar(xn[:, b_ % 2, h, :], x[:, tile, :], mv[:, tile, 0:1],
                                                   rstd[:, tile:tile + 1], ALU.subtract, ALU.mult)
                last.then_inc(sems["normed"], 1)
            if b_ >= 1:
                dve.wait_ge(sems["high"], b_)
                where = slice((b_ - 1) * SEQ, b_ * SEQ)
                nc.vector.tensor_tensor(xl[:, :, where], stage[:, (b_ - 1) % 2], xh[:, :, where].bitcast(F32),
                                        ALU.subtract).then_inc(sems["low"], 1)
        dve.wait_ge(sems["routed"], NBATCH)
        dve.wait_ge(sems["consts"], 32 + 16 * bool(NB))
        wide = [P, TILES, E]

        def over(v):
            return v.unsqueeze(2).to_broadcast(wide)

        if n == 3:
            nc.vector.tensor_copy(logits[:], rt_ps[:, :, 0:E]).then_inc(sems["logits_read"], 1)
        else:
            nc.vector.tensor_tensor(logits[:], rt_ps[:, :, 0:E], rb[:].unsqueeze(1).to_broadcast(wide),
                                    ALU.add).then_inc(sems["logits_read"], 1)
        dve.wait_ge(sems["logits_read"], 1)

        def softmax_rows(dst):
            step.then(nc.vector.tensor_reduce(m1[:], logits[:], AX.X, ALU.max))
            nc.vector.tensor_tensor(a[:], logits[:], over(m1[:]), ALU.subtract).then_inc(sems["shifted"], 1)
            dve.wait_ge(sems["exped"], 1)
            step.then(nc.vector.tensor_reduce(m2[:], b[:], AX.X, ALU.add))
            step.then(nc.vector.reciprocal(m2[:], m2[:]))
            step.then(nc.vector.tensor_tensor(dst[:], b[:], over(m2[:]), ALU.mult))

        def first_largest(dst, values):
            step.then(nc.vector.tensor_reduce(m1[:], values[:], AX.X, ALU.max))
            step.then(nc.vector.tensor_tensor(dst[:], values[:], over(m1[:]), ALU.is_equal))
            step.then(nc.vector.tensor_tensor(dst[:], dst[:], rank[:], ALU.mult))
            step.then(nc.vector.tensor_reduce(m2[:], dst[:], AX.X, ALU.max))
            step.then(nc.vector.tensor_tensor(dst[:], dst[:], over(m2[:]), ALU.is_equal))

        def second_largest(values, spare):
            step.then(nc.vector.scalar_tensor_tensor(spare[:], oh1[:], -HUGE, values[:], ALU.mult, ALU.add))
            first_largest(oh2, spare)
            step.then(nc.vector.tensor_tensor(oh1[:], oh1[:], oh2[:], ALU.add))

        def set_gates(weights):
            return nc.vector.tensor_scalar(gates[:, :, 0:E], weights[:], gate, None, ALU.mult)

        def set_plain_gates(first):
            return nc.vector.tensor_scalar(gates[:, :, first:NG], rank[:, :, 0:NG - first], 0.0, gate,
                                           ALU.mult, ALU.add)

        if n in (0, 3):
            softmax_rows(c)
            if n == 3:
                step.then(nc.vector.tensor_tensor(b[:], c[:], rb[:].unsqueeze(1).to_broadcast(wide), ALU.add))
                first_largest(oh1, b)
                second_largest(b, a)
            else:
                first_largest(oh1, c)
                second_largest(c, a)
            step.then(nc.vector.tensor_tensor(a[:], c[:], oh1[:], ALU.mult))
            set_gates(a)
            last = set_plain_gates(E)
        elif n == 1:
            first_largest(oh1, logits)
            second_largest(logits, a)
            step.then(nc.vector.tensor_reduce(m1[:], logits[:], AX.X, ALU.max))
            nc.vector.tensor_tensor(a[:], logits[:], over(m1[:]), ALU.subtract).then_inc(sems["shifted"], 1)
            dve.wait_ge(sems["exped"], 1)
            step.then(nc.vector.tensor_tensor(c[:], b[:], oh1[:], ALU.mult))
            step.then(nc.vector.tensor_reduce(m2[:], c[:], AX.X, ALU.add))
            step.then(nc.vector.reciprocal(m2[:], m2[:]))
            step.then(nc.vector.tensor_tensor(a[:], c[:], over(m2[:]), ALU.mult))
            last = set_gates(a)
        else:
            softmax_rows(c)
            first_largest(oh1, c)
            set_plain_gates(0)
            with_r = [P, TILES, E, cfg["lora"]]
            last = nc.vector.tensor_tensor(
                um[:].rearrange("p t (e r) -> p t e r", r=cfg["lora"]),
                rt_ps[:, :, E:NR].rearrange("p t (e r) -> p t e r", r=cfg["lora"]),
                oh1[:].unsqueeze(3).to_broadcast(with_r), ALU.mult)
        last.then_inc(sems["gates_done"], 1)
        if cfg["lora"]:
            for k in range(4):
                dve.wait_ge(sems["u_high"], k + 1)
                nc.vector.tensor_tensor(t["ul"][:, k * 512:(k + 1) * 512], ust[:, k % 2, :],
                                        t["uh"][:, k * 512:(k + 1) * 512].bitcast(F32),
                                        ALU.subtract).then_inc(sems["u_staged"], 1)

        for k in range(TILES // 2 if NB else 0):
            dve.wait_ge(sems["bias_mm"], k + 1)
            nc.vector.tensor_tensor(x[:, 2 * k:2 * k + 2, :], x[:, 2 * k:2 * k + 2, :],
                                    psum[:, 6 + k % 2, :].rearrange("p (t d) -> p t d", t=2),
                                    ALU.add).then_inc(sems["bias_added"], 1)
    def scalar(act):
        for b_ in range(NBATCH):
            act.wait_ge(sems["turned"], b_ + 1)
            if b_ >= 2:
                act.wait_ge(sems["low"], b_ - 1)
                act.wait_ge(sems["routed"], b_ - 1)
            nc.scalar.activation(stage[:, b_ % 2], xT_ps(b_), ACT.Copy).then_inc(sems["staged"], 1)
            nc.scalar.activation(xh[:, :, b_ * SEQ:(b_ + 1) * SEQ], xT_ps(b_), ACT.Copy).then_inc(sems["high"], 1)
        act.wait_ge(sems["shifted"], 1)
        nc.scalar.activation(b[:], a[:], ACT.Exp).then_inc(sems["exped"], 1)
        for k in range(4 if cfg["lora"] else 0):
            act.wait_ge(sems["u_turned"], k + 1)
            if k >= 2:
                act.wait_ge(sems["u_staged"], k - 1)
            nc.scalar.activation(ust[:, k % 2, :], psum[0:32, 4 + k % 2, :], ACT.Copy)
            nc.scalar.activation(t["uh"][:, k * 512:(k + 1) * 512], psum[0:32, 4 + k % 2, :], ACT.Copy).then_inc(
                sems["u_high"], 1)

        for k in range(4 if NB else 0):
            act.wait_ge(sems["gates_turned"], k + 1)
            if k >= 2:
                act.wait_ge(sems["bias_mm"], 2 * (k - 1))
            nc.scalar.activation(gT[:, k % 2, :], psum[0:NB, 4 + k % 2, :], ACT.Copy).then_inc(
                sems["gates_copied"], 1)
    def tensor(pe):
        pe.wait_ge(sems["consts"], 32 + 16 * bool(NB))
        for b_ in range(NBATCH + 1):
            if b_ < NBATCH:
                pe.wait_ge(sems["normed"], b_ + 1)
                if b_ >= 2:
                    pe.wait_ge(sems["high"], b_ - 1)
                for c_ in range(DC):
                    for h in range(TPB):
                        last = nc.tensor.transpose(xT_ps(b_)[:, c_, h * P:(h + 1) * P],
                                                   xn[:, b_ % 2, h, c_ * P:(c_ + 1) * P], ident[:])
                last.then_inc(sems["turned"], 1)
            if b_ >= 1:
                pe.wait_ge(sems["staged"], b_)
                for h in range(TPB):
                    for c_ in range(DC):
                        last = nc.tensor.matmul(rt_ps[:, (b_ - 1) * TPB + h, 0:NR],
                                                stage[:, (b_ - 1) % 2, c_, h * P:(h + 1) * P],
                                                wr[:, c_, :], start=(c_ == 0), stop=(c_ == DC - 1))
                last.then_inc(sems["routed"], 1)
        pe.wait_ge(sems["low"], NBATCH)
        pe.wait_ge(sems["gates_done" if cfg["lora"] else "logits_read"], 1)
        if cfg["lora"]:
            low_rank_inputs(pe)

    def turn_gates(pe, k):
        if k >= 2:
            pe.wait_ge(sems["gates_copied"], k - 1)
        for q in range(4):
            last = nc.tensor.transpose(psum[0:NB, 4 + k % 2, q * P:(q + 1) * P],
                                       gates[:, 4 * k + q, 0:NB], ident[:])
        last.then_inc(sems["gates_turned"], 1)

    def add_biases(pe, k):
        pe.wait_ge(sems["gates_copied"], k // 2 + 1)
        if k >= 2:
            pe.wait_ge(sems["bias_added"], k - 1)
        for q in range(2):
            tt = 2 * k + q
            last = nc.tensor.matmul(psum[:, 6 + k % 2, q * D:(q + 1) * D],
                                    gT[:, tt // 4 % 2, tt % 4 * P:(tt % 4 + 1) * P], b2[:], start=True, stop=True)
        last.then_inc(sems["bias_mm"], 1)

    def low_rank_inputs(pe):
        for k in range(4):
            if k >= 2:
                pe.wait_ge(sems["u_high"], k - 1)
            for q in range(4):
                last = nc.tensor.transpose(psum[0:32, 4 + k % 2, q * P:(q + 1) * P], um[:, 4 * k + q, :], ident[:])
            last.then_inc(sems["u_turned"], 1)
        pe.wait_ge(sems["u_staged"], 4)

    def biases(pe):
        if NB:
            pe.wait_ge(sems["gates_done"], 1)
            turn_gates(pe, 0)
            for k in range(4):
                if k < 3:
                    turn_gates(pe, k + 1)
                add_biases(pe, 2 * k)
                add_biases(pe, 2 * k + 1)
            pe.wait_ge(sems["bias_added"], TILES // 2)

    return sync, gpsimd, tensor, biases, scalar, vector


def experts(env, scope, n, t):
    cfg = FFN[n]
    nc, dram, psum, x = env["nc"], env["dram"], env["psum"], env["x"]
    name, U = cfg["name"], cfg["units"]
    silu = cfg["act"] == "silu"
    HB = UNIT // P
    HC = HB // 2 if silu else HB
    xh, xl, gates = t["xh"], t["xl"], t["gates"]
    func = {"gelu": ACT.Gelu, "relu": ACT.Relu, "silu": ACT.Silu}[cfg["act"]]
    pairs, odd = divmod(U, 2)
    looped = pairs - (0 if odd else 1)

    def sb(nm, shape, dt=F32):
        return scope.enter_context(nc.sbuf_tensor(f"{name}_{nm}_sb", shape, dt))

    zero = env["zero"][:]
    w1raw = [sb(f"w1raw{s}", [P, DC, UNIT]) for s in range(2)]
    w2raw = [sb(f"w2raw{s}", [P, HC, D]) for s in range(2)]
    w1h = [sb(f"w1h{s}", [P, DC, UNIT], F32R) for s in range(2)]
    w1l = [sb(f"w1l{s}", [P, DC, UNIT], F32R) for s in range(2)]
    w2h = [sb(f"w2h{s}", [P, HC, D], F32R) for s in range(2)]
    w2l = [sb(f"w2l{s}", [P, HC, D], F32R) for s in range(2)]
    h32 = sb("h32", [P, HC, CHUNK])
    hh = sb("hh", [P, 2, HC, CHUNK], F32R)
    hl = sb("hl", [P, 2, HC, CHUNK], F32R)
    b1 = None if silu else sb("b1", [P, U, HB])
    b1u = None if silu else sb("b1u", [P, 2, HB])
    s32 = sb("s32", [P, HC, CHUNK]) if silu else None
    if cfg["lora"]:
        lb = h32[0:32, 0:U, :]
        lbh, lbl = sb("lbh", [32, U, UNIT], F32R), sb("lbl", [32, U, UNIT], F32R)
    sems = {k: env["sem"](f"{name}x_{k}") for k in (
        "bias_in", "raw_in0", "raw_in1", "split_high", "split", "hidden", "gated", "multiplied",
        "activated", "lowered", "product", "added", "lora_split", "bias_set")}
    SPLIT0 = 3
    HID0 = HC if silu else HB
    LOW0 = HC
    PROD0 = 4 * CHUNKS + 1
    ADD0 = 4
    hid_ps = [psum[:, m, :] for m in range(HB)]
    y_ps = [psum[:, 4 + q, 0:D] for q in range(4)]

    def run(engine, body):
        if looped:
            with engine.Fori(0, looped) as i:
                body(i, 0, False)
                body(i, 1, False)
        body(looped, 0, bool(odd))
        if not odd:
            body(looped, 1, True)

    def run_ahead(engine, first, second, between=None):
        def body(i, s, last):
            for c in range(CHUNKS):
                if c < CHUNKS - 1:
                    first(i, s, c + 1)
                elif not last:
                    first(i + s, 1 - s, 0)
                second(i, s, c)

        first(0, 0, 0)
        if between:
            between(engine)
        run(engine, body)

    def sync(sp):
        if b1 is not None:
            sp.dma_start(b1[:], dram[f"{name}_b1"]).then_inc(sems["bias_in"], 16)
        if cfg["lora"]:
            sp.dma_start(lb[:], dram[f"{name}_lb"]).then_inc(sems["bias_in"], 16)

        def body(i, s, last):
            u = i * 2 + s
            sp.wait_ge(sems["split"], u * 2 + SPLIT0 - 2)
            sp.dma_start(w1raw[s][:], dram[f"{name}_w1"][u]).then_inc(sems[f"raw_in{s}"], 16)
            sp.dma_start(w2raw[s][:], dram[f"{name}_w2"][u]).then_inc(sems[f"raw_in{s}"], 16)

        run(sp, body)

    def gpsimd(pool):
        pool.sem_inc(sems["split"], SPLIT0)
        if cfg["lora"]:
            pool.wait_ge(sems["bias_in"], 32)
            nc.gpsimd.tensor_copy(lbh[:], lb[:]).then_inc(sems["lora_split"], 1)
            pool.wait_ge(sems["lora_split"], 1)
            nc.gpsimd.tensor_tensor(lbl[:], lb[:], lbh[:].bitcast(F32), ALU.subtract).then_inc(
                sems["lora_split"], 1)

        def body(i, s, last):
            u = i * 2 + s
            pool.wait_ge(sems[f"raw_in{s}"], i * 32 + 32)
            pool.wait_ge(sems["product"], u * 4 * CHUNKS + PROD0 - 4 * CHUNKS)
            nc.gpsimd.tensor_tensor(w1h[s][:], w1raw[s][:], zero.unsqueeze(2).to_broadcast([P, DC, UNIT]),
                                    ALU.add).then_inc(sems["split_high"], 1)
            nc.gpsimd.tensor_tensor(w2h[s][:], w2raw[s][:], zero.unsqueeze(2).to_broadcast([P, HC, D]),
                                    ALU.add).then_inc(sems["split_high"], 1)
            pool.wait_ge(sems["split_high"], u * 2 + 2)
            nc.gpsimd.tensor_tensor(w1l[s][:], w1raw[s][:], w1h[s][:].bitcast(F32),
                                    ALU.subtract).then_inc(sems["split"], 1)
            nc.gpsimd.tensor_tensor(w2l[s][:], w2raw[s][:], w2h[s][:].bitcast(F32),
                                    ALU.subtract).then_inc(sems["split"], 1)

        run(pool, body)

    def tensor(pe, between):
        if cfg["lora"]:
            pe.wait_ge(sems["lora_split"], 2)

        def first(i, s, c):
            u = i * 2 + s
            g = u * CHUNKS + c
            if c == 0:
                pe.wait_ge(sems["split"], u * 2 + 2 + SPLIT0)
            tok = slice(c * CHUNK, (c + 1) * CHUNK)
            for m in range(HB):
                if not silu:
                    pe.wait_ge(sems["activated"], g * HB + m + 1)
                else:
                    pe.wait_ge(sems["gated" if m < HC else "multiplied"], g * HC + m % HC + 1)
                cols = slice(m * P, (m + 1) * P)
                terms = [(w[s][:, k, cols], v[:, k, tok]) for k in range(DC)
                         for w, v in ((w1h, xh), (w1h, xl), (w1l, xh))]
                if cfg["lora"]:
                    terms += [(w[:, u, cols], v[:, tok]) for w, v in
                              ((lbh, t["uh"]), (lbh, t["ul"]), (lbl, t["uh"]))]
                for j, (w, v) in enumerate(terms):
                    last = nc.tensor.matmul(hid_ps[m], w, v, start=(j == 0), stop=(j == len(terms) - 1))
                last.then_inc(sems["hidden"], 1)

        def second(i, s, c):
            g = (i * 2 + s) * CHUNKS + c
            pe.wait_ge(sems["lowered"], g * HC + HC + LOW0)
            for q in range(4):
                pe.wait_ge(sems["added"], g * 4 + q + 1)
                tok = slice(q * P, (q + 1) * P)
                terms = [(v[:, c % 2, k, tok], w[s][:, k, :]) for k in range(HC)
                         for v, w in ((hh, w2h), (hh, w2l), (hl, w2h))]
                for j, (v, w) in enumerate(terms):
                    last = nc.tensor.matmul(y_ps[q], v, w, start=(j == 0), stop=(j == len(terms) - 1))
                last.then_inc(sems["product"], 1)

        run_ahead(pe, first, second, between)

    def scalar(act):
        if b1 is not None:
            act.wait_ge(sems["bias_in"], 16 + 16 * bool(cfg["lora"]))

        def plain(i, s, last):
            u = i * 2 + s
            nc.scalar.activation(b1u[:, s, :], b1[:, u, :], ACT.Copy).then_inc(sems["bias_set"], 1)
            for c in range(CHUNKS):
                g = u * CHUNKS + c
                if c == 0:
                    act.wait_ge(sems["bias_set"], u + 1)
                act.wait_ge(sems["product"], g * 4 + 4 + PROD0 - 8)
                for m in range(HB):
                    act.wait_ge(sems["hidden"], g * HB + m + 1)
                    act.wait_ge(sems["lowered"], g * HC + m + 1)
                    bias = b1u[:, s, m:m + 1]
                    nc.scalar.activation(h32[:, m, :], hid_ps[m], func, bias=bias)
                    nc.scalar.activation(hh[:, c % 2, m, :], hid_ps[m], func, bias=bias).then_inc(
                        sems["activated"], 1)

        def with_product(i, s, last):
            u = i * 2 + s
            for c in range(CHUNKS):
                g = u * CHUNKS + c
                act.wait_ge(sems["product"], g * 4 + 4 + PROD0 - 8)
                for m in range(HC):
                    act.wait_ge(sems["hidden"], g * HB + m + 1)
                    act.wait_ge(sems["multiplied"], g * HC + m + 1)
                    nc.scalar.activation(s32[:, m, :], hid_ps[m], func).then_inc(sems["gated"], 1)
                for m in range(HC):
                    act.wait_ge(sems["multiplied"], g * HC + m + 1 + HID0)
                    nc.scalar.activation(hh[:, c % 2, m, :], h32[:, m, :], ACT.Copy).then_inc(
                        sems["activated"], 1)

        run(act, with_product if silu else plain)

    def vector(dve):
        def first(i, s, c):
            g = (i * 2 + s) * CHUNKS + c
            if silu:
                for m in range(HC):
                    dve.wait_ge(sems["gated"], g * HC + m + 1 + HID0)
                    dve.wait_ge(sems["hidden"], g * HB + HC + m + 1)
                    dve.wait_ge(sems["lowered"], g * HC + m + 1)
                    nc.vector.tensor_tensor(h32[:, m, :], s32[:, m, :], hid_ps[HC + m], ALU.mult).then_inc(
                        sems["multiplied"], 1)
            for m in range(HC):
                dve.wait_ge(sems["activated"], g * HC + m + 1 + (0 if silu else HID0))
                nc.vector.tensor_tensor(hl[:, c % 2, m, :], h32[:, m, :], hh[:, c % 2, m, :].bitcast(F32),
                                        ALU.subtract).then_inc(sems["lowered"], 1)

        def second(i, s, c):
            u = i * 2 + s
            g = u * CHUNKS + c
            column = (i if cfg["per_expert"] == 2 else u)
            for q in range(4):
                tile = c * 4 + q
                dve.wait_ge(sems["product"], g * 4 + q + 1 + PROD0)
                nc.vector.scalar_tensor_tensor(x[:, tile, :], y_ps[q], gates[:, tile, bass.ds(column, 1)],
                                               x[:, tile, :], ALU.mult, ALU.add).then_inc(sems["added"], 1)

        run_ahead(dve, first, second)

    def tensor_credits(pe):
        pe.sem_inc(sems["product"], PROD0)

    def scalar_credits(act):
        act.sem_inc(sems["gated" if silu else "activated"], HID0)

    def vector_credits(dve):
        dve.sem_inc(sems["lowered"], LOW0)
        dve.sem_inc(sems["added"], ADD0)
        if silu:
            dve.sem_inc(sems["multiplied"], HID0)

    return sync, gpsimd, tensor, scalar, vector, (tensor_credits, scalar_credits, vector_credits)


def attention_layer(env, scope, n):
    cfg = ATTN[n]
    nc = env["nc"]
    name, hd, keys = cfg["name"], cfg["hd"], cfg["keys"]
    inner = HEADS * hd
    NC = inner // P
    per_chunk = P // hd

    def sb(nm, shape, dt=F32):
        return scope.enter_context(nc.sbuf_tensor(f"{name}_{nm}_sb", shape, dt))

    t = dict(
        inner=inner, NC=NC, per_chunk=per_chunk,
        xT=sb("xT", [P, DC, TOKENS]),
        keysT=sb("keysT", [P, NC, NBATCH, per_chunk, keys]),
        values=sb("values", [keys, NBATCH, HEADS, hd + 1]),
    )
    if cfg["mask"] == "given":
        t["mask_mul"] = sb("mask_mul", [P, TILES, CTX])
        t["mask_add"] = sb("mask_add", [P, TILES, CTX])
    if cfg["l2norm"]:
        t["gain"] = sb("gain", [P, D])
    t["wq"], t["wo"] = sb("wq", [P, DC, inner]), sb("wo", [P, NC, D])
    t["loads"] = [(t["wq"][:], env["dram"][f"{name}_wq"]), (t["wo"][:], env["dram"][f"{name}_wo"])]
    with ExitStack() as part:
        prepare_layer(env, part, n, t)
    with ExitStack() as part:
        attend(env, part, n, t)


def prepare_layer(env, scope, n, t):
    cfg = ATTN[n]
    nc, dram, psum, x, ident = env["nc"], env["dram"], env["psum"], env["x"], env["ident"]
    ctxT, tg, mv, rstd = env["ctxT"], env["tg"], env["mv"], env["rstd"]
    name, hd, keys, inner, NC, per_chunk = cfg["name"], cfg["hd"], cfg["keys"], t["inner"], t["NC"], t["per_chunk"]
    keysT, values, xT = t["keysT"], t["values"], t["xT"]
    own = cfg["l2norm"]
    gate = tg[:, n:n + 1]
    HALF = NBATCH // 2 * CTX

    def sb(nm, shape, dt=F32):
        return scope.enter_context(nc.sbuf_tensor(f"{name}_{nm}_sb", shape, dt))

    weights = context_weights(env, n)
    wk, wv = weights["wk"], weights["wv"]
    xn = sb("xn", [P, 2, TPB, D])
    loads = []
    if own:
        once = sb("once", [P, TILES, D])
        ln_in, ln_ctx = sb("ln_in", [P, 2, DC]), sb("ln_ctx", [P, 2, DC])
        ctx = sb("ctx", [CTX, NBATCH, D])
        ctxnT = sb("ctxnT", [P, DC, NBATCH * CTX])
        cs = dict(stats=sb("cstats", [P, NBATCH, 6]), mv=sb("cmv", [P, NBATCH, 2]), var=sb("cvar", [P, NBATCH]))
        crstd = sb("crstd", [P, NBATCH])
        out_rows = sb("out_rows", [P, 2, D])
        k_scale = sb("k_scale", [P, 1])
        ktm = [sb(f"ktm{i}", [keys, HEADS, hd]) for i in range(2)]
        kn = [sb(f"kn{i}", [keys, HEADS, hd]) for i in range(2)]
        square = sb("square", [keys, HEADS, hd])
        ss = [sb(f"ss{i}", [keys, HEADS]) for i in range(2)]
        rn = [sb(f"rnk{i}", [keys, HEADS]) for i in range(2)]
        loads += [(ctx[:], dram["ctx"]), (ln_ctx[:], dram[f"{name}_ln_ctx"]), (ln_in[:], dram[f"{name}_ln_in"]),
                  (out_rows[:], dram[f"{name}_ln_out"].partition_broadcast(P)),
                  (k_scale[:], dram[f"{name}_k_scale"]),
                  (ktm[0][CTX:keys, :, :], dram[f"{name}_null"][0:1, 0]),
                  (ktm[1][CTX:keys, :, :], dram[f"{name}_null"][0:1, 0]),
                  (values[CTX:keys, :, :, 0:hd], dram[f"{name}_null_v"])]
        source = ctxnT
    else:
        bk = sb("bk", [P, NC])
        bv = sb("bv", [CTX, inner])
        bo = sb("bo", [P, D])
        loads += [(bk[:], dram[f"{name}_bk"]), (bv[:], dram[f"{name}_bv"].partition_broadcast(CTX)),
                  (bo[:], dram[f"{name}_bo"].partition_broadcast(P))]
        source = ctxT
    if hd == 16:
        kT = sb("kT", [P, NC, NBATCH * CTX])
        own_rows = sb("own_rows", [P, per_chunk])
        loads += [(own_rows[:], dram["own_rows"])]
    if cfg["rope"]:
        wkr = weights["wkr"]
        bkr = sb("bkr", [P, NC])
        kr = sb("kr", [P, NC, NBATCH * CTX])
        cos, sin = sb("cos", [P, CTX]), sb("sin", [P, CTX])
        loads += [(bkr[:], dram[f"{name}_bkr"]),
                  (cos[:], dram["cos"][:, 0:CTX]), (sin[:], dram["sin"][:, 0:CTX])]
    if cfg["mask"] == "given":
        mask8 = sb("mask8", [P, TILES, CTX], U8)
        loads += [(mask8[:], dram["mask"])]
    later = t["loads"]
    added_row = sb("added_row", [P, D])
    sems = {k: env["sem"](f"{name}k_{k}") for k in (
        "loaded", "later", "chain", "pool_chain", "k_ready", "k_out", "v_ready", "v_out", "gated_row", "shaped",
        "stats", "stats2", "cstats", "var_done", "rstd_done", "cvar_done", "crstd_done", "ctxn_done", "ctx_turned",
        "ctx_out", "squares", "squared", "inverted", "k_normed", "kn_turned", "kn_out", "applied", "x_normed",
        "x_turned", "x_out")}
    k_list = [] if own else [(w, c, half) for w in ((wk, wkr) if cfg["rope"] else (wk,))
                             for c in range(NC) for half in range(2)]
    v_list = [(b, part) for b in range(NBATCH) for part in range(max(1, inner // BANK))]
    VN = min(inner, BANK)
    v_bank = lambda j: psum[0:CTX, 4 + j % 4, 0:VN]
    k_bank = lambda j: psum[:, j % 4, 0:HALF]
    x_bank = lambda b: psum[:, b % 2, :].rearrange("p (c s) -> p c s", c=DC)
    key_banks = lambda b: slice(4 * (b % 2), 4 * (b % 2) + 2)

    with nc.Block() as block:
        @block.sync
        def _(sp):
            for dst, src in loads:
                sp.dma_start(dst, src).then_inc(sems["loaded"], 16)
            for dst, src in later:
                sp.dma_start(dst, src).then_inc(sems["later"], 16)
            sp.wait_ge(sems["later"], 16 * len(later))

        @block.gpsimd
        def _(pool):
            step = Step(pool, sems["pool_chain"])
            if own:
                pool.wait_ge(sems["cvar_done"], 1)
                nc.gpsimd.tensor_tensor(crstd[0:CTX, :], cs["var"][0:CTX, :],
                                        env["half"][0:CTX, 0:NBATCH], ALU.pow).then_inc(sems["crstd_done"], 1)
            for k in range(2 if own else 1):
                pool.wait_ge(sems["var_done"], k + 1)
                nc.gpsimd.tensor_tensor(rstd[:], env["var"][:], env["half"][:], ALU.pow).then_inc(
                    sems["rstd_done"], 1)
            if per_chunk == 2:
                step.then(nc.gpsimd.memset(keysT[0:hd, :, :, 1, :], 0.0))
                step.then(nc.gpsimd.memset(keysT[hd:P, :, :, 0, :], 0.0))
            step.then(nc.gpsimd.memset(values[:, :, :, hd:hd + 1], 1.0))
            for b in range(NBATCH if own else 0):
                pool.wait_ge(sems["squared"], b + 1)
                nc.gpsimd.tensor_tensor(rn[b % 2][:], ss[b % 2][:], env["half"][0:keys, 0:HEADS],
                                        ALU.pow).then_inc(sems["inverted"], 1)
            pool.wait_ge(sems["gated_row"], 1)
            pool.wait_ge(sems["applied" if own else "x_normed"], 1 if own else NBATCH)
            nc.gpsimd.tensor_tensor(x[:], x[:], added_row[:].unsqueeze(1).to_broadcast([P, TILES, D]),
                                    ALU.add).then_inc(sems["pool_chain"], 1)

        @block.tensor
        def _(pe):
            def turn_x():
                for b in range(NBATCH):
                    pe.wait_ge(sems["x_normed"], b + 1)
                    if b >= 2:
                        pe.wait_ge(sems["x_out"], b - 1)
                    for c in range(DC):
                        for h in range(TPB):
                            last = nc.tensor.transpose(x_bank(b)[:, c, h * P:(h + 1) * P],
                                                       xn[:, b % 2, h, c * P:(c + 1) * P], ident[:])
                    last.then_inc(sems["x_turned"], 1)

            pe.wait_ge(sems["loaded"], 16 * len(loads))
            if own:
                pe.wait_ge(sems["ctxn_done"], 1)
                for j in range(4):
                    for q in range(4):
                        b = 4 * (j % 2) + q
                        last = nc.tensor.transpose(psum[:, j, q * CTX:(q + 1) * CTX],
                                                   ctx[:, b, (j // 2) * P:(j // 2 + 1) * P], ident[0:CTX, 0:CTX])
                    last.then_inc(sems["ctx_turned"], 1)
                pe.wait_ge(sems["ctx_out"], 4)
            for j, (w, c, half) in enumerate(k_list):
                if j >= 4:
                    pe.wait_ge(sems["k_out"], j - 3)
                for k in range(DC):
                    last = nc.tensor.matmul(k_bank(j), w[:, k, c * P:(c + 1) * P],
                                            source[:, k, half * HALF:(half + 1) * HALF],
                                            start=(k == 0), stop=(k == DC - 1))
                last.then_inc(sems["k_ready"], 1)
            if not own:
                pe.wait_ge(sems["k_out"], len(k_list))
                turn_x()
            for j, (b, part) in enumerate(v_list):
                if j >= 4:
                    pe.wait_ge(sems["v_out"], j - 3)
                for k in range(DC):
                    last = nc.tensor.matmul(v_bank(j), source[:, k, b * CTX:(b + 1) * CTX],
                                            wv[:, k, part * VN:(part + 1) * VN], start=(k == 0), stop=(k == DC - 1))
                last.then_inc(sems["v_ready"], 1)
            if own:
                turn_x()
                pe.wait_ge(sems["x_out"], NBATCH)
                pe.wait_ge(sems["v_out"], len(v_list))

                def project(b):
                    if b >= 2:
                        pe.wait_ge(sems["k_out"], b - 1)
                    for part in range(2):
                        for k in range(DC):
                            last = nc.tensor.matmul(psum[0:CTX, key_banks(b).start + part, :],
                                                    source[:, k, b * CTX:(b + 1) * CTX],
                                                    wk[:, k, part * BANK:(part + 1) * BANK],
                                                    start=(k == 0), stop=(k == DC - 1))
                    last.then_inc(sems["k_ready"], 1)

                project(0)
                project(1)
                for b in range(NBATCH):
                    if b + 2 < NBATCH:
                        project(b + 2)
                    pe.wait_ge(sems["k_normed"], b + 1)
                    if b:
                        pe.wait_ge(sems["kn_out"], b)
                    for c in range(NC):
                        last = nc.tensor.transpose(psum[:, 2 + c // 4, (c % 4) * keys:(c % 4 + 1) * keys],
                                                   kn[b % 2][:, 2 * c:2 * c + 2, :].rearrange("p h d -> p (h d)"),
                                                   ident[0:keys, 0:keys])
                    last.then_inc(sems["kn_turned"], 1)

        @block.scalar
        def _(act):
            def x_out():
                for b in range(NBATCH):
                    act.wait_ge(sems["x_turned"], b + 1)
                    where = slice(b * SEQ, (b + 1) * SEQ)
                    if own:
                        for c in range(DC):
                            last = nc.scalar.activation(xT[:, c, where], x_bank(b)[:, c, :], ACT.Identity,
                                                        scale=ln_in[:, 0, c:c + 1], bias=ln_in[:, 1, c:c + 1])
                    else:
                        last = nc.scalar.activation(xT[:, :, where], x_bank(b), ACT.Copy)
                    last.then_inc(sems["x_out"], 1)

            act.wait_ge(sems["loaded"], 16 * len(loads))
            if own:
                for j in range(4):
                    act.wait_ge(sems["ctx_turned"], j + 1)
                    nc.scalar.activation(ctxnT[:, j // 2, (j % 2) * HALF:(j % 2 + 1) * HALF], psum[:, j, 0:HALF],
                                         ACT.Identity, scale=ln_ctx[:, 0, j // 2:j // 2 + 1],
                                         bias=ln_ctx[:, 1, j // 2:j // 2 + 1]).then_inc(sems["ctx_out"], 1)
            for j, (w, c, half) in enumerate(k_list):
                act.wait_ge(sems["k_ready"], j + 1)
                bias = bk if w is wk else bkr
                if hd == 16:
                    dst = kT if w is wk else kr
                    nc.scalar.activation(dst[:, c, half * HALF:(half + 1) * HALF], k_bank(j), ACT.Identity,
                                         bias=bias[:, c:c + 1]).then_inc(sems["k_out"], 1)
                else:
                    for s in range(2):
                        rows = slice(s * hd, (s + 1) * hd)
                        last = nc.scalar.activation(
                            keysT[rows, c, half * 4:half * 4 + 4, s, :],
                            psum[rows, j % 4, 0:HALF].rearrange("p (b k) -> p b k", k=CTX), ACT.Identity,
                            bias=bias[rows, c:c + 1])
                    last.then_inc(sems["k_out"], 1)
            if not own:
                x_out()
            else:
                for j, (b, part) in enumerate(v_list):
                    act.wait_ge(sems["v_ready"], j + 1)
                    heads = slice(part * (VN // hd), (part + 1) * (VN // hd))
                    nc.scalar.activation(values[0:CTX, b, heads, 0:hd],
                                         v_bank(j).rearrange("p (h d) -> p h d", d=hd), ACT.Copy).then_inc(
                                             sems["v_out"], 1)
                x_out()

                def take(b):
                    act.wait_ge(sems["k_ready"], b + 1)
                    if b >= 2:
                        act.wait_ge(sems["k_normed"], b - 1)
                    nc.scalar.activation(ktm[b % 2][0:CTX, :, :].rearrange("p h d -> p (h d)").rearrange(
                        "p (a c) -> p a c", a=2), psum[0:CTX, key_banks(b), :], ACT.Copy).then_inc(sems["k_out"], 1)
                    act.wait_ge(sems["k_out"], b + 1)
                    if b:
                        act.wait_ge(sems["squared"], b)
                    nc.scalar.activation(square[:], ktm[b % 2][:], ACT.Square).then_inc(sems["squares"], 1)

                def spread(b):
                    act.wait_ge(sems["kn_turned"], b + 1)
                    if b == 0:
                        act.wait_ge(sems["pool_chain"], 2)
                    for part in range(2):
                        for s in range(2):
                            rows = slice(s * hd, (s + 1) * hd)
                            last = nc.scalar.activation(
                                keysT[rows, part * 4:part * 4 + 4, b, s, :],
                                psum[rows, 2 + part, 0:4 * keys].rearrange("p (c k) -> p c k", k=keys),
                                ACT.Copy, scale=k_scale[rows, :])
                    last.then_inc(sems["kn_out"], 1)

                take(0)
                for b in range(NBATCH):
                    if b + 1 < NBATCH:
                        take(b + 1)
                    spread(b)

        @block.vector
        def _(dve):
            step = Step(dve, sems["chain"])
            if own:
                dve.wait_ge(sems["loaded"], 16 * len(loads))
                emit_statistics(nc, dve, ctx, cs, sems["cstats"], sems["cvar_done"], CTX, NBATCH)
                step.then(nc.vector.tensor_scalar(added_row[:], out_rows[:, 1, :], gate, None, ALU.mult))
                nc.vector.tensor_scalar(t["gain"][:], out_rows[:, 0, :], gate, None, ALU.mult).then_inc(
                    sems["gated_row"], 1)
                dve.wait_ge(sems["crstd_done"], 1)
                for b in range(NBATCH):
                    last = nc.vector.tensor_scalar(ctx[:, b, :], ctx[:, b, :], cs["mv"][0:CTX, b, 0:1],
                                                   crstd[0:CTX, b:b + 1], ALU.subtract, ALU.mult)
                last.then_inc(sems["ctxn_done"], 1)
            emit_statistics(nc, dve, x, env, sems["stats"], sems["var_done"])
            dve.wait_ge(sems["rstd_done"], 1)
            if own:
                for tile in range(TILES):
                    last = nc.vector.tensor_scalar(once[:, tile, :], x[:, tile, :], mv[:, tile, 0:1],
                                                   rstd[:, tile:tile + 1], ALU.subtract, ALU.mult)
                last.then_inc(sems["applied"], 1)
                dve.wait_ge(sems["applied"], 1)
                emit_statistics(nc, dve, once, env, sems["stats2"], sems["var_done"])
                dve.wait_ge(sems["rstd_done"], 2)
            for b in range(NBATCH):
                if b >= 2:
                    dve.wait_ge(sems["x_turned"], b - 1)
                for h in range(TPB):
                    tile = b * TPB + h
                    last = nc.vector.tensor_scalar(xn[:, b % 2, h, :], (once if own else x)[:, tile, :],
                                                   mv[:, tile, 0:1], rstd[:, tile:tile + 1], ALU.subtract, ALU.mult)
                last.then_inc(sems["x_normed"], 1)
            if not own:
                dve.wait_ge(sems["loaded"], 16 * len(loads))
                nc.vector.tensor_scalar(added_row[:], bo[:], gate, None, ALU.mult).then_inc(sems["gated_row"], 1)
            if cfg["mask"] == "given":
                step.then(nc.vector.tensor_copy(t["mask_mul"][:], mask8[:]))
                step.did(nc.vector.tensor_scalar(t["mask_add"][:], t["mask_mul"][:], -1.0, -L2_FILL / cfg["scale"],
                                                 ALU.add, ALU.mult))
            if hd == 16:
                dve.wait_ge(sems["k_out"], len(k_list))
                if cfg["rope"]:
                    wide = [P, NC * NBATCH, CTX]
                    for v, table in ((kT, cos), (kr, sin)):
                        v3 = v[:].rearrange("p c (b k) -> p (c b) k", k=CTX)
                        step.then(nc.vector.tensor_tensor(v3, v3, table[:].unsqueeze(1).to_broadcast(wide), ALU.mult))
                    step.then(nc.vector.tensor_tensor(kT[:], kT[:], kr[:], ALU.add))
                for c in range(NC):
                    for h in range(per_chunk):
                        last = nc.vector.tensor_scalar(keysT[:, c, :, h, :],
                                                       kT[:, c, :].rearrange("p (b k) -> p b k", k=CTX),
                                                       own_rows[:, h:h + 1], None, ALU.mult)
                last.then_inc(sems["shaped"], 1)
            if not own:
                for j, (b, part) in enumerate(v_list):
                    dve.wait_ge(sems["v_ready"], j + 1)
                    heads = slice(part * (VN // hd), (part + 1) * (VN // hd))
                    nc.vector.tensor_tensor(values[0:CTX, b, heads, 0:hd],
                                            v_bank(j).rearrange("p (h d) -> p h d", d=hd),
                                            bv[:, part * VN:(part + 1) * VN].rearrange("p (h d) -> p h d", d=hd),
                                            ALU.add).then_inc(sems["v_out"], 1)
            else:
                def sum_squares(b):
                    dve.wait_ge(sems["squares"], b + 1)
                    step.then(nc.vector.tensor_reduce(ss[b % 2][:], square[:], AX.X, ALU.add))
                    nc.vector.tensor_scalar(ss[b % 2][:], ss[b % 2][:], 1e-24, None, ALU.max).then_inc(
                        sems["squared"], 1)

                sum_squares(0)
                for b in range(NBATCH):
                    if b + 1 < NBATCH:
                        sum_squares(b + 1)
                    dve.wait_ge(sems["inverted"], b + 1)
                    if b >= 2:
                        dve.wait_ge(sems["kn_turned"], b - 1)
                    nc.vector.tensor_tensor(kn[b % 2][:], ktm[b % 2][:],
                                            rn[b % 2][:].unsqueeze(2).to_broadcast([keys, HEADS, hd]),
                                            ALU.mult).then_inc(sems["k_normed"], 1)


def attend(env, scope, n, t):
    cfg = ATTN[n]
    nc, dram, psum, x, ident, tg = env["nc"], env["dram"], env["psum"], env["x"], env["ident"], env["tg"]
    name, hd, keys, inner, NC = cfg["name"], cfg["hd"], cfg["keys"], t["inner"], t["NC"]
    xT, keysT, values = t["xT"], t["keysT"], t["values"]
    rope, own, mask = cfg["rope"], cfg["l2norm"], cfg["mask"]
    gate = tg[:, n:n + 1]
    STEPS = TPB * GROUPS
    wide = [P, GROUP, keys]

    def sb(nm, shape, dt=F32):
        return scope.enter_context(nc.sbuf_tensor(f"{name}_{nm}_sb", shape, dt))

    wq, wo = t["wq"], t["wo"]
    qT = sb("qT", [P, NC, SEQ])
    shifted = [sb(f"shifted{i}", wide) for i in range(2)]
    probs = [sb(f"probs{i}", wide) for i in range(2)]
    probsT = [sb(f"probsT{i}", [keys, GROUP * P]) for i in range(2)]
    top = [sb(f"top{i}", [P, GROUP]) for i in range(2)]
    inv = [sb(f"inv{i}", [P, GROUP]) for i in range(2)]
    att = [sb(f"att{i}", [P, HEADS, hd]) for i in range(TPB)]
    attT = [sb(f"attT{i}", [P, NC, P]) for i in range(TPB)]
    loads = []
    if own:
        q_scale = sb("q_scale", [P, 1])
        of_head = sb("of_head", [P, 2])
        q2 = sb("q2", [P, NC, SEQ])
        qss, qrn = sb("qss", [P, TPB, HEADS]), sb("qrn", [P, TPB, HEADS])
        y_all = env["context_w"][:].rearrange("p (t d) -> p t d", d=D)
        loads += [(q_scale[:], dram[f"{name}_q_scale"]), (of_head[:], dram["of_head"])]
    else:
        bq = sb("bq", [P, NC])
        loads += [(bq[:], dram[f"{name}_bq"])]
    if rope:
        wqr, bqr = sb("wqr", [P, DC, inner]), sb("bqr", [P, NC])
        q_raw, qr = sb("q_raw", [P, NC, SEQ]), sb("qr", [P, NC, SEQ])
        cos, sin = sb("cosq", [P, SEQ]), sb("sinq", [P, SEQ])
        loads += [(wqr[:], dram[f"{name}_wqr"]), (bqr[:], dram[f"{name}_bqr"]), (cos[:], dram["cos"]),
                  (sin[:], dram["sin"])]
    if mask == "window":
        window, seen = sb("window", [P, TPB, CTX]), sb("seen", [P, TPB])
        loads += [(window[:], dram["window"]), (seen[:], dram["seen"])]
    sems = {k: env["sem"](f"{name}l_{k}") for k in (
        "loaded", "q_ready", "q_out", "q_done", "sq_ready", "sq_out", "q_inverted", "scored", "s_free",
        "shift", "probs", "turned", "pt_out", "summed", "normed", "att_turned", "y_ready", "left", "chain",
        "stats", "var_done", "rstd_done", "applied", "gained")}

    SCORES, EXPS, TURN, SUMS = 6, 5, 4, 3
    NQ = (2 if rope else 1) * max(1, NC // 2)
    AT = max(1, NC // 4)
    QPS = 2
    Q_SLOTS = [range(q, min(q + QPS, NQ)) for q in range(0, NQ, QPS)]
    SQ_SLOT = len(Q_SLOTS)
    TURN_SLOT, OUT_SLOT = (2, 6), (3, 7)

    uses = [("q_out", j + 1) for j in range(NQ)] + ([("sq_out", 1)] if own else [])
    LEFT = TPB * (AT + 1)
    CREDIT = 1
    first_left = len(uses)
    uses += [("left", j + 1) for j in range(LEFT)]
    spare = lambda use: psum[:, 6 + use % 2, :]

    def count(b, o, per, k):
        if isinstance(b, int):
            return max((b + o) * per + k, 0)
        assert o * per + k >= 0
        return b * per + (o * per + k)

    def at_spare(pe, b, o, use, last):
        kind = uses[use - 2][0] if use >= 2 else None
        if kind == "left" and uses[use][0] == "left":
            pe.wait_ge(sems["left"], count(b, o, LEFT, uses[use - 2][1] + CREDIT))
        elif use < 2 or (last and uses[use][0] == "left"):
            pe.wait_ge(sems["left"], count(b, 0, LEFT, CREDIT))
            pe.wait_ge(sems["q_out"], count(b, 0, NQ, NQ if o or last else 0))
            if own:
                pe.wait_ge(sems["sq_out"], count(b, 0, 1, 1 if o or last else 0))
        else:
            per = NQ if kind == "q_out" else 1
            ahead = 1 if uses[use][0] == "left" else o
            pe.wait_ge(sems[kind], count(b, ahead, per, uses[use - 2][1]))
        return spare(use)

    def stream(engine, prepare, slot, step=None):
        prepare(0, 0)
        for s in range(-SCORES, 0):
            slot(0, s, False)
        if step:
            step.filled()
        with engine.Fori(0, NBATCH - 1) as bi:
            if step:
                step.round(bi)
            for s in range(STEPS):
                slot(bi, s, False)
            if step:
                step.check()
        if step:
            step.round(NBATCH - 1)
        for s in range(STEPS):
            slot(NBATCH - 1, s, True)

    def item(fn, b, s, lead, last):
        g = s + lead
        if 0 <= g < STEPS:
            fn(b, 0, g)
        elif g >= STEPS and not last:
            fn(b, 1, g - STEPS)

    with nc.Block() as block:
        @block.sync
        def _(sp):
            for dst, src in loads:
                sp.dma_start(dst, src).then_inc(sems["loaded"], 16)

        @block.tensor
        def _(pe):
            def queries(b, o, j):
                w = wqr if rope and j >= NQ // 2 else wq
                bank = at_spare(pe, b, o, j, False)
                for s in range(2):
                    c = (2 * j + s) % NC
                    for k in range(DC):
                        last = nc.tensor.matmul(bank[:, s * SEQ:(s + 1) * SEQ], w[:, k, c * P:(c + 1) * P],
                                                xT[:, k, bass.ds((b + o) * SEQ, SEQ)],
                                                start=(k == 0), stop=(k == DC - 1))
                last.then_inc(sems["q_ready"], 1)

            def query_squares(b, o):
                pe.wait_ge(sems["q_out"], count(b, o, NQ, NQ))
                bank = at_spare(pe, b, o, NQ, False)
                for tile in range(TPB):
                    for c in range(NC):
                        col = tile * HEADS + 2 * c
                        last = nc.tensor.matmul(bank[:, col:col + 2], q2[:, c, tile * P:(tile + 1) * P],
                                                of_head[:], start=True, stop=True)
                last.then_inc(sems["sq_ready"], 1)

            def scores(b, o, g):
                tile, quad = divmod(g, GROUPS)
                if g < GROUPS:
                    if rope:
                        pe.wait_ge(sems["q_done"], count(b, o, 2, quad // 2 + 1))
                    else:
                        pe.wait_ge(sems["q_out"], count(b, o, NQ, min(quad + 1, NQ)))
                pe.wait_ge(sems["s_free" if own or mask else "shift"], count(b, o, STEPS, g - 1))
                rows = slice(tile * P, (tile + 1) * P)
                if hd == 16:
                    first = (quad % 2) * GROUP
                    last = nc.tensor.matmul(psum[:, g % 2, 0:GROUP * keys], qT[:, quad // 2, rows],
                                            keysT[:, quad // 2, b + o, first:first + GROUP, :], start=True, stop=True)
                else:
                    for s in range(2):
                        c = 2 * quad + s
                        last = nc.tensor.matmul(psum[:, g % 2, s * 2 * keys:(s + 1) * 2 * keys], qT[:, c, rows],
                                                keysT[:, c, b + o, :, :], start=True, stop=True)
                last.then_inc(sems["scored"], 1)

            def turn(b, o, g):
                pe.wait_ge(sems["probs"], count(b, o, STEPS, g + 1))
                pe.wait_ge(sems["pt_out"], count(b, o, STEPS, g - 1))
                for h in range(GROUP):
                    last = nc.tensor.transpose(psum[0:keys, 2 + g % 2, h * P:(h + 1) * P],
                                               probs[g % 2][:, h, :], ident[:])
                last.then_inc(sems["turned"], 1)

            def sums(b, o, g):
                quad = g % GROUPS
                pe.wait_ge(sems["pt_out"], count(b, o, STEPS, g + 1))
                pe.wait_ge(sems["normed"], count(b, o, STEPS, g - 1))
                for h in range(GROUP):
                    last = nc.tensor.matmul(psum[:, 4 + g % 2, h * (hd + 1):(h + 1) * (hd + 1)],
                                            probsT[g % 2][:, h * P:(h + 1) * P],
                                            values[:, b + o, quad * GROUP + h, :], start=True, stop=True)
                last.then_inc(sems["summed"], 1)

            def turn_sums(b, tile, end):
                pe.wait_ge(sems["normed"], count(b, 0, STEPS, (tile + 1) * GROUPS))
                for j in range(AT):
                    bank = at_spare(pe, b, 0, first_left + tile * (AT + 1) + j, end)
                    per = NC // AT
                    for q in range(per):
                        c = j * per + q
                        last = nc.tensor.transpose(
                            bank[:, q * P:(q + 1) * P],
                            att[tile][:].rearrange("p h d -> p (h d)")[:, c * P:(c + 1) * P], ident[:])
                    last.then_inc(sems["att_turned"], 1)

            def output(b, tile, end):
                pe.wait_ge(sems["left"], count(b, 0, LEFT, tile * (AT + 1) + AT + CREDIT))
                bank = at_spare(pe, b, 0, first_left + tile * (AT + 1) + AT, end)
                for c in range(NC):
                    last = nc.tensor.matmul(bank[:, 0:D], attT[tile][:, c, :], wo[:, c, :],
                                            start=(c == 0), stop=(c == NC - 1))
                last.then_inc(sems["y_ready"], 1)

            def prepare(b, o):
                for j in range(NQ):
                    queries(b, o, j)
                if own:
                    query_squares(b, o)

            def slot(b, s, end):
                item(scores, b, s, SCORES, end)
                if 0 <= s < len(Q_SLOTS) and not end:
                    for j in Q_SLOTS[s]:
                        queries(b, 1, j)
                if own and s == SQ_SLOT and not end:
                    query_squares(b, 1)
                item(turn, b, s, TURN, end)
                item(sums, b, s, SUMS, end)
                for tile in range(TPB):
                    if s == TURN_SLOT[tile]:
                        turn_sums(b, tile, end)
                    if s == OUT_SLOT[tile]:
                        output(b, tile, end)

            pe.sem_inc(sems["att_turned"], CREDIT)
            pe.wait_ge(sems["loaded"], 16 * len(loads))
            stream(pe, prepare, slot)

        @block.scalar
        def _(act):
            def queries_out(b, o, j):
                act.wait_ge(sems["q_ready"], count(b, o, NQ, j + 1))
                if own:
                    act.wait_ge(sems["scored"], count(b, o, STEPS, j + 1 - GROUPS))
                    both = spare(j).rearrange("p (c s) -> p c s", c=2)
                    nc.scalar.activation(q2[:, 2 * j:2 * j + 2, :], both, ACT.Square)
                    nc.scalar.activation(qT[:, 2 * j:2 * j + 2, :], both, ACT.Copy,
                                         scale=q_scale[:]).then_inc(sems["q_out"], 1)
                    return
                if rope:
                    act.wait_ge(sems["q_done"], count(b, o, 2, 0))
                for s in range(2):
                    c = (2 * j + s) % NC
                    if not rope:
                        read = GROUPS // NC * (s + 1) if hd == 16 else j + 1
                        act.wait_ge(sems["scored"], count(b, o, STEPS, read - GROUPS))
                    turned = rope and j >= NQ // 2
                    dst = (qr if turned else q_raw) if rope else qT
                    last = nc.scalar.activation(dst[:, c, :], spare(j)[:, s * SEQ:(s + 1) * SEQ], ACT.Identity,
                                                bias=(bqr if turned else bq)[:, c:c + 1])
                last.then_inc(sems["q_out"], 1)

            def exps(b, o, g):
                act.wait_ge(sems["shift"], count(b, o, STEPS, g + 1))
                act.wait_ge(sems["turned"], count(b, o, STEPS, g - 1))
                nc.scalar.activation(probs[g % 2][:], shifted[g % 2][:], ACT.Exp,
                                     scale=cfg["scale"]).then_inc(sems["probs"], 1)

            def turned_out(b, o, g):
                act.wait_ge(sems["turned"], count(b, o, STEPS, g + 1))
                act.wait_ge(sems["summed"], count(b, o, STEPS, g - 1))
                nc.scalar.activation(probsT[g % 2][:], psum[0:keys, 2 + g % 2, :], ACT.Copy).then_inc(
                    sems["pt_out"], 1)

            def prepare(b, o):
                for j in range(NQ):
                    queries_out(b, o, j)

            def slot(b, s, end):
                item(exps, b, s, EXPS, end)
                if 0 <= s < len(Q_SLOTS) and not end:
                    for j in Q_SLOTS[s]:
                        queries_out(b, 1, j)
                item(turned_out, b, s, TURN, end)

            act.wait_ge(sems["loaded"], 16 * len(loads))
            stream(act, prepare, slot)

        if own:
            @block.gpsimd
            def _(pool):
                with pool.Fori(0, NBATCH) as bi:
                    pool.wait_ge(sems["sq_out"], bi + 1)
                    nc.gpsimd.tensor_tensor(qrn[:].rearrange("p t h -> p (t h)"), qss[:].rearrange("p t h -> p (t h)"),
                                            env["half32"][:], ALU.pow).then_inc(sems["q_inverted"], 1)
                pool.wait_ge(sems["var_done"], 1)
                nc.gpsimd.tensor_tensor(env["rstd"][:], env["var"][:], env["half"][:], ALU.pow).then_inc(
                    sems["rstd_done"], 1)

        @block.vector
        def _(dve):
            dve.sem_inc(sems["left"], CREDIT)
            step = Step(dve, sems["chain"], per=STEPS * (3 if mask else 2) + (2 if rope else 0))
            dve.wait_ge(sems["loaded"], 16 * len(loads))

            def soft(b, o, g):
                tile, quad = divmod(g, GROUPS)
                s3 = psum[:, g % 2, 0:GROUP * keys].rearrange("p (h k) -> p h k", k=keys)
                dst, mx = shifted[g % 2], top[g % 2]
                if own and g == 0:
                    dve.wait_ge(sems["q_inverted"], count(b, o, 1, 1))
                dve.wait_ge(sems["scored"], count(b, o, STEPS, g + 1))
                dve.wait_ge(sems["probs"], count(b, o, STEPS, g - 1))
                source = dst[:]
                if own:
                    ins = nc.vector.tensor_tensor(
                        dst[:], s3, qrn[:, tile, quad * GROUP:(quad + 1) * GROUP].unsqueeze(2).to_broadcast(wide),
                        ALU.mult)
                elif mask == "given":
                    row = t["mask_mul"][:, bass.ds((b + o) * TPB + tile, 1), :].to_broadcast(wide)
                    ins = nc.vector.tensor_tensor(dst[:], s3, row, ALU.mult)
                elif mask == "window":
                    ins = nc.vector.tensor_tensor(dst[:], s3, window[:, tile, :].unsqueeze(1).to_broadcast(wide),
                                                  ALU.add)
                else:
                    ins, source = None, s3
                if ins is not None:
                    ins.then_inc(sems["s_free"], 1)
                    dve.wait_ge(sems["s_free"], count(b, o, STEPS, g + 1))
                if mask == "given":
                    row = t["mask_add"][:, bass.ds((b + o) * TPB + tile, 1), :].to_broadcast(wide)
                    step.then(nc.vector.tensor_tensor(dst[:], dst[:], row, ALU.add))
                step.then(nc.vector.tensor_reduce(mx[:], source, AX.X, ALU.max))
                nc.vector.tensor_tensor(dst[:], source, mx[:].unsqueeze(2).to_broadcast(wide),
                                        ALU.subtract).then_inc(sems["shift"], 1)

            def norm(b, o, g):
                tile, quad = divmod(g, GROUPS)
                dve.wait_ge(sems["summed"], count(b, o, STEPS, g + 1))
                if quad == 0:
                    dve.wait_ge(sems["att_turned"], count(b, o, TPB * AT, (tile + 1 - TPB) * AT + CREDIT))
                o3 = psum[:, 4 + g % 2, 0:GROUP * (hd + 1)].rearrange("p (h d) -> p h d", d=hd + 1)
                step.then(nc.vector.reciprocal(inv[g % 2][:], o3[:, :, hd]))
                if mask == "window":
                    step.then(nc.vector.tensor_scalar(inv[g % 2][:], inv[g % 2][:], seen[:, tile:tile + 1], None,
                                                      ALU.mult))
                nc.vector.tensor_tensor(att[tile][:, quad * GROUP:(quad + 1) * GROUP, :], o3[:, :, 0:hd],
                                        inv[g % 2][:].unsqueeze(2).to_broadcast([P, GROUP, hd]),
                                        ALU.mult).then_inc(sems["normed"], 1)

            def copy_turned(b, tile):
                per = NC // AT
                for j in range(AT):
                    dve.wait_ge(sems["att_turned"], count(b, 0, TPB * AT, tile * AT + j + 1 + CREDIT))
                    nc.vector.tensor_copy(attT[tile][:, j * per:(j + 1) * per, :],
                                          spare(first_left + tile * (AT + 1) + j)[:, 0:per * P].rearrange(
                                              "p (c s) -> p c s", s=P)).then_inc(sems["left"], 1)

            def add_output(b, tile):
                dve.wait_ge(sems["y_ready"], count(b, 0, TPB, tile + 1))
                y = spare(first_left + tile * (AT + 1) + AT)[:, 0:D]
                where = bass.ds(b * TPB + tile, 1)
                if own:
                    nc.vector.tensor_scalar(y_all[:, where, :], y.unsqueeze(1), 1.0, None, ALU.mult).then_inc(
                        sems["left"], 1)
                else:
                    nc.vector.scalar_tensor_tensor(x[:, where, :], y.unsqueeze(1), gate, x[:, where, :],
                                                   ALU.mult, ALU.add).then_inc(sems["left"], 1)

            def turn_positions(b, o):
                table = lambda v: v[:].unsqueeze(1).to_broadcast([P, NC, SEQ])
                dve.wait_ge(sems["q_out"], count(b, o, NQ, NQ))
                step.did(nc.vector.tensor_tensor(q_raw[:], q_raw[:], table(cos), ALU.mult))
                step.then(nc.vector.tensor_tensor(qr[:], qr[:], table(sin), ALU.mult))
                for c in range(NC):
                    dve.wait_ge(sems["scored"], count(b, o, STEPS, GROUPS // NC * (c + 1) - GROUPS))
                    nc.vector.tensor_tensor(qT[:, c, :], q_raw[:, c, :], qr[:, c, :], ALU.add).then_inc(
                        sems["q_done"], 1)

            def sum_squares(b, o):
                dve.wait_ge(sems["sq_ready"], count(b, o, 1, 1))
                nc.vector.tensor_scalar(qss[:].rearrange("p t h -> p (t h)"), spare(NQ)[:, 0:TPB * HEADS], 1e-24,
                                        None, ALU.max).then_inc(sems["sq_out"], 1)

            def prepare(b, o):
                if rope:
                    turn_positions(b, o)
                if own:
                    sum_squares(b, o)

            def slot(b, s, end):
                if own and s == SQ_SLOT and not end:
                    sum_squares(b, 1)
                item(soft, b, s, SCORES, end)
                if rope and s == 0 and not end:
                    turn_positions(b, 1)
                item(norm, b, s, SUMS, end)
                for tile in range(TPB):
                    if s == TURN_SLOT[tile]:
                        copy_turned(b, tile)
                    if s == OUT_SLOT[tile]:
                        add_output(b, tile)

            stream(dve, prepare, slot, step)
            if own:
                dve.wait_ge(sems["left"], NBATCH * LEFT + CREDIT)
                emit_statistics(nc, dve, y_all, env, sems["stats"], sems["var_done"])
                dve.wait_ge(sems["rstd_done"], 1)
                for tile in range(TILES):
                    nc.vector.tensor_scalar(y_all[:, tile, :], y_all[:, tile, :], env["mv"][:, tile, 0:1],
                                            env["rstd"][:, tile:tile + 1], ALU.subtract, ALU.mult).then_inc(
                                                sems["applied"], 1)
                dve.wait_ge(sems["applied"], TILES)
                nc.vector.tensor_tensor(y_all[:], y_all[:], t["gain"][:].unsqueeze(1).to_broadcast([P, TILES, D]),
                                        ALU.mult).then_inc(sems["gained"], 1)
                dve.wait_ge(sems["gained"], 1)
                nc.vector.tensor_tensor(x[:], x[:], y_all[:], ALU.add).then_inc(sems["gained"], 1)


def _chunks(w):
    r, c = w.shape
    return np.ascontiguousarray(w.reshape(r // P, P, c).transpose(1, 0, 2))


def _units(w1, w2, b1=None):
    out = [np.stack([_chunks(w) for w in w1]), np.stack([_chunks(w) for w in w2])]
    if b1 is not None:
        out.append(np.ascontiguousarray(np.stack([b.reshape(UNIT // P, P).T for b in b1], axis=1)))
    return out


def layout(inputs):
    a = {k: np.asarray(v) for k, v in inputs.items()}
    out = {"x": a["x"], "g_xattn": a["g_xattn"], "g_ffn": a["g_ffn"]}
    ctx = a["ctx_1024"]
    out["ctxT"] = _chunks(np.ascontiguousarray(ctx.reshape(-1, D).T))
    out["ctx"] = np.ascontiguousarray(ctx.transpose(1, 0, 2))
    out["mask"] = np.ascontiguousarray(
        a["mask_BxSxS2_bf1"].view(np.uint8).reshape(TILES, P, CTX).transpose(1, 0, 2))
    out["ident"] = np.eye(P, dtype=np.float32)
    out["rank"] = np.ascontiguousarray(np.broadcast_to((8 - np.arange(8)).astype(np.float32), (P, TILES, 8)))
    w1 = [*a["L0_ffn_rw1"], a["L0_ffn_sw1"]]
    w2 = [*a["L0_ffn_rw2"], a["L0_ffn_sw2"]]
    out["f0_w1"], out["f0_w2"], out["f0_b1"] = _units(w1, w2, [*a["L0_ffn_rb1"], a["L0_ffn_sb1"]])
    out["f0_b2"] = np.concatenate([a["L0_ffn_rb2"], a["L0_ffn_sb2"][None]])
    out["f0_wr"], out["f0_rb"] = _chunks(a["L0_ffn_router_w"]), a["L0_ffn_router_b"]
    halves = [slice(0, UNIT), slice(UNIT, 2 * UNIT)]
    out["f1_w1"], out["f1_w2"], out["f1_b1"] = _units(
        [w[:, h] for w in a["L1_ffn_W1"] for h in halves], [w[h] for w in a["L1_ffn_W2"] for h in halves],
        [b[h] for b in a["L1_ffn_b1"] for h in halves])
    out["f1_b2"], out["f1_wr"], out["f1_rb"] = a["L1_ffn_b2"], _chunks(a["L1_ffn_Wr"]), a["L1_ffn_br"]
    wi, wo = a["L2_ffn_wi_W"].T, a["L2_ffn_wo_W"].T
    out["f2_w1"], out["f2_w2"], out["f2_b1"] = _units(
        [wi[:, h] for h in halves], [wo[h] for h in halves], [a["L2_ffn_wi_b"][h] for h in halves])
    out["f2_b2"], out["f2_rb"] = a["L2_ffn_wo_b"][None], a["L2_ffn_gate_b"]
    out["f2_wr"] = _chunks(np.concatenate([a["L2_ffn_gate_W"], a["L2_ffn_lora_A"].reshape(-1, D)]).T)
    lb = a["L2_ffn_lora_B"].transpose(0, 2, 1).reshape(32, 2, UNIT)
    out["f2_lb"] = np.ascontiguousarray(lb)
    w1 = [np.concatenate([p, q]).T for p, q in zip(a["L3_ffn_w1"], a["L3_ffn_w3"])]
    w2 = [w.T for w in a["L3_ffn_w2"]]
    for h in (slice(0, D), slice(D, 2 * D)):
        w1.append(np.concatenate([a["L3_ffn_sw1"][h], a["L3_ffn_sw3"][h]]).T)
        w2.append(a["L3_ffn_sw2"][:, h].T)
    out["f3_w1"], out["f3_w2"] = _units(w1, w2)
    out["f3_wr"], out["f3_rb"] = _chunks(a["L3_ffn_gate_w"].T), a["L3_ffn_gate_bias"]
    for n in range(4):
        c, pre = ATTN[n], f"L{n}_xattn_"
        w = {k: a[pre + k] for k in ("Wq", "Wk", "Wv", "Wo") if pre + k in a}
        if n == 1:
            w["Wk"], w["Wv"] = a[pre + "Wkv"][:, :HEADS * c["hd"]], a[pre + "Wkv"][:, HEADS * c["hd"]:]
        if n in (0, 3):
            w = {k: v.T for k, v in w.items()}
        for k, v in w.items():
            out[f"a{n}_w{k[1]}"] = _chunks(v)
        if n != 1:
            for k in ("bq", "bk"):
                out[f"a{n}_{k}"] = np.ascontiguousarray(a[pre + k].reshape(-1, P).T)
            out[f"a{n}_bv"], out[f"a{n}_bo"] = a[pre + "bv"], a[pre + "bo"]
    per_feature = lambda g, b: np.ascontiguousarray(np.stack([g, b]).reshape(2, DC, P).transpose(2, 0, 1))
    out["a1_ln_in"] = per_feature(a["L1_xattn_ln_in_g"], a["L1_xattn_ln_in_b"])
    out["a1_ln_ctx"] = per_feature(a["L1_xattn_ln_ctx_g"], a["L1_xattn_ln_ctx_b"])
    out["a1_ln_out"] = np.stack([a["L1_xattn_ln_out_g"], a["L1_xattn_ln_out_b"]])
    out["a1_k_scale"] = np.ascontiguousarray(np.tile(a["L1_xattn_k_scale"], 2)[:, None])
    out["a1_q_scale"] = np.ascontiguousarray(np.tile(a["L1_xattn_q_scale"], 2)[:, None])
    null = a["L1_xattn_null_kv"]
    out["a1_null"] = np.ascontiguousarray(np.broadcast_to(null[0], (1, 1, HEADS, 64)))
    out["a1_null_v"] = np.ascontiguousarray(np.broadcast_to(null[1], (1, NBATCH, HEADS, 64)))
    partner = (np.arange(D) // 16) * 16 + (np.arange(D) + 8) % 16
    for k in "qk":
        out[f"a3_w{k}r"] = _chunks(a[f"L3_xattn_W{k}"][partner].T)
        out[f"a3_b{k}r"] = np.ascontiguousarray(a[f"L3_xattn_b{k}"][partner].reshape(-1, P).T)
    f = np.arange(P)
    out["own_rows"] = (f[:, None] // 16 == np.arange(8)[None]).astype(np.float32)
    out["of_head"] = (f[:, None] // 64 == np.arange(2)[None]).astype(np.float32)
    freq = (1.0 / np.float32(10000.0) ** (np.arange(8, dtype=np.float32) / np.float32(8))).astype(np.float32)
    angle = np.arange(SEQ, dtype=np.float32)[None, :] * freq[f % 8][:, None]
    out["cos"] = np.cos(angle).astype(np.float32)
    out["sin"] = (np.sin(angle) * np.where(f % 16 < 8, -1.0, 1.0)[:, None]).astype(np.float32)
    tok, key = np.arange(SEQ).reshape(TPB, P).T[:, :, None], np.arange(CTX)[None, None]
    hidden = (key > tok) | (key < tok - 128)
    out["window"] = np.where(hidden, np.float32(MASKED), np.float32(0))
    out["seen"] = (~hidden.all(-1)).astype(np.float32)
    return {k: np.ascontiguousarray(v) for k, v in out.items()}


STAGES = [("a", 0), ("f", 0), ("a", 1), ("f", 1), ("a", 2), ("f", 2), ("a", 3), ("f", 3)]


def kernel(**inputs):
    import concourse.bacc as bacc
    from concourse.bass_utils import run_bass_kernel_spmd

    nc = bacc.Bacc("TRN2", target_bir_lowering=False, num_devices=1)
    arrays, dram = {}, {}
    for name, v in layout(inputs).items():
        arrays[f"in_{name}"] = v
        dram[name] = nc.dram_tensor(f"in_{name}", v.shape, mybir.dt.from_np(v.dtype), kind="ExternalInput").ap()
    out = nc.dram_tensor("out", (NBATCH, SEQ, D), F32, kind="ExternalOutput").ap()
    build(nc, dram, out, STAGES)
    return run_bass_kernel_spmd(nc, [arrays], core_ids=[0]).results[0]["out"]
```

```python
from contextlib import ExitStack

import concourse.bass as bass
import numpy as np
from concourse import mybir

F32 = mybir.dt.float32
F32R = mybir.dt.float32r
U8 = mybir.dt.uint8
I32 = mybir.dt.int32
ACT = mybir.ActivationFunctionType
ALU = mybir.AluOpType
AX = mybir.AxisListType

P = 128
NBATCH = 8
SEQ = 256
D = 256
DC = D // P
TOKENS = NBATCH * SEQ
TILES = TOKENS // P
TPB = SEQ // P
CTX = 77
HEADS = 16
GROUP = 4
GROUPS = HEADS // GROUP
EPS = 1e-5
BANK = 512
UNIT = 512
CHUNK = 512
CHUNKS = TOKENS // CHUNK
BLOCK = 256
BLOCKS = (2 * TOKENS + 8 * (BLOCK - 1)) // BLOCK
HUGE = 3.0e38
MASKED = -1.0e30
L2_FILL = -1.0e9

ATTN = [
    dict(name="a0", hd=16, keys=CTX, scale=0.25, rope=False, l2norm=False, mask=None),
    dict(name="a1", hd=64, keys=CTX + 1, scale=8.0, rope=False, l2norm=True, mask=None),
    dict(name="a2", hd=64, keys=CTX, scale=0.125, rope=False, l2norm=False, mask="given"),
    dict(name="a3", hd=16, keys=CTX, scale=0.25, rope=True, l2norm=False, mask="window"),
]
FFN = [
    dict(name="f0", routed=True, shared=1, units=9, per_expert=1, experts=8, gates=9, bias_rows=9, lora=0, act="gelu"),
    dict(name="f1", routed=True, shared=0, units=16, per_expert=2, experts=8, gates=8, bias_rows=8, lora=0, act="relu"),
    dict(name="f2", units=2, per_expert=2, experts=8, gates=1, bias_rows=1, lora=4, act="relu"),
    dict(name="f3", routed=True, shared=2, units=10, per_expert=1, experts=8, gates=10, bias_rows=0, lora=0, act="silu"),
]


class Tally:

    def __init__(self, sem, per=0, base=0):
        self.sem, self.per, self.base, self.k, self.i = sem, per, base, 0, 0

    def round(self, i):
        self.i, self.k = i, 0

    def add(self, ins):
        ins.then_inc(self.sem, 1)
        self.k += 1

    def value(self):
        return self.i * self.per + (self.base + self.k)


class Step:

    def __init__(self, engine, sem, per=0, base=0):
        self.engine, self.t = engine, Tally(sem, per, base)

    def round(self, i):
        self.t.round(i)

    def did(self, ins):
        self.t.add(ins)

    def then(self, ins):
        self.t.add(ins)
        self.engine.wait_ge(self.t.sem, self.t.value())

    def filled(self):
        self.t.base, self.t.k = self.t.base + self.t.k, 0

    def check(self):
        assert self.t.k == self.t.per, (self.t.k, self.t.per)


def build(nc, dram, out, stages):
    with ExitStack() as whole:

        in_use = []

        def sem(name):
            in_use.append(nc.alloc_semaphore(name=name))
            return in_use[-1]

        def clear_semaphores():
            nc.clear_and_free_semaphores(in_use)
            nc.all_engine_barrier()
            in_use.clear()

        def resident(name, shape, dt=F32):
            return whole.enter_context(nc.sbuf_tensor(name, shape, dt))

        psum = whole.enter_context(nc.psum_tensor("psum", [P, 8, BANK], F32))
        x = resident("residual", [P, TILES, D])
        ident = resident("identity", [P, P])
        half = resident("half", [P, TILES])
        zero = resident("zero", [P, 1])
        half32 = resident("half32", [P, TPB * HEADS])
        ctxT = resident("ctx_features", [P, DC, NBATCH * CTX])
        g_all = resident("g_all", [P, 8])
        tg = resident("tg", [P, 8])
        rank = resident("ranks", [P, TILES, 8])
        stats = resident("stats", [P, TILES, 6])
        mv = resident("mv", [P, TILES, 2])
        var = resident("var", [P, TILES])
        rstd = resident("rstd", [P, TILES])

        context_w = resident("context_w", [P, 4 * DC * D * 2])
        env = dict(nc=nc, context_w=context_w, dram=dram, sem=sem, psum=psum, x=x, ident=ident, half=half, zero=zero, half32=half32, ctxT=ctxT, tg=tg,
                   rank=rank, stats=stats, mv=mv, var=var, rstd=rstd)
        if any(kind == "f" and FFN[n].get("routed") for kind, n in stages):
            env["sorted_x"] = nc.dram_tensor("sorted_x", (BLOCKS * BLOCK, D), F32, kind="Internal").ap()
            env["sorted_y"] = nc.dram_tensor("sorted_y", (BLOCKS * BLOCK, D), F32, kind="Internal").ap()
        env["x_stats_ready"] = False
        setup(env, g_all, stages[0][1] if stages[0][0] == "a" else None)
        for (kind, n), following in zip(stages, stages[1:] + [("", 0)]):
            with ExitStack() as scope:
                if kind == "a":
                    attention_layer(env, scope, n)
                else:
                    ffn_layer(env, scope, n, following[1] if following[0] == "a" else None)
            env["x_stats_ready"] = True
            clear_semaphores()
        store(env, out)


def context_weights(env, n):
    inner = HEADS * ATTN[n]["hd"]
    names = ["wk", "wv"] + (["wkr"] if ATTN[n]["rope"] else [])
    return {w: env["context_w"][:, j * DC * inner:(j + 1) * DC * inner].rearrange("p (c i) -> p c i", c=DC)
            for j, w in enumerate(names)}


def context_weight_loads(env, n):
    return [(v, env["dram"][f"{ATTN[n]['name']}_{w}"]) for w, v in context_weights(env, n).items()]


def setup(env, g_all, first_attention):
    nc, dram, x = env["nc"], env["dram"], env["x"]
    loaded, gates_loaded, made, tanhed = (env["sem"](n) for n in ("loaded", "gates_loaded", "made", "tanhed"))
    with nc.Block() as block:
        @block.sync
        def _(sp):
            sp.dma_start(x[:], dram["x"].rearrange("b (h p) d -> p (b h) d", p=P)).then_inc(loaded, 16)
            sp.dma_start(env["ctxT"][:], dram["ctxT"]).then_inc(loaded, 16)
            sp.dma_start(env["ident"][:], dram["ident"]).then_inc(loaded, 16)
            sp.dma_start(env["rank"][:], dram["rank"]).then_inc(loaded, 16)
            ahead = [] if first_attention is None else context_weight_loads(env, first_attention)
            for dst, src in ahead:
                sp.dma_start(dst, src).then_inc(loaded, 16)
            sp.wait_ge(loaded, 16 * (4 + len(ahead)))

        @block.scalar
        def _(act):
            act.dma_start(g_all[:, 0:4], dram["g_xattn"].partition_broadcast(P)).then_inc(gates_loaded, 16)
            act.dma_start(g_all[:, 4:8], dram["g_ffn"].partition_broadcast(P)).then_inc(gates_loaded, 16)
            act.wait_ge(gates_loaded, 32)
            nc.scalar.activation(env["tg"][:], g_all[:], ACT.Tanh).then_inc(tanhed, 1)

        @block.gpsimd
        def _(pool):
            nc.gpsimd.memset(env["half"][:], -0.5).then_inc(made, 1)
            nc.gpsimd.memset(env["half32"][:], -0.5).then_inc(made, 1)
            nc.gpsimd.memset(env["zero"][:], 0.0).then_inc(made, 1)


def store(env, out):
    stored = env["sem"]("stored")
    with env["nc"].Block() as block:
        @block.sync
        def _(sp):
            sp.dma_start(out.rearrange("b (h p) d -> p (b h) d", p=P), env["x"][:]).then_inc(stored, 16)
            sp.wait_ge(stored, 16)


def emit_statistics(nc, dve, source, into, stats_done, var_done, rows=P, tiles=TILES, ready=False):
    stats, mv, var = into["stats"], into["mv"], into["var"]
    if not ready:
        for t in range(tiles):
            last = nc.vector.bn_stats(stats[0:rows, t, :], source[0:rows, t, :])
        last.then_inc(stats_done, 1)
        dve.wait_ge(stats_done, 1)
    for t in range(tiles):
        last = nc.vector.bn_aggr(mv[0:rows, t, :], stats[0:rows, t, :])
    last.then_inc(stats_done, 1)
    dve.wait_ge(stats_done, 1 + (not ready))
    nc.vector.tensor_scalar(var[0:rows, 0:tiles], mv[0:rows, 0:tiles, 1], EPS, None, ALU.add).then_inc(var_done, 1)


def ffn_layer(env, scope, n, following):
    cfg = FFN[n]
    nc = env["nc"]

    def sb(name, shape, dt=F32):
        return scope.enter_context(nc.sbuf_tensor(f"{cfg['name']}_{name}", shape, dt))

    routed = cfg.get("routed", False)
    t = dict(gates=sb("gates", [P, TILES, cfg["gates"]]), last=following is None)
    if routed:
        t["xn_all"] = sb("xn_all", [P, TILES, D])
        if cfg["shared"]:
            t["xT_all"] = sb("xT_all", [P, DC, TOKENS])
        t["rows"] = sb("rows", [P, 2 * TILES], I32)
        t["chosen_gates"] = sb("chosen_gates", [P, 2, TILES])
        t["block_expert"] = sb("block_expert", [P, BLOCKS], I32)
    else:
        t["xh"], t["xl"] = sb("xh", [P, DC, TOKENS], F32R), sb("xl", [P, DC, TOKENS], F32R)
    if cfg["lora"]:
        t["uh"] = sb("uh", [32, TOKENS], F32R)
        t["ul"] = sb("ul", [32, TOKENS], F32R)
    r_sync, r_gpsimd, r_tensor, r_biases, r_scalar, r_vector = route(env, scope, n, t)
    e_sync, e_gpsimd, e_tensor, e_scalar, e_vector, credits = (routed_experts if routed else experts)(env, scope, n, t)
    ahead = [] if following is None else context_weight_loads(env, following)
    ahead_in = env["sem"](f"{cfg['name']}_ahead_in")
    with nc.Block() as block:
        @block.sync
        def _(sp):
            r_sync(sp)
            e_sync(sp)
            for dst, src in ahead:
                sp.dma_start(dst, src).then_inc(ahead_in, 16)
            if ahead:
                sp.wait_ge(ahead_in, 16 * len(ahead))

        @block.gpsimd
        def _(pool):
            r_gpsimd(pool)
            e_gpsimd(pool)

        @block.tensor
        def _(pe):
            credits[0](pe)
            r_tensor(pe)
            e_tensor(pe, r_biases)

        @block.scalar
        def _(act):
            credits[1](act)
            r_scalar(act)
            e_scalar(act)

        @block.vector
        def _(dve):
            credits[2](dve)
            r_vector(dve)
            e_vector(dve)


def route(env, scope, n, t):
    cfg = FFN[n]
    nc, dram, psum, x, ident = env["nc"], env["dram"], env["psum"], env["x"], env["ident"]
    mv, var, rstd, tg, rank = env["mv"], env["var"], env["rstd"], env["tg"], env["rank"]
    name, E, NG, NB = cfg["name"], cfg["experts"], cfg["gates"], cfg["bias_rows"]
    NR = E * (1 + cfg["lora"])
    gate = tg[:, 4 + n:5 + n]
    routed, gates = cfg.get("routed", False), t["gates"]
    if not routed:
        xh, xl = t["xh"], t["xl"]

    def sb(nm, shape, dt=F32):
        return scope.enter_context(nc.sbuf_tensor(f"{name}_{nm}_sb", shape, dt))

    wr = sb("wr", [P, DC, NR])
    rb = sb("rb", [P, E])
    if not routed:
        xn_ring = sb("xn", [P, 2, TPB, D])
    xn = lambda b: t["xn_all"][:, b * TPB:(b + 1) * TPB, :] if routed else xn_ring[:, b % 2]
    shared = routed and cfg["shared"]
    if not shared:
        stage_ring = sb("stage", [P, 2, DC, SEQ])
    stage = lambda b: t["xT_all"][:, :, b * SEQ:(b + 1) * SEQ] if shared else stage_ring[:, b % 2]
    consts = [(wr[:], dram[f"{name}_wr"]), (rb[:], dram[f"{name}_rb"].partition_broadcast(P))]
    columns = sb("columns", [NR, 2, SEQ])
    logits = sb("logits", [P, TILES, E])
    a, b, c, oh1, oh2 = (sb(nm, [P, TILES, E]) for nm in ("ra", "rexp", "rc", "oh1", "oh2"))
    m1, m2 = sb("m1", [P, TILES]), sb("m2", [P, TILES])
    if NB:
        b2 = sb("b2", [NB, D])
        gT = sb("gT", [NB, 2, 512])
        consts += [(b2[:], dram[f"{name}_b2"])]
    if routed:
        before, ones = sb("before", [P, P]), sb("ones", [P, P])
        thresholds, up_to = sb("thresholds", [P, E, 8]), sb("up_to", [P, E, E])
        block_index = sb("block_index", [P, BLOCKS, E])
        totals, scan, behind = (sb(nm, [P, TILES, E]) for nm in ("totals", "scan", "behind"))
        spread8 = sb("spread8", [P, E, 8])
        used, ends, starts = (sb(nm, [P, E]) for nm in ("used", "ends", "starts"))
        past = sb("past", [P, BLOCKS, E])
        expert_f, rows_f = sb("expert_f", [P, BLOCKS]), sb("rows_f", [P, 2, TILES])
        consts += [(before[:], dram["before"]), (ones[:], dram["ones"]), (thresholds[:], dram["thresholds"]),
                   (up_to[:], dram["up_to"]), (block_index[:], dram["block_index"])]
    if cfg["lora"]:
        um = sb("um", [P, TILES, 32])
        ust = sb("ust", [32, 2, 512])
    sems = {k: env["sem"](f"{name}_{k}") for k in (
        "consts", "stats1", "chain", "var_done", "rstd_done", "normed", "turned", "staged", "high",
        "low", "routed", "columns_out", "columns_turned", "logits_read", "shifted", "exped", "gates_done", "gates_turned", "gates_copied", "bias_mm",
        "bias_added", "u_turned", "u_staged", "u_high", "chosen", "counted", "rows_done", "blocks_done")}
    t["rows_done"], t["blocks_done"] = sems["rows_done"], sems["blocks_done"]
    n_consts = 16 * len(consts)
    xT_ps = lambda b: psum[:, 3 * (b % 2), :].rearrange("p (c s) -> p c s", c=DC)
    lt_ps = lambda b: psum[0:NR, 1 + b % 2, 0:SEQ]
    rt_ps = psum[:, 4:6, :].rearrange("p k (t r) -> p (k t) r", r=64)

    def sync(sp):
        for dst, src in consts:
            sp.dma_start(dst, src).then_inc(sems["consts"], 16)

    def find_rows(dve, step):
        pairs, wide = [P, TILES, E], [P, E, E]
        dve.wait_ge(sems["counted"], 1)
        step.then(nc.vector.tensor_copy(totals[:].rearrange("p t e -> p (t e)"),
                                        psum[:, 3, TILES * E:2 * TILES * E]))
        have, other, d = totals, scan, 1
        while d < TILES:
            step.did(nc.vector.tensor_copy(other[:, 0:d, :], have[:, 0:d, :]))
            step.then(nc.vector.tensor_tensor(other[:, d:, :], have[:, d:, :], have[:, 0:TILES - d, :], ALU.add))
            have, other, d = other, (behind if have is totals else have), 2 * d
        counts = have[:, TILES - 1:TILES, :]
        step.then(nc.vector.tensor_tensor(spread8[:], counts.rearrange("p o e -> p e o").to_broadcast([P, E, 8]),
                                          thresholds[:], ALU.is_gt))
        step.then(nc.vector.tensor_reduce(used[:], spread8[:], AX.X, ALU.add))
        step.then(nc.vector.tensor_tensor(spread8[:], used[:].unsqueeze(1).to_broadcast(wide), up_to[:], ALU.mult))
        step.then(nc.vector.tensor_reduce(ends[:], spread8[:], AX.X, ALU.add))
        step.did(nc.vector.tensor_tensor(starts[:], ends[:], used[:], ALU.subtract))
        step.then(nc.vector.tensor_tensor(other[:], have[:], totals[:], ALU.subtract))
        step.then(nc.vector.tensor_tensor(other[:], other[:], psum[:, 3, 0:TILES * E].rearrange(
            "p (t e) -> p t e", e=E), ALU.add))
        step.then(nc.vector.scalar_tensor_tensor(other[:], starts[:].unsqueeze(1).to_broadcast(pairs), float(BLOCK),
                                                 other[:], ALU.mult, ALU.add))
        first = totals
        step.then(nc.vector.tensor_tensor(first[:], oh1[:], oh2[:], ALU.subtract))
        for k, choice in enumerate((first, oh2)):
            step.then(nc.vector.tensor_tensor(have[:], other[:], choice[:], ALU.mult))
            step.then(nc.vector.tensor_reduce(rows_f[:, k, :], have[:], AX.X, ALU.add))
        nc.vector.tensor_copy(t["rows"][:], rows_f[:].rearrange("p k t -> p (k t)")).then_inc(sems["rows_done"], 1)
        step.then(nc.vector.tensor_tensor(past[:], block_index[:], ends[:].unsqueeze(1).to_broadcast([P, BLOCKS, E]),
                                          ALU.is_ge))
        step.then(nc.vector.tensor_reduce(expert_f[:], past[:], AX.X, ALU.add))
        nc.vector.tensor_scalar(t["block_expert"][:], expert_f[:], float(E - 1), None, ALU.min).then_inc(
            sems["blocks_done"], 1)
        for k, choice in enumerate((first, oh2)):
            step.then(nc.vector.tensor_tensor(have[:], gates[:, :, 0:E], choice[:], ALU.mult))
            step.then(nc.vector.tensor_reduce(t["chosen_gates"][:, k, :], have[:], AX.X, ALU.add))

    def gpsimd(pool):
        pool.wait_ge(sems["var_done"], 1)
        nc.gpsimd.tensor_tensor(rstd[:], var[:], env["half"][:], ALU.pow).then_inc(sems["rstd_done"], 1)

    def vector(dve):
        step = Step(dve, sems["chain"])
        emit_statistics(nc, dve, x, env, sems["stats1"], sems["var_done"], ready=env["x_stats_ready"])
        dve.wait_ge(sems["rstd_done"], 1)
        for b_ in range(NBATCH + 1):
            if b_ < NBATCH:
                if b_ >= 2 and not routed:
                    dve.wait_ge(sems["turned"], b_ - 1)
                for h in range(TPB):
                    tile = b_ * TPB + h
                    last = nc.vector.tensor_scalar(xn(b_)[:, h, :], x[:, tile, :], mv[:, tile, 0:1],
                                                   rstd[:, tile:tile + 1], ALU.subtract, ALU.mult)
                last.then_inc(sems["normed"], 1)
            if b_ >= 1 and not routed:
                dve.wait_ge(sems["high"], b_)
                where = slice((b_ - 1) * SEQ, b_ * SEQ)
                nc.vector.tensor_tensor(xl[:, :, where], stage(b_ - 1), xh[:, :, where].bitcast(F32),
                                        ALU.subtract).then_inc(sems["low"], 1)
        dve.wait_ge(sems["columns_turned"], NBATCH)
        dve.wait_ge(sems["consts"], n_consts)
        wide = [P, TILES, E]

        def over(v):
            return v.unsqueeze(2).to_broadcast(wide)

        if n == 3:
            nc.vector.tensor_copy(logits[:], rt_ps[:, :, 0:E]).then_inc(sems["logits_read"], 1)
        else:
            nc.vector.tensor_tensor(logits[:], rt_ps[:, :, 0:E], rb[:].unsqueeze(1).to_broadcast(wide),
                                    ALU.add).then_inc(sems["logits_read"], 1)
        dve.wait_ge(sems["logits_read"], 1)

        def softmax_rows(dst):
            step.then(nc.vector.tensor_reduce(m1[:], logits[:], AX.X, ALU.max))
            nc.vector.tensor_tensor(a[:], logits[:], over(m1[:]), ALU.subtract).then_inc(sems["shifted"], 1)
            dve.wait_ge(sems["exped"], 1)
            step.then(nc.vector.tensor_reduce(m2[:], b[:], AX.X, ALU.add))
            step.then(nc.vector.reciprocal(m2[:], m2[:]))
            step.then(nc.vector.tensor_tensor(dst[:], b[:], over(m2[:]), ALU.mult))

        def first_largest(dst, values):
            step.then(nc.vector.tensor_reduce(m1[:], values[:], AX.X, ALU.max))
            step.then(nc.vector.tensor_tensor(dst[:], values[:], over(m1[:]), ALU.is_equal))
            step.then(nc.vector.tensor_tensor(dst[:], dst[:], rank[:], ALU.mult))
            step.then(nc.vector.tensor_reduce(m2[:], dst[:], AX.X, ALU.max))
            step.then(nc.vector.tensor_tensor(dst[:], dst[:], over(m2[:]), ALU.is_equal))

        def second_largest(values, spare):
            step.then(nc.vector.scalar_tensor_tensor(spare[:], oh1[:], -HUGE, values[:], ALU.mult, ALU.add))
            first_largest(oh2, spare)
            nc.vector.tensor_tensor(oh1[:], oh1[:], oh2[:], ALU.add).then_inc(sems["chosen"], 1)
            dve.wait_ge(sems["chosen"], 1)

        def set_gates(weights):
            return nc.vector.tensor_scalar(gates[:, :, 0:E], weights[:], gate, None, ALU.mult)

        def set_plain_gates(first):
            return nc.vector.tensor_scalar(gates[:, :, first:NG], rank[:, :, 0:NG - first], 0.0, gate,
                                           ALU.mult, ALU.add)

        if n in (0, 3):
            softmax_rows(c)
            if n == 3:
                step.then(nc.vector.tensor_tensor(b[:], c[:], rb[:].unsqueeze(1).to_broadcast(wide), ALU.add))
                first_largest(oh1, b)
                second_largest(b, a)
            else:
                first_largest(oh1, c)
                second_largest(c, a)
            step.then(nc.vector.tensor_tensor(a[:], c[:], oh1[:], ALU.mult))
            set_gates(a)
            last = set_plain_gates(E)
        elif n == 1:
            first_largest(oh1, logits)
            second_largest(logits, a)
            step.then(nc.vector.tensor_reduce(m1[:], logits[:], AX.X, ALU.max))
            nc.vector.tensor_tensor(a[:], logits[:], over(m1[:]), ALU.subtract).then_inc(sems["shifted"], 1)
            dve.wait_ge(sems["exped"], 1)
            step.then(nc.vector.tensor_tensor(c[:], b[:], oh1[:], ALU.mult))
            step.then(nc.vector.tensor_reduce(m2[:], c[:], AX.X, ALU.add))
            step.then(nc.vector.reciprocal(m2[:], m2[:]))
            step.then(nc.vector.tensor_tensor(a[:], c[:], over(m2[:]), ALU.mult))
            last = set_gates(a)
        else:
            softmax_rows(c)
            first_largest(oh1, c)
            set_plain_gates(0)
            with_r = [P, TILES, E, cfg["lora"]]
            last = nc.vector.tensor_tensor(
                um[:].rearrange("p t (e r) -> p t e r", r=cfg["lora"]),
                rt_ps[:, :, E:NR].rearrange("p t (e r) -> p t e r", r=cfg["lora"]),
                oh1[:].unsqueeze(3).to_broadcast(with_r), ALU.mult)
        last.then_inc(sems["gates_done"], 1)
        if routed:
            find_rows(dve, step)
        if cfg["lora"]:
            for k in range(4):
                dve.wait_ge(sems["u_high"], k + 1)
                nc.vector.tensor_tensor(t["ul"][:, k * 512:(k + 1) * 512], ust[:, k % 2, :],
                                        t["uh"][:, k * 512:(k + 1) * 512].bitcast(F32),
                                        ALU.subtract).then_inc(sems["u_staged"], 1)

        for k in range(TILES // 2 if NB else 0):
            dve.wait_ge(sems["bias_mm"], k + 1)
            nc.vector.tensor_tensor(x[:, 2 * k:2 * k + 2, :], x[:, 2 * k:2 * k + 2, :],
                                    psum[:, 6 + k % 2, :].rearrange("p (t d) -> p t d", t=2),
                                    ALU.add).then_inc(sems["bias_added"], 1)
    def scalar(act):
        for b_ in range(NBATCH + 1):
            if b_ < NBATCH:
                act.wait_ge(sems["turned"], b_ + 1)
                if b_ >= 2:
                    if not routed:
                        act.wait_ge(sems["low"], b_ - 1)
                    act.wait_ge(sems["routed"], b_ - 1)
                nc.scalar.activation(stage(b_), xT_ps(b_), ACT.Copy).then_inc(sems["staged"], 1)
                if not routed:
                    nc.scalar.activation(xh[:, :, b_ * SEQ:(b_ + 1) * SEQ], xT_ps(b_), ACT.Copy).then_inc(
                        sems["high"], 1)
            if b_ >= 1:
                act.wait_ge(sems["routed"], b_)
                if b_ >= 3:
                    act.wait_ge(sems["columns_turned"], b_ - 2)
                nc.scalar.activation(columns[:, (b_ - 1) % 2, :], lt_ps(b_ - 1), ACT.Copy).then_inc(
                    sems["columns_out"], 1)
        act.wait_ge(sems["shifted"], 1)
        nc.scalar.activation(b[:], a[:], ACT.Exp).then_inc(sems["exped"], 1)
        for k in range(4 if cfg["lora"] else 0):
            act.wait_ge(sems["u_turned"], k + 1)
            if k >= 2:
                act.wait_ge(sems["u_staged"], k - 1)
            nc.scalar.activation(ust[:, k % 2, :], psum[0:32, 4 + k % 2, :], ACT.Copy)
            nc.scalar.activation(t["uh"][:, k * 512:(k + 1) * 512], psum[0:32, 4 + k % 2, :], ACT.Copy).then_inc(
                sems["u_high"], 1)

        for k in range(4 if NB else 0):
            act.wait_ge(sems["gates_turned"], k + 1)
            if k >= 2:
                act.wait_ge(sems["bias_mm"], 2 * (k - 1))
            nc.scalar.activation(gT[:, k % 2, :], psum[0:NB, 4 + k % 2, :], ACT.Copy).then_inc(
                sems["gates_copied"], 1)
    def tensor(pe):
        pe.wait_ge(sems["consts"], n_consts)
        for b_ in range(NBATCH + 2):
            if b_ < NBATCH:
                pe.wait_ge(sems["normed"], b_ + 1)
                if b_ >= 2:
                    pe.wait_ge(sems["staged" if routed else "high"], b_ - 1)
                for c_ in range(DC):
                    for h in range(TPB):
                        last = nc.tensor.transpose(xT_ps(b_)[:, c_, h * P:(h + 1) * P],
                                                   xn(b_)[:, h, c_ * P:(c_ + 1) * P], ident[:])
                last.then_inc(sems["turned"], 1)
            if 1 <= b_ <= NBATCH:
                pe.wait_ge(sems["staged"], b_)
                if b_ >= 3:
                    pe.wait_ge(sems["columns_out"], b_ - 2)
                for c_ in range(DC):
                    last = nc.tensor.matmul(lt_ps(b_ - 1), wr[:, c_, :], stage(b_ - 1)[:, c_, :],
                                            start=(c_ == 0), stop=(c_ == DC - 1))
                last.then_inc(sems["routed"], 1)
            if b_ >= 2:
                pe.wait_ge(sems["columns_out"], b_ - 1)
                for h in range(TPB):
                    last = nc.tensor.transpose(rt_ps[:, (b_ - 2) * TPB + h, 0:NR],
                                               columns[:, (b_ - 2) % 2, h * P:(h + 1) * P], ident[0:NR, 0:NR])
                last.then_inc(sems["columns_turned"], 1)
        if not routed:
            pe.wait_ge(sems["low"], NBATCH)
        pe.wait_ge(sems["gates_done" if cfg["lora"] else "logits_read"], 1)
        if cfg["lora"]:
            low_rank_inputs(pe)

    def turn_gates(pe, k):
        if k >= 2:
            pe.wait_ge(sems["gates_copied"], k - 1)
        for q in range(4):
            last = nc.tensor.transpose(psum[0:NB, 4 + k % 2, q * P:(q + 1) * P],
                                       gates[:, 4 * k + q, 0:NB], ident[:])
        last.then_inc(sems["gates_turned"], 1)

    def add_biases(pe, k):
        pe.wait_ge(sems["gates_copied"], k // 2 + 1)
        if k >= 2:
            pe.wait_ge(sems["bias_added"], k - 1)
        for q in range(2):
            tt = 2 * k + q
            last = nc.tensor.matmul(psum[:, 6 + k % 2, q * D:(q + 1) * D],
                                    gT[:, tt // 4 % 2, tt % 4 * P:(tt % 4 + 1) * P], b2[:], start=True, stop=True)
        last.then_inc(sems["bias_mm"], 1)

    def low_rank_inputs(pe):
        for k in range(4):
            if k >= 2:
                pe.wait_ge(sems["u_high"], k - 1)
            for q in range(4):
                last = nc.tensor.transpose(psum[0:32, 4 + k % 2, q * P:(q + 1) * P], um[:, 4 * k + q, :], ident[:])
            last.then_inc(sems["u_turned"], 1)
        pe.wait_ge(sems["u_staged"], 4)

    def biases(pe):
        if routed:
            pe.wait_ge(sems["chosen"], 1)
            choice = oh1[:].rearrange("p t e -> p (t e)")
            nc.tensor.matmul(psum[:, 3, 0:TILES * E], before[:], choice, start=True, stop=True)
            nc.tensor.matmul(psum[:, 3, TILES * E:2 * TILES * E], ones[:], choice, start=True,
                             stop=True).then_inc(sems["counted"], 1)
        if NB:
            pe.wait_ge(sems["gates_done"], 1)
            turn_gates(pe, 0)
            for k in range(4):
                if k < 3:
                    turn_gates(pe, k + 1)
                add_biases(pe, 2 * k)
                add_biases(pe, 2 * k + 1)
            pe.wait_ge(sems["bias_added"], TILES // 2)

    return sync, gpsimd, tensor, biases, scalar, vector


def experts(env, scope, n, t):
    cfg = FFN[n]
    nc, dram, psum, x = env["nc"], env["dram"], env["psum"], env["x"]
    name, U = cfg["name"], cfg["units"]
    silu = cfg["act"] == "silu"
    HB = UNIT // P
    HC = HB // 2 if silu else HB
    xh, xl, gates = t["xh"], t["xl"], t["gates"]
    func = {"gelu": ACT.Gelu, "relu": ACT.Relu, "silu": ACT.Silu}[cfg["act"]]
    pairs, odd = divmod(U, 2)
    looped = pairs - (0 if odd else 1)

    def sb(nm, shape, dt=F32):
        return scope.enter_context(nc.sbuf_tensor(f"{name}_{nm}_sb", shape, dt))

    zero = env["zero"][:]
    w1raw = [sb(f"w1raw{s}", [P, DC, UNIT]) for s in range(2)]
    w2raw = [sb(f"w2raw{s}", [P, HC, D]) for s in range(2)]
    w1h = [sb(f"w1h{s}", [P, DC, UNIT], F32R) for s in range(2)]
    w1l = [sb(f"w1l{s}", [P, DC, UNIT], F32R) for s in range(2)]
    w2h = [sb(f"w2h{s}", [P, HC, D], F32R) for s in range(2)]
    w2l = [sb(f"w2l{s}", [P, HC, D], F32R) for s in range(2)]
    h32 = sb("h32", [P, HC, CHUNK])
    hh = sb("hh", [P, 2, HC, CHUNK], F32R)
    hl = sb("hl", [P, 2, HC, CHUNK], F32R)
    b1 = None if silu else sb("b1", [P, U, HB])
    b1u = None if silu else sb("b1u", [P, 2, HB])
    s32 = sb("s32", [P, HC, CHUNK]) if silu else None
    if cfg["lora"]:
        lb = h32[0:32, 0:U, :]
        lbh, lbl = sb("lbh", [32, U, UNIT], F32R), sb("lbl", [32, U, UNIT], F32R)
    sems = {k: env["sem"](f"{name}x_{k}") for k in (
        "bias_in", "raw_in0", "raw_in1", "split_high", "split", "hidden", "gated", "multiplied",
        "activated", "lowered", "product", "added", "lora_split", "bias_set")}
    SPLIT0 = 3
    HID0 = HC if silu else HB
    LOW0 = HC
    PROD0 = 4 * CHUNKS + 1
    ADD0 = 4
    hid_ps = [psum[:, m, :] for m in range(HB)]
    y_ps = [psum[:, 4 + q, 0:D] for q in range(4)]

    def run(engine, body):
        if looped:
            with engine.Fori(0, looped) as i:
                body(i, 0, False)
                body(i, 1, False)
        body(looped, 0, bool(odd))
        if not odd:
            body(looped, 1, True)

    def run_ahead(engine, first, second, between=None):
        def body(i, s, last):
            for c in range(CHUNKS):
                if c < CHUNKS - 1:
                    first(i, s, c + 1)
                elif not last:
                    first(i + s, 1 - s, 0)
                second(i, s, c)

        first(0, 0, 0)
        if between:
            between(engine)
        run(engine, body)

    def sync(sp):
        if b1 is not None:
            sp.dma_start(b1[:], dram[f"{name}_b1"]).then_inc(sems["bias_in"], 16)
        if cfg["lora"]:
            sp.dma_start(lb[:], dram[f"{name}_lb"]).then_inc(sems["bias_in"], 16)

        def body(i, s, last):
            u = i * 2 + s
            sp.wait_ge(sems["split"], u * 2 + SPLIT0 - 2)
            sp.dma_start(w1raw[s][:], dram[f"{name}_w1"][u]).then_inc(sems[f"raw_in{s}"], 16)
            sp.dma_start(w2raw[s][:], dram[f"{name}_w2"][u]).then_inc(sems[f"raw_in{s}"], 16)

        run(sp, body)

    def gpsimd(pool):
        pool.sem_inc(sems["split"], SPLIT0)
        if cfg["lora"]:
            pool.wait_ge(sems["bias_in"], 32)
            nc.gpsimd.tensor_copy(lbh[:], lb[:]).then_inc(sems["lora_split"], 1)
            pool.wait_ge(sems["lora_split"], 1)
            nc.gpsimd.tensor_tensor(lbl[:], lb[:], lbh[:].bitcast(F32), ALU.subtract).then_inc(
                sems["lora_split"], 1)

        def body(i, s, last):
            u = i * 2 + s
            pool.wait_ge(sems[f"raw_in{s}"], i * 32 + 32)
            pool.wait_ge(sems["product"], u * 4 * CHUNKS + PROD0 - 4 * CHUNKS)
            nc.gpsimd.tensor_tensor(w1h[s][:], w1raw[s][:], zero.unsqueeze(2).to_broadcast([P, DC, UNIT]),
                                    ALU.add).then_inc(sems["split_high"], 1)
            nc.gpsimd.tensor_tensor(w2h[s][:], w2raw[s][:], zero.unsqueeze(2).to_broadcast([P, HC, D]),
                                    ALU.add).then_inc(sems["split_high"], 1)
            pool.wait_ge(sems["split_high"], u * 2 + 2)
            nc.gpsimd.tensor_tensor(w1l[s][:], w1raw[s][:], w1h[s][:].bitcast(F32),
                                    ALU.subtract).then_inc(sems["split"], 1)
            nc.gpsimd.tensor_tensor(w2l[s][:], w2raw[s][:], w2h[s][:].bitcast(F32),
                                    ALU.subtract).then_inc(sems["split"], 1)

        run(pool, body)

    def tensor(pe, between):
        if cfg["lora"]:
            pe.wait_ge(sems["lora_split"], 2)

        def first(i, s, c):
            u = i * 2 + s
            g = u * CHUNKS + c
            if c == 0:
                pe.wait_ge(sems["split"], u * 2 + 2 + SPLIT0)
            tok = slice(c * CHUNK, (c + 1) * CHUNK)
            for m in range(HB):
                if not silu:
                    pe.wait_ge(sems["activated"], g * HB + m + 1)
                else:
                    pe.wait_ge(sems["gated" if m < HC else "multiplied"], g * HC + m % HC + 1)
                cols = slice(m * P, (m + 1) * P)
                terms = [(w[s][:, k, cols], v[:, k, tok]) for k in range(DC)
                         for w, v in ((w1h, xh), (w1h, xl), (w1l, xh))]
                if cfg["lora"]:
                    terms += [(w[:, u, cols], v[:, tok]) for w, v in
                              ((lbh, t["uh"]), (lbh, t["ul"]), (lbl, t["uh"]))]
                for j, (w, v) in enumerate(terms):
                    last = nc.tensor.matmul(hid_ps[m], w, v, start=(j == 0), stop=(j == len(terms) - 1))
                last.then_inc(sems["hidden"], 1)

        def second(i, s, c):
            g = (i * 2 + s) * CHUNKS + c
            pe.wait_ge(sems["lowered"], g * HC + HC + LOW0)
            for q in range(4):
                pe.wait_ge(sems["added"], g * 4 + q + 1)
                tok = slice(q * P, (q + 1) * P)
                terms = [(v[:, c % 2, k, tok], w[s][:, k, :]) for k in range(HC)
                         for v, w in ((hh, w2h), (hh, w2l), (hl, w2h))]
                for j, (v, w) in enumerate(terms):
                    last = nc.tensor.matmul(y_ps[q], v, w, start=(j == 0), stop=(j == len(terms) - 1))
                last.then_inc(sems["product"], 1)

        run_ahead(pe, first, second, between)

    def scalar(act):
        if b1 is not None:
            act.wait_ge(sems["bias_in"], 16 + 16 * bool(cfg["lora"]))

        def plain(i, s, last):
            u = i * 2 + s
            nc.scalar.activation(b1u[:, s, :], b1[:, u, :], ACT.Copy).then_inc(sems["bias_set"], 1)
            for c in range(CHUNKS):
                g = u * CHUNKS + c
                if c == 0:
                    act.wait_ge(sems["bias_set"], u + 1)
                act.wait_ge(sems["product"], g * 4 + 4 + PROD0 - 8)
                for m in range(HB):
                    act.wait_ge(sems["hidden"], g * HB + m + 1)
                    act.wait_ge(sems["lowered"], g * HC + m + 1)
                    bias = b1u[:, s, m:m + 1]
                    nc.scalar.activation(h32[:, m, :], hid_ps[m], func, bias=bias)
                    nc.scalar.activation(hh[:, c % 2, m, :], hid_ps[m], func, bias=bias).then_inc(
                        sems["activated"], 1)

        def with_product(i, s, last):
            u = i * 2 + s
            for c in range(CHUNKS):
                g = u * CHUNKS + c
                act.wait_ge(sems["product"], g * 4 + 4 + PROD0 - 8)
                for m in range(HC):
                    act.wait_ge(sems["hidden"], g * HB + m + 1)
                    act.wait_ge(sems["multiplied"], g * HC + m + 1)
                    nc.scalar.activation(s32[:, m, :], hid_ps[m], func).then_inc(sems["gated"], 1)
                for m in range(HC):
                    act.wait_ge(sems["multiplied"], g * HC + m + 1 + HID0)
                    nc.scalar.activation(hh[:, c % 2, m, :], h32[:, m, :], ACT.Copy).then_inc(
                        sems["activated"], 1)

        run(act, with_product if silu else plain)

    def vector(dve):
        def first(i, s, c):
            g = (i * 2 + s) * CHUNKS + c
            if silu:
                for m in range(HC):
                    dve.wait_ge(sems["gated"], g * HC + m + 1 + HID0)
                    dve.wait_ge(sems["hidden"], g * HB + HC + m + 1)
                    dve.wait_ge(sems["lowered"], g * HC + m + 1)
                    nc.vector.tensor_tensor(h32[:, m, :], s32[:, m, :], hid_ps[HC + m], ALU.mult).then_inc(
                        sems["multiplied"], 1)
            for m in range(HC):
                dve.wait_ge(sems["activated"], g * HC + m + 1 + (0 if silu else HID0))
                nc.vector.tensor_tensor(hl[:, c % 2, m, :], h32[:, m, :], hh[:, c % 2, m, :].bitcast(F32),
                                        ALU.subtract).then_inc(sems["lowered"], 1)

        def second(i, s, c):
            u = i * 2 + s
            g = u * CHUNKS + c
            column = (i if cfg["per_expert"] == 2 else u)
            for q in range(4):
                tile = c * 4 + q
                dve.wait_ge(sems["product"], g * 4 + q + 1 + PROD0)
                final = isinstance(u, int) and u == U - 1
                nc.vector.scalar_tensor_tensor(x[:, tile, :], y_ps[q], gates[:, tile, bass.ds(column, 1)],
                                               x[:, tile, :], ALU.mult, ALU.add).then_inc(sems["added"], 1)
                if final:
                    dve.wait_ge(sems["added"], g * 4 + q + 1 + ADD0)
                    nc.vector.bn_stats(env["stats"][:, tile, :], x[:, tile, :])

        run_ahead(dve, first, second)

    def tensor_credits(pe):
        pe.sem_inc(sems["product"], PROD0)

    def scalar_credits(act):
        act.sem_inc(sems["gated" if silu else "activated"], HID0)

    def vector_credits(dve):
        dve.sem_inc(sems["lowered"], LOW0)
        dve.sem_inc(sems["added"], ADD0)
        if silu:
            dve.sem_inc(sems["multiplied"], HID0)

    return sync, gpsimd, tensor, scalar, vector, (tensor_credits, scalar_credits, vector_credits)


def routed_experts(env, scope, n, t):
    cfg = FFN[n]
    nc, dram, psum, x, ident = env["nc"], env["dram"], env["psum"], env["x"], env["ident"]
    xs, ys = env["sorted_x"], env["sorted_y"]
    name, per_expert = cfg["name"], cfg["per_expert"]
    HB = UNIT // P
    silu = cfg["act"] == "silu"
    HC = HB // 2 if silu else HB
    func = {"gelu": ACT.Gelu, "relu": ACT.Relu, "silu": ACT.Silu}[cfg["act"]]
    shared, experts_units = cfg["shared"], cfg["experts"] * per_expert
    HEAD = range(0, NBATCH // 2) if shared else range(0)
    TAIL = range(NBATCH // 2, NBATCH) if shared else range(0)
    gate, zero = env["tg"][:, 4 + n:5 + n], env["zero"][:]
    BT = BLOCK // P
    DEPTH = 4 // per_expert
    RING = 8

    def sb(nm, shape, dt=F32):
        return scope.enter_context(nc.sbuf_tensor(f"{name}_{nm}_sb", shape, dt))

    w1 = [sb(f"w1_{k}", [P, DC, UNIT]) for k in range(DEPTH * per_expert)]
    w2 = [sb(f"w2_{k}", [P, HC, D]) for k in range(DEPTH * per_expert)]
    b1 = None if silu else [sb(f"b1_{k}", [P, 1, HB]) for k in range(DEPTH * per_expert)]
    w1s = [sb(f"w1s_{u}", [P, DC, UNIT]) for u in range(shared)]
    w2s = [sb(f"w2s_{u}", [P, HC, D]) for u in range(shared)]
    b1s = None if silu else [sb(f"b1s_{u}", [P, 1, HB]) for u in range(shared)]
    PER_UNIT = 32
    block_rows = [sb(f"block_rows{s}", [P, BT, D]) for s in range(2)]
    block_T = [sb(f"block_T{s}", [P, DC, BLOCK]) for s in range(2)]
    block_h = [sb(f"block_h{s}", [P, DC, BLOCK], F32R) for s in range(2)]
    block_l = [sb(f"block_l{s}", [P, DC, BLOCK], F32R) for s in range(2)]
    w1h, w1l = ([sb(f"w1{part}{q}", [P, DC, UNIT], F32R) for q in range(2)] for part in "hl")
    w2h, w2l = ([sb(f"w2{part}{q}", [P, HC, D], F32R) for q in range(2)] for part in "hl")
    hidden = [sb(f"hidden{s}", [P, HC, BLOCK]) for s in range(2)]
    hidden_h = [sb(f"hidden_h{s}", [P, HC, BLOCK], F32R) for s in range(2)]
    hidden_l = [sb(f"hidden_l{s}", [P, HC, BLOCK], F32R) for s in range(2)]
    silus = [sb(f"silus{s}", [P, HC, BLOCK]) for s in range(2)] if silu else None
    result = [sb(f"result{s}", [P, BT, D]) for s in range(2)]
    gathered = [w1[j // 4][:].rearrange("p c i -> p (c i)")[:, j % 4 * D:(j % 4 + 1) * D] for j in range(RING)]
    nothing = sb("nothing", [P, 1, D])
    sems = {k: env["sem"](f"{name}x_{k}") for k in (
        ["cleared", "clear_in", "scattered", "turned", "turned_out", "hidden_out", "multiplied", "result_out",
         "combined", "shared_in", "shared_added", "silu_out", "rows_in0", "hid_ready", "w1_high", "w1_low", "w2_high", "w2_low",
         "block_low", "rounded", "lowered", "rows_in1", "stored0", "stored1"]
        + [f"{kind}_in{k}" for k in range(DEPTH * per_expert) for kind in "wb"] + [f"gathered{k}" for k in range(RING)])}
    OUT = 1 if silu else HB
    MULTIPLIED0, HIDDEN0, RESULT0, STORED0, READY0 = 2, 2 * OUT, 1, 16, 2 * HB
    hid_ready = sems["hid_ready"]
    U0, R0 = len(HEAD) * shared, len(HEAD)
    hid_ps = lambda k: psum[:, 2 * k:2 * k + 2, :].rearrange("p b (m s) -> p (b m) s", s=BLOCK)
    y_ps = [psum[:, 4 + q, 0:D] for q in range(BT)]
    turn_ps = lambda s: psum[:, 6 + s, :].rearrange("p (c s) -> p c s", c=DC)

    def run(engine, body):
        looped = (BLOCKS - max(DEPTH, 3)) // DEPTH
        with engine.Fori(0, looped) as i:
            for s in range(DEPTH):
                body(i * DEPTH + s, i, s, max(DEPTH, 3))
        for b in range(DEPTH * looped, BLOCKS):
            body(b, b // DEPTH, b % DEPTH, BLOCKS - 1 - b)

    def later(i, s, d):
        return i + (s + d) // DEPTH, (s + d) % DEPTH

    def unit_later(i, s, u, d):
        k = s * per_expert + u + d
        return i + k // (DEPTH * per_expert), k % (DEPTH * per_expert)

    def follows(ahead, u, d):
        return u + d < (ahead + 1) * per_expert

    def uses(i, s):
        return i * (DEPTH // 2) + s // 2

    def sync(sp):
        for u in range(shared):
            unit = experts_units + u
            sp.dma_start(w1s[u][:], dram[f"{name}_w1"][unit]).then_inc(sems["shared_in"], 16)
            sp.dma_start(w2s[u][:], dram[f"{name}_w2"][unit]).then_inc(sems["shared_in"], 16)
            if not silu:
                sp.dma_start(b1s[u][:], dram[f"{name}_b1"][:, unit:unit + 1, :]).then_inc(sems["shared_in"], 16)
        sp.wait_ge(sems["cleared"], 1)
        sp.dma_start(xs.rearrange("(k p) d -> p k d", p=P),
                     nothing[:].to_broadcast([P, BLOCKS * BT, D])).then_inc(sems["clear_in"], 16)
        for s in range(2):
            sp.dma_start(ys[s * BLOCK:s * BLOCK + P, :], nothing[:, 0, :]).then_inc(sems[f"stored{s}"], 16)

        def rows(b, s):
            sp.dma_start(block_rows[s][:], xs[bass.ds(b * BLOCK, BLOCK), :].rearrange(
                "(h p) d -> p h d", p=P)).then_inc(sems[f"rows_in{s}"], 16)

        def weights(b, s, freed):
            expert = sp.value_load(t["block_expert"][0:1, bass.ds(b, 1)], min_val=0, max_val=cfg["experts"] - 1)
            units = [expert * per_expert + u for u in range(per_expert)]
            for u, unit in enumerate(units):
                k = s * per_expert + u
                if freed:
                    sp.wait_ge(sems["w2_low"], (b - DEPTH) * per_expert + (u + 1))
                sp.dma_start(w1[k][:], dram[f"{name}_w1"][unit]).then_inc(sems[f"w_in{k}"], 16)
                sp.dma_start(w2[k][:], dram[f"{name}_w2"][unit]).then_inc(sems[f"w_in{k}"], 16)
            return units

        def biases(units, s):
            for u, unit in enumerate(units if not silu else []):
                k = s * per_expert + u
                sp.dma_start(b1[k][:], dram[f"{name}_b1"][:, bass.ds(unit, 1), :]).then_inc(sems[f"b_in{k}"], 16)

        sp.wait_ge(t["blocks_done"], 1)
        for b in range(DEPTH):
            biases(weights(b, b, False), b)
        sp.wait_ge(sems["scattered"], 2 * TILES * 16)
        rows(0, 0)
        rows(1, 1)
        sp.wait_ge(sems["turned"], 1)
        rows(2, 0)

        def body(b, i, s, ahead):
            if ahead >= 3:
                sp.wait_ge(sems["turned"], b + 2)
                rows(b + 3, (s + 1) % 2)
            units = weights(b + DEPTH, s, True) if ahead >= DEPTH else []
            sp.wait_ge(sems["result_out"], b + (R0 + 1 + RESULT0))
            sp.dma_start(ys[bass.ds(b * BLOCK, BLOCK), :].rearrange("(h p) d -> p h d", p=P),
                         result[s % 2][:]).then_inc(sems[f"stored{s % 2}"], 16)
            biases(units, s)

        run(sp, body)

    def gpsimd(pool):
        nc.gpsimd.memset(nothing[:], 0.0).then_inc(sems["cleared"], 1)
        pool.wait_ge(t["rows_done"], 1)
        pool.wait_ge(sems["clear_in"], 16)
        for j in range(2 * TILES):
            nc.gpsimd.indirect_dma_start(xs, bass.IndirectOffsetOnAxis(ap=t["rows"][:, j:j + 1], axis=0),
                                         t["xn_all"][:, j % TILES, :], None).then_inc(sems["scattered"], 16)

        def high(out, raw):
            return nc.gpsimd.tensor_tensor(out[:], raw[:], zero.unsqueeze(2).to_broadcast(raw.shape), ALU.add)

        def body(b, i, s, ahead):
            for u in range(per_expert):
                if follows(ahead, u, 2):
                    v, q = b * per_expert + (u + U0), (s * per_expert + u) % 2
                    round_, k = unit_later(i, s, u, 2)
                    pool.wait_ge(sems[f"w_in{k}"], round_ * PER_UNIT + PER_UNIT)
                    pool.wait_ge(hid_ready, v * HB + (HB + READY0))
                    high(w1h[q], w1[k]).then_inc(sems["w1_high"], 1)
                    pool.wait_ge(sems["multiplied"], v + (1 + MULTIPLIED0))
                    high(w2h[q], w2[k]).then_inc(sems["w2_high"], 1)

        run(pool, body)
        for s in range(2):
            pool.wait_ge(sems[f"stored{s}"], STORED0 + 16 * len(range(s, BLOCKS, 2)))
        for j in range(2 * TILES):
            if j >= RING:
                pool.wait_ge(sems["combined"], j - RING + 1)
            col = (j % 2) * TILES + j // 2
            nc.gpsimd.indirect_dma_start(gathered[j % RING], None, ys,
                                         bass.IndirectOffsetOnAxis(ap=t["rows"][:, col:col + 1], axis=0)).then_inc(
                                             sems[f"gathered{j % RING}"], 16)

    def tensor(pe, between):
        between(pe)

        def hidden_products(v, q, terms):
            pe.wait_ge(sems["hidden_out"], v * OUT - OUT + HIDDEN0)
            for m in range(HB):
                parts = [(w[:, c, m * P:(m + 1) * P], rhs[:, c, :]) for c in range(DC) for w, rhs in terms]
                for j, (w, rhs) in enumerate(parts):
                    last = nc.tensor.matmul(hid_ps(q)[:, m, :], w, rhs, start=(j == 0), stop=(j == len(parts) - 1))
                last.then_inc(hid_ready, 1)

        def result_products(r, terms, begin, end):
            if begin:
                pe.wait_ge(sems["result_out"], r + RESULT0)
            for h in range(BT):
                parts = [(v[:, m, h * P:(h + 1) * P], w[:, m, :]) for m in range(HC) for v, w in terms]
                for j, (v, w) in enumerate(parts):
                    last = nc.tensor.matmul(y_ps[h], v, w, start=(begin and j == 0),
                                            stop=(end and j == len(parts) - 1))
            last.then_inc(sems["multiplied"], 1)

        def turn(b, i, s):
            pe.wait_ge(sems[f"rows_in{s % 2}"], uses(i, s) * 16 + 16)
            pe.wait_ge(sems["turned_out"], b + 1)
            for c in range(DC):
                for h in range(BT):
                    last = nc.tensor.transpose(turn_ps(s % 2)[:, c, h * P:(h + 1) * P],
                                               block_rows[s % 2][:, h, c * P:(c + 1) * P], ident[:])
            last.then_inc(sems["turned"], 1)

        def first(b, i, s, u):
            k, v = s * per_expert + u, b * per_expert + u
            q = (s * per_expert + u) % 2
            pe.wait_ge(sems["w1_low"], v + 1)
            if u == 0:
                pe.wait_ge(sems["block_low"], b + 1 + 2)
            xh, xl = block_h[s % 2], block_l[s % 2]
            hidden_products(v + U0, q, ((w1h[q], xh), (w1h[q], xl), (w1l[q], xh)))

        def second(b, i, s, u):
            k, v = s * per_expert + u, b * per_expert + u
            q = (s * per_expert + u) % 2
            pe.wait_ge(sems["lowered"], v + 1)
            pe.wait_ge(sems["w2_low"], v + 1)
            result_products(b + R0, ((hidden_h[q], w2h[q]), (hidden_h[q], w2l[q]), (hidden_l[q], w2h[q])),
                            u == 0, u == per_expert - 1)

        def shared_blocks(blocks, v0, r0):
            order = [(b, u) for b in blocks for u in range(shared)]
            for j in range(len(order) + 1):
                if j < len(order):
                    b, u = order[j]
                    hidden_products(v0 + j, (v0 + j) % 2, ((w1s[u], t["xT_all"][:, :, b * BLOCK:(b + 1) * BLOCK]),))
                if j:
                    b, u = order[j - 1]
                    pe.wait_ge(sems["hidden_out"], (v0 + j) * OUT + HIDDEN0)
                    result_products(r0 + b - blocks.start, ((hidden[(v0 + j - 1) % 2], w2s[u]),), u == 0,
                                    u == shared - 1)

        def body(b, i, s, ahead):
            for u in range(per_expert):
                if u + 1 < per_expert:
                    first(b, i, s, u + 1)
                elif ahead:
                    first(b + 1, *later(i, s, 1), 0)
                if u == per_expert - 1 and ahead >= 2:
                    turn(b + 2, *later(i, s, 2))
                second(b, i, s, u)

        if shared:
            pe.wait_ge(sems["shared_in"], shared * (PER_UNIT + 16 * (not silu)))
            pe.wait_ge(t["rows_done"], 1)
        shared_blocks(HEAD, 0, 0)
        turn(0, 0, 0)
        turn(1, 0, 1)
        first(0, 0, 0, 0)
        run(pe, body)
        shared_blocks(TAIL, U0 + BLOCKS * per_expert, R0 + BLOCKS)

    def scalar(act):
        def take(b, s):
            act.wait_ge(sems["turned"], b + 1)
            act.wait_ge(sems["block_low"], b + 1)
            nc.scalar.activation(block_T[s][:], turn_ps(s), ACT.Copy)
            nc.scalar.activation(block_h[s][:], turn_ps(s), ACT.Copy).then_inc(sems["turned_out"], 1)

        def activate(v, q, bias, split):
            if silu:
                act.wait_ge(hid_ready, v * HB + (HC + READY0))
                nc.scalar.activation(silus[q][:], hid_ps(q)[:, 0:HC, :], func).then_inc(sems["silu_out"], 1)
                if split:
                    act.wait_ge(sems["hidden_out"], v + (1 + HIDDEN0))
                    nc.scalar.activation(hidden_h[q][:], hidden[q][:], ACT.Copy).then_inc(sems["rounded"], 1)
                return
            act.wait_ge(sems["multiplied"], v + (MULTIPLIED0 - 1))
            for m in range(HB):
                if m % 2 == 0:
                    act.wait_ge(hid_ready, v * HB + (m + 2 + READY0))
                if split:
                    nc.scalar.activation(hidden_h[q][:, m, :], hid_ps(q)[:, m, :], func, bias=bias[:, 0, m:m + 1])
                nc.scalar.activation(hidden[q][:, m, :], hid_ps(q)[:, m, :], func,
                                     bias=bias[:, 0, m:m + 1]).then_inc(sems["hidden_out"], 1)

        def shared_blocks(blocks, v0):
            for j in range(len(blocks) * shared):
                activate(v0 + j, (v0 + j) % 2, None if silu else b1s[j % shared], False)

        def body(b, i, s, ahead):
            for u in range(per_expert):
                k, v = s * per_expert + u, b * per_expert + u
                if not silu:
                    act.wait_ge(sems[f"b_in{k}"], i * 16 + 16)
                activate(v + U0, k % 2, None if silu else b1[k], True)
            if ahead >= 2:
                take(b + 2, s % 2)

        if shared:
            act.wait_ge(sems["shared_in"], shared * (PER_UNIT + 16 * (not silu)))
        shared_blocks(HEAD, 0)
        for v in range(2):
            act.wait_ge(sems[f"w_in{v}"], PER_UNIT)
            nc.scalar.activation(w1h[v][:], w1[v][:], ACT.Copy).then_inc(sems["w1_high"], 1)
            nc.scalar.activation(w2h[v][:], w2[v][:], ACT.Copy).then_inc(sems["w2_high"], 1)
        take(0, 0)
        take(1, 1)
        run(act, body)
        shared_blocks(TAIL, U0 + BLOCKS * per_expert)

    def vector(dve):
        def gated(v, q):
            dve.wait_ge(sems["silu_out"], v + 1)
            dve.wait_ge(hid_ready, v * HB + (HB + READY0))
            dve.wait_ge(sems["multiplied"], v + (MULTIPLIED0 - 1))
            nc.vector.tensor_tensor(hidden[q][:], silus[q][:], hid_ps(q)[:, HC:HB, :], ALU.mult).then_inc(
                sems["hidden_out"], 1)

        def shared_block(b, v0):
            for u in range(shared if silu else 0):
                gated(v0 + u, (v0 + u) % 2)
            dve.wait_ge(sems["multiplied"], v0 + shared + MULTIPLIED0)
            where = slice(b * BT, (b + 1) * BT)
            nc.vector.scalar_tensor_tensor(x[:, where, :], psum[:, 4:4 + BT, 0:D], gate, x[:, where, :],
                                           ALU.mult, ALU.add).then_inc(sems["result_out"], 1)

        def low(out, whole, part, sem):
            nc.vector.tensor_tensor(out[:], whole[:], part[:].bitcast(F32), ALU.subtract).then_inc(sems[sem], 1)

        def split_block(b, s):
            dve.wait_ge(sems["turned_out"], b + 1 + 2)
            low(block_l[s], block_T[s], block_h[s], "block_low")

        def body(b, i, s, ahead):
            for u in range(per_expert):
                v, q = b * per_expert + u, (s * per_expert + u) % 2
                if silu:
                    gated(v + U0, q)
                    dve.wait_ge(sems["rounded"], v + 1)
                else:
                    dve.wait_ge(sems["hidden_out"], v * OUT + (U0 * OUT + OUT + HIDDEN0))
                low(hidden_l[q], hidden[q], hidden_h[q], "lowered")
                if follows(ahead, u, 1):
                    dve.wait_ge(sems["w2_high"], v + 2)
                    low(w2l[1 - q], w2[unit_later(i, s, u, 1)[1]], w2h[1 - q], "w2_low")
                if follows(ahead, u, 2):
                    dve.wait_ge(sems["w1_high"], v + 3)
                    low(w1l[q], w1[unit_later(i, s, u, 2)[1]], w1h[q], "w1_low")
            if ahead >= 2:
                split_block(b + 2, s % 2)
            dve.wait_ge(sems["multiplied"], b * per_expert + (per_expert + U0 + MULTIPLIED0))
            dve.wait_ge(sems[f"stored{s % 2}"], uses(i, s) * 16 + STORED0)
            nc.vector.tensor_scalar(result[s % 2][:], psum[:, 4:4 + BT, 0:D], 1.0, None, ALU.mult).then_inc(
                sems["result_out"], 1)

        def combine(j):
            tile, k = divmod(j, 2)
            dve.wait_ge(sems[f"gathered{j % RING}"], 16 * (j // RING + 1))
            if j:
                dve.wait_ge(sems["combined"], j)
            if j and k == 0 and not t["last"]:
                nc.vector.bn_stats(env["stats"][:, tile - 1, :], x[:, tile - 1, :])
            nc.vector.scalar_tensor_tensor(x[:, tile, :], gathered[j % RING],
                                           t["chosen_gates"][:, k, tile:tile + 1], x[:, tile, :],
                                           ALU.mult, ALU.add).then_inc(sems["combined"], 1)

        for b in HEAD:
            shared_block(b, b * shared)
        dve.wait_ge(sems["w1_high"], 2)
        dve.wait_ge(sems["w2_high"], 1)
        low(w1l[0], w1[0], w1h[0], "w1_low")
        low(w2l[0], w2[0], w2h[0], "w2_low")
        low(w1l[1], w1[1], w1h[1], "w1_low")
        split_block(0, 0)
        split_block(1, 1)
        run(dve, body)
        if shared:
            dve.wait_ge(sems["result_out"], R0 + BLOCKS + RESULT0)
        for k, b in enumerate(TAIL):
            shared_block(b, U0 + BLOCKS * per_expert + k * shared)
            if k >= len(TAIL) // 2:
                dve.wait_ge(sems["result_out"], R0 + BLOCKS + k + 1 + RESULT0)
            for j in range(2 * TILES * k // len(TAIL), 2 * TILES * (k + 1) // len(TAIL)):
                combine(j)
        for j in range(0 if not shared else 2 * TILES, 2 * TILES):
            combine(j)
        if not t["last"]:
            dve.wait_ge(sems["combined"], 2 * TILES)
            nc.vector.bn_stats(env["stats"][:, TILES - 1, :], x[:, TILES - 1, :])

    def tensor_credits(pe):
        pe.sem_inc(sems["multiplied"], MULTIPLIED0)
        pe.sem_inc(hid_ready, READY0)

    def scalar_credits(act):
        act.sem_inc(sems["hidden_out"], HIDDEN0)
        act.sem_inc(sems["turned_out"], 2)

    def vector_credits(dve):
        dve.sem_inc(sems["result_out"], RESULT0)
        dve.sem_inc(sems["block_low"], 2)

    return sync, gpsimd, tensor, scalar, vector, (tensor_credits, scalar_credits, vector_credits)


def attention_layer(env, scope, n):
    cfg = ATTN[n]
    nc = env["nc"]
    name, hd, keys = cfg["name"], cfg["hd"], cfg["keys"]
    inner = HEADS * hd
    NC = inner // P
    per_chunk = P // hd

    def sb(nm, shape, dt=F32):
        return scope.enter_context(nc.sbuf_tensor(f"{name}_{nm}_sb", shape, dt))

    t = dict(
        inner=inner, NC=NC, per_chunk=per_chunk,
        xT=sb("xT", [P, DC, TOKENS]),
        keysT=sb("keysT", [P, NC, NBATCH, per_chunk, keys]),
        values=sb("values", [keys, NBATCH, HEADS, hd + 1]),
    )
    if cfg["mask"] == "given":
        t["mask_mul"] = sb("mask_mul", [P, TILES, CTX])
        t["mask_add"] = sb("mask_add", [P, TILES, CTX])
    if cfg["l2norm"]:
        t["gain"] = sb("gain", [P, D])
    t["wq"], t["wo"] = sb("wq", [P, DC, inner]), sb("wo", [P, NC, D])
    t["loads"] = [(t["wq"][:], env["dram"][f"{name}_wq"]), (t["wo"][:], env["dram"][f"{name}_wo"])]
    with ExitStack() as part:
        prepare_layer(env, part, n, t)
    with ExitStack() as part:
        attend(env, part, n, t)


def prepare_layer(env, scope, n, t):
    cfg = ATTN[n]
    nc, dram, psum, x, ident = env["nc"], env["dram"], env["psum"], env["x"], env["ident"]
    ctxT, tg, mv, rstd = env["ctxT"], env["tg"], env["mv"], env["rstd"]
    name, hd, keys, inner, NC, per_chunk = cfg["name"], cfg["hd"], cfg["keys"], t["inner"], t["NC"], t["per_chunk"]
    keysT, values, xT = t["keysT"], t["values"], t["xT"]
    own = cfg["l2norm"]
    gate = tg[:, n:n + 1]
    HALF = NBATCH // 2 * CTX

    def sb(nm, shape, dt=F32):
        return scope.enter_context(nc.sbuf_tensor(f"{name}_{nm}_sb", shape, dt))

    weights = context_weights(env, n)
    wk, wv = weights["wk"], weights["wv"]
    xn = sb("xn", [P, 2, TPB, D])
    loads = []
    if own:
        once = sb("once", [P, TILES, D])
        ln_in, ln_ctx = sb("ln_in", [P, 2, DC]), sb("ln_ctx", [P, 2, DC])
        ctx = sb("ctx", [CTX, NBATCH, D])
        ctxnT = sb("ctxnT", [P, DC, NBATCH * CTX])
        cs = dict(stats=sb("cstats", [P, NBATCH, 6]), mv=sb("cmv", [P, NBATCH, 2]), var=sb("cvar", [P, NBATCH]))
        crstd = sb("crstd", [P, NBATCH])
        out_rows = sb("out_rows", [P, 2, D])
        k_scale = sb("k_scale", [P, 1])
        ktm = [sb(f"ktm{i}", [keys, HEADS, hd]) for i in range(2)]
        kn = [sb(f"kn{i}", [keys, HEADS, hd]) for i in range(2)]
        square = sb("square", [keys, HEADS, hd])
        ss = [sb(f"ss{i}", [keys, HEADS]) for i in range(2)]
        rn = [sb(f"rnk{i}", [keys, HEADS]) for i in range(2)]
        loads += [(ctx[:], dram["ctx"]), (ln_ctx[:], dram[f"{name}_ln_ctx"]), (ln_in[:], dram[f"{name}_ln_in"]),
                  (out_rows[:], dram[f"{name}_ln_out"].partition_broadcast(P)),
                  (k_scale[:], dram[f"{name}_k_scale"]),
                  (ktm[0][CTX:keys, :, :], dram[f"{name}_null"][0:1, 0]),
                  (ktm[1][CTX:keys, :, :], dram[f"{name}_null"][0:1, 0]),
                  (values[CTX:keys, :, :, 0:hd], dram[f"{name}_null_v"])]
        source = ctxnT
    else:
        bk = sb("bk", [P, NC])
        bv = sb("bv", [CTX, inner])
        bo = sb("bo", [P, D])
        loads += [(bk[:], dram[f"{name}_bk"]), (bv[:], dram[f"{name}_bv"].partition_broadcast(CTX)),
                  (bo[:], dram[f"{name}_bo"].partition_broadcast(P))]
        source = ctxT
    if hd == 16:
        kT = sb("kT", [P, NC, NBATCH * CTX])
        own_rows = sb("own_rows", [P, per_chunk])
        loads += [(own_rows[:], dram["own_rows"])]
    if cfg["rope"]:
        wkr = weights["wkr"]
        bkr = sb("bkr", [P, NC])
        kr = sb("kr", [P, NC, NBATCH * CTX])
        cos, sin = sb("cos", [P, CTX]), sb("sin", [P, CTX])
        loads += [(bkr[:], dram[f"{name}_bkr"]),
                  (cos[:], dram["cos"][:, 0:CTX]), (sin[:], dram["sin"][:, 0:CTX])]
    if cfg["mask"] == "given":
        mask8 = sb("mask8", [P, TILES, CTX], U8)
        loads += [(mask8[:], dram["mask"])]
    later = t["loads"]
    added_row = sb("added_row", [P, D])
    sems = {k: env["sem"](f"{name}k_{k}") for k in (
        "loaded", "later", "chain", "pool_chain", "k_ready", "k_out", "v_ready", "v_out", "gated_row", "shaped",
        "stats", "stats2", "cstats", "var_done", "rstd_done", "cvar_done", "crstd_done", "ctxn_done", "ctx_turned",
        "ctx_out", "squares", "squared", "inverted", "k_normed", "kn_turned", "kn_out", "applied", "x_normed",
        "x_turned", "x_out")}
    k_list = [] if own else [(w, c, half) for w in ((wk, wkr) if cfg["rope"] else (wk,))
                             for c in range(NC) for half in range(2)]
    v_list = [(b, part) for b in range(NBATCH) for part in range(max(1, inner // BANK))]
    VN = min(inner, BANK)
    v_bank = lambda j: psum[0:CTX, 4 + j % 4, 0:VN]
    k_bank = lambda j: psum[:, j % 4, 0:HALF]
    x_bank = lambda b: psum[:, b % 2, :].rearrange("p (c s) -> p c s", c=DC)
    key_banks = lambda b: slice(4 * (b % 2), 4 * (b % 2) + 2)

    with nc.Block() as block:
        @block.sync
        def _(sp):
            for dst, src in loads:
                sp.dma_start(dst, src).then_inc(sems["loaded"], 16)
            for dst, src in later:
                sp.dma_start(dst, src).then_inc(sems["later"], 16)
            sp.wait_ge(sems["later"], 16 * len(later))

        @block.gpsimd
        def _(pool):
            step = Step(pool, sems["pool_chain"])
            if own:
                pool.wait_ge(sems["cvar_done"], 1)
                nc.gpsimd.tensor_tensor(crstd[0:CTX, :], cs["var"][0:CTX, :],
                                        env["half"][0:CTX, 0:NBATCH], ALU.pow).then_inc(sems["crstd_done"], 1)
            for k in range(2 if own else 1):
                pool.wait_ge(sems["var_done"], k + 1)
                nc.gpsimd.tensor_tensor(rstd[:], env["var"][:], env["half"][:], ALU.pow).then_inc(
                    sems["rstd_done"], 1)
            if per_chunk == 2:
                step.then(nc.gpsimd.memset(keysT[0:hd, :, :, 1, :], 0.0))
                step.then(nc.gpsimd.memset(keysT[hd:P, :, :, 0, :], 0.0))
            step.then(nc.gpsimd.memset(values[:, :, :, hd:hd + 1], 1.0))
            for b in range(NBATCH if own else 0):
                pool.wait_ge(sems["squared"], b + 1)
                nc.gpsimd.tensor_tensor(rn[b % 2][:], ss[b % 2][:], env["half"][0:keys, 0:HEADS],
                                        ALU.pow).then_inc(sems["inverted"], 1)
            pool.wait_ge(sems["gated_row"], 1)
            pool.wait_ge(sems["applied" if own else "x_normed"], 1 if own else NBATCH)
            nc.gpsimd.tensor_tensor(x[:], x[:], added_row[:].unsqueeze(1).to_broadcast([P, TILES, D]),
                                    ALU.add).then_inc(sems["pool_chain"], 1)

        @block.tensor
        def _(pe):
            def turn_x():
                for b in range(NBATCH):
                    pe.wait_ge(sems["x_normed"], b + 1)
                    if b >= 2:
                        pe.wait_ge(sems["x_out"], b - 1)
                    for c in range(DC):
                        for h in range(TPB):
                            last = nc.tensor.transpose(x_bank(b)[:, c, h * P:(h + 1) * P],
                                                       xn[:, b % 2, h, c * P:(c + 1) * P], ident[:])
                    last.then_inc(sems["x_turned"], 1)

            pe.wait_ge(sems["loaded"], 16 * len(loads))
            if own:
                pe.wait_ge(sems["ctxn_done"], 1)
                for j in range(4):
                    for q in range(4):
                        b = 4 * (j % 2) + q
                        last = nc.tensor.transpose(psum[:, j, q * CTX:(q + 1) * CTX],
                                                   ctx[:, b, (j // 2) * P:(j // 2 + 1) * P], ident[0:CTX, 0:CTX])
                    last.then_inc(sems["ctx_turned"], 1)
                pe.wait_ge(sems["ctx_out"], 4)
            for j, (w, c, half) in enumerate(k_list):
                if j >= 4:
                    pe.wait_ge(sems["k_out"], j - 3)
                for k in range(DC):
                    last = nc.tensor.matmul(k_bank(j), w[:, k, c * P:(c + 1) * P],
                                            source[:, k, half * HALF:(half + 1) * HALF],
                                            start=(k == 0), stop=(k == DC - 1))
                last.then_inc(sems["k_ready"], 1)
            if not own:
                pe.wait_ge(sems["k_out"], len(k_list))
                turn_x()
            for j, (b, part) in enumerate(v_list):
                if j >= 4:
                    pe.wait_ge(sems["v_out"], j - 3)
                for k in range(DC):
                    last = nc.tensor.matmul(v_bank(j), source[:, k, b * CTX:(b + 1) * CTX],
                                            wv[:, k, part * VN:(part + 1) * VN], start=(k == 0), stop=(k == DC - 1))
                last.then_inc(sems["v_ready"], 1)
            if own:
                turn_x()
                pe.wait_ge(sems["x_out"], NBATCH)
                pe.wait_ge(sems["v_out"], len(v_list))

                def project(b):
                    if b >= 2:
                        pe.wait_ge(sems["k_out"], b - 1)
                    for part in range(2):
                        for k in range(DC):
                            last = nc.tensor.matmul(psum[0:CTX, key_banks(b).start + part, :],
                                                    source[:, k, b * CTX:(b + 1) * CTX],
                                                    wk[:, k, part * BANK:(part + 1) * BANK],
                                                    start=(k == 0), stop=(k == DC - 1))
                    last.then_inc(sems["k_ready"], 1)

                project(0)
                project(1)
                for b in range(NBATCH):
                    if b + 2 < NBATCH:
                        project(b + 2)
                    pe.wait_ge(sems["k_normed"], b + 1)
                    if b:
                        pe.wait_ge(sems["kn_out"], b)
                    for c in range(NC):
                        last = nc.tensor.transpose(psum[:, 2 + c // 4, (c % 4) * keys:(c % 4 + 1) * keys],
                                                   kn[b % 2][:, 2 * c:2 * c + 2, :].rearrange("p h d -> p (h d)"),
                                                   ident[0:keys, 0:keys])
                    last.then_inc(sems["kn_turned"], 1)

        @block.scalar
        def _(act):
            def x_out():
                for b in range(NBATCH):
                    act.wait_ge(sems["x_turned"], b + 1)
                    where = slice(b * SEQ, (b + 1) * SEQ)
                    if own:
                        for c in range(DC):
                            last = nc.scalar.activation(xT[:, c, where], x_bank(b)[:, c, :], ACT.Identity,
                                                        scale=ln_in[:, 0, c:c + 1], bias=ln_in[:, 1, c:c + 1])
                    else:
                        last = nc.scalar.activation(xT[:, :, where], x_bank(b), ACT.Copy)
                    last.then_inc(sems["x_out"], 1)

            act.wait_ge(sems["loaded"], 16 * len(loads))
            if own:
                for j in range(4):
                    act.wait_ge(sems["ctx_turned"], j + 1)
                    nc.scalar.activation(ctxnT[:, j // 2, (j % 2) * HALF:(j % 2 + 1) * HALF], psum[:, j, 0:HALF],
                                         ACT.Identity, scale=ln_ctx[:, 0, j // 2:j // 2 + 1],
                                         bias=ln_ctx[:, 1, j // 2:j // 2 + 1]).then_inc(sems["ctx_out"], 1)
            for j, (w, c, half) in enumerate(k_list):
                act.wait_ge(sems["k_ready"], j + 1)
                bias = bk if w is wk else bkr
                if hd == 16:
                    dst = kT if w is wk else kr
                    nc.scalar.activation(dst[:, c, half * HALF:(half + 1) * HALF], k_bank(j), ACT.Identity,
                                         bias=bias[:, c:c + 1]).then_inc(sems["k_out"], 1)
                else:
                    for s in range(2):
                        rows = slice(s * hd, (s + 1) * hd)
                        last = nc.scalar.activation(
                            keysT[rows, c, half * 4:half * 4 + 4, s, :],
                            psum[rows, j % 4, 0:HALF].rearrange("p (b k) -> p b k", k=CTX), ACT.Identity,
                            bias=bias[rows, c:c + 1])
                    last.then_inc(sems["k_out"], 1)
            if not own:
                x_out()
            else:
                for j, (b, part) in enumerate(v_list):
                    act.wait_ge(sems["v_ready"], j + 1)
                    heads = slice(part * (VN // hd), (part + 1) * (VN // hd))
                    nc.scalar.activation(values[0:CTX, b, heads, 0:hd],
                                         v_bank(j).rearrange("p (h d) -> p h d", d=hd), ACT.Copy).then_inc(
                                             sems["v_out"], 1)
                x_out()

                def take(b):
                    act.wait_ge(sems["k_ready"], b + 1)
                    if b >= 2:
                        act.wait_ge(sems["k_normed"], b - 1)
                    nc.scalar.activation(ktm[b % 2][0:CTX, :, :].rearrange("p h d -> p (h d)").rearrange(
                        "p (a c) -> p a c", a=2), psum[0:CTX, key_banks(b), :], ACT.Copy).then_inc(sems["k_out"], 1)
                    act.wait_ge(sems["k_out"], b + 1)
                    if b:
                        act.wait_ge(sems["squared"], b)
                    nc.scalar.activation(square[:], ktm[b % 2][:], ACT.Square).then_inc(sems["squares"], 1)

                def spread(b):
                    act.wait_ge(sems["kn_turned"], b + 1)
                    if b == 0:
                        act.wait_ge(sems["pool_chain"], 2)
                    for part in range(2):
                        for s in range(2):
                            rows = slice(s * hd, (s + 1) * hd)
                            last = nc.scalar.activation(
                                keysT[rows, part * 4:part * 4 + 4, b, s, :],
                                psum[rows, 2 + part, 0:4 * keys].rearrange("p (c k) -> p c k", k=keys),
                                ACT.Copy, scale=k_scale[rows, :])
                    last.then_inc(sems["kn_out"], 1)

                take(0)
                for b in range(NBATCH):
                    if b + 1 < NBATCH:
                        take(b + 1)
                    spread(b)

        @block.vector
        def _(dve):
            step = Step(dve, sems["chain"])
            if own:
                dve.wait_ge(sems["loaded"], 16 * len(loads))
                emit_statistics(nc, dve, ctx, cs, sems["cstats"], sems["cvar_done"], CTX, NBATCH)
                step.then(nc.vector.tensor_scalar(added_row[:], out_rows[:, 1, :], gate, None, ALU.mult))
                nc.vector.tensor_scalar(t["gain"][:], out_rows[:, 0, :], gate, None, ALU.mult).then_inc(
                    sems["gated_row"], 1)
                dve.wait_ge(sems["crstd_done"], 1)
                for b in range(NBATCH):
                    last = nc.vector.tensor_scalar(ctx[:, b, :], ctx[:, b, :], cs["mv"][0:CTX, b, 0:1],
                                                   crstd[0:CTX, b:b + 1], ALU.subtract, ALU.mult)
                last.then_inc(sems["ctxn_done"], 1)
            emit_statistics(nc, dve, x, env, sems["stats"], sems["var_done"], ready=env["x_stats_ready"])
            dve.wait_ge(sems["rstd_done"], 1)
            if own:
                for tile in range(TILES):
                    last = nc.vector.tensor_scalar(once[:, tile, :], x[:, tile, :], mv[:, tile, 0:1],
                                                   rstd[:, tile:tile + 1], ALU.subtract, ALU.mult)
                last.then_inc(sems["applied"], 1)
                dve.wait_ge(sems["applied"], 1)
                emit_statistics(nc, dve, once, env, sems["stats2"], sems["var_done"])
                dve.wait_ge(sems["rstd_done"], 2)
            for b in range(NBATCH):
                if b >= 2:
                    dve.wait_ge(sems["x_turned"], b - 1)
                for h in range(TPB):
                    tile = b * TPB + h
                    last = nc.vector.tensor_scalar(xn[:, b % 2, h, :], (once if own else x)[:, tile, :],
                                                   mv[:, tile, 0:1], rstd[:, tile:tile + 1], ALU.subtract, ALU.mult)
                last.then_inc(sems["x_normed"], 1)
            if not own:
                dve.wait_ge(sems["loaded"], 16 * len(loads))
                nc.vector.tensor_scalar(added_row[:], bo[:], gate, None, ALU.mult).then_inc(sems["gated_row"], 1)
            if cfg["mask"] == "given":
                step.then(nc.vector.tensor_copy(t["mask_mul"][:], mask8[:]))
                step.did(nc.vector.tensor_scalar(t["mask_add"][:], t["mask_mul"][:], -1.0, -L2_FILL / cfg["scale"],
                                                 ALU.add, ALU.mult))
            if hd == 16:
                dve.wait_ge(sems["k_out"], len(k_list))
                if cfg["rope"]:
                    wide = [P, NC * NBATCH, CTX]
                    for v, table in ((kT, cos), (kr, sin)):
                        v3 = v[:].rearrange("p c (b k) -> p (c b) k", k=CTX)
                        step.then(nc.vector.tensor_tensor(v3, v3, table[:].unsqueeze(1).to_broadcast(wide), ALU.mult))
                    step.then(nc.vector.tensor_tensor(kT[:], kT[:], kr[:], ALU.add))
                for c in range(NC):
                    for h in range(per_chunk):
                        last = nc.vector.tensor_scalar(keysT[:, c, :, h, :],
                                                       kT[:, c, :].rearrange("p (b k) -> p b k", k=CTX),
                                                       own_rows[:, h:h + 1], None, ALU.mult)
                last.then_inc(sems["shaped"], 1)
            if not own:
                for j, (b, part) in enumerate(v_list):
                    dve.wait_ge(sems["v_ready"], j + 1)
                    heads = slice(part * (VN // hd), (part + 1) * (VN // hd))
                    nc.vector.tensor_tensor(values[0:CTX, b, heads, 0:hd],
                                            v_bank(j).rearrange("p (h d) -> p h d", d=hd),
                                            bv[:, part * VN:(part + 1) * VN].rearrange("p (h d) -> p h d", d=hd),
                                            ALU.add).then_inc(sems["v_out"], 1)
            else:
                def sum_squares(b):
                    dve.wait_ge(sems["squares"], b + 1)
                    step.then(nc.vector.tensor_reduce(ss[b % 2][:], square[:], AX.X, ALU.add))
                    nc.vector.tensor_scalar(ss[b % 2][:], ss[b % 2][:], 1e-24, None, ALU.max).then_inc(
                        sems["squared"], 1)

                sum_squares(0)
                for b in range(NBATCH):
                    if b + 1 < NBATCH:
                        sum_squares(b + 1)
                    dve.wait_ge(sems["inverted"], b + 1)
                    if b >= 2:
                        dve.wait_ge(sems["kn_turned"], b - 1)
                    nc.vector.tensor_tensor(kn[b % 2][:], ktm[b % 2][:],
                                            rn[b % 2][:].unsqueeze(2).to_broadcast([keys, HEADS, hd]),
                                            ALU.mult).then_inc(sems["k_normed"], 1)


def attend(env, scope, n, t):
    cfg = ATTN[n]
    nc, dram, psum, x, ident, tg = env["nc"], env["dram"], env["psum"], env["x"], env["ident"], env["tg"]
    name, hd, keys, inner, NC = cfg["name"], cfg["hd"], cfg["keys"], t["inner"], t["NC"]
    xT, keysT, values = t["xT"], t["keysT"], t["values"]
    rope, own, mask = cfg["rope"], cfg["l2norm"], cfg["mask"]
    gate = tg[:, n:n + 1]
    STEPS = TPB * GROUPS
    wide = [P, GROUP, keys]

    def sb(nm, shape, dt=F32):
        return scope.enter_context(nc.sbuf_tensor(f"{name}_{nm}_sb", shape, dt))

    wq, wo = t["wq"], t["wo"]
    qT = sb("qT", [P, NC, SEQ])
    shifted = [sb(f"shifted{i}", wide) for i in range(2)]
    probs = [sb(f"probs{i}", wide) for i in range(2)]
    probsT = [sb(f"probsT{i}", [keys, GROUP * P]) for i in range(2)]
    top = [sb(f"top{i}", [P, GROUP]) for i in range(2)]
    inv = [sb(f"inv{i}", [P, GROUP]) for i in range(2)]
    att = [sb(f"att{i}", [P, HEADS, hd]) for i in range(TPB)]
    attT = [sb(f"attT{i}", [P, NC, P]) for i in range(TPB)]
    loads = []
    if own:
        q_scale = sb("q_scale", [P, 1])
        of_head = sb("of_head", [P, 2])
        q2 = sb("q2", [P, NC, SEQ])
        shift_by = sb("shift_by", [P, TILES])
        qss, qrn = sb("qss", [P, TPB, HEADS]), sb("qrn", [P, TPB, HEADS])
        y_all = env["context_w"][:].rearrange("p (t d) -> p t d", d=D)
        loads += [(q_scale[:], dram[f"{name}_q_scale"]), (of_head[:], dram["of_head"])]
    else:
        bq = sb("bq", [P, NC])
        loads += [(bq[:], dram[f"{name}_bq"])]
    if rope:
        wqr, bqr = sb("wqr", [P, DC, inner]), sb("bqr", [P, NC])
        q_raw, qr = sb("q_raw", [P, NC, SEQ]), sb("qr", [P, NC, SEQ])
        cos, sin = sb("cosq", [P, SEQ]), sb("sinq", [P, SEQ])
        loads += [(wqr[:], dram[f"{name}_wqr"]), (bqr[:], dram[f"{name}_bqr"]), (cos[:], dram["cos"]),
                  (sin[:], dram["sin"])]
    if mask == "window":
        window, seen = sb("window", [P, TPB, CTX]), sb("seen", [P, TPB])
        loads += [(window[:], dram["window"]), (seen[:], dram["seen"])]
    sems = {k: env["sem"](f"{name}l_{k}") for k in (
        "loaded", "q_ready", "q_out", "q_done", "sq_ready", "sq_out", "q_inverted", "scored", "s_free",
        "shift", "probs", "turned", "pt_out", "summed", "normed", "att_turned", "y_ready", "left", "chain",
        "stats", "var_done", "rstd_done", "applied", "gained", "shift_done", "added")}
    QUADS = TILES // 4

    SCORES, EXPS, TURN, SUMS = 6, 5, 4, 3
    NQ = (2 if rope else 1) * max(1, NC // 2)
    AT = max(1, NC // 4)
    QPS = 2
    Q_SLOTS = [range(q, min(q + QPS, NQ)) for q in range(0, NQ, QPS)]
    SQ_SLOT = len(Q_SLOTS)
    TURN_SLOT, OUT_SLOT, STATS_SLOT = (2, 5), (4, 6), (5, 7)

    uses = [("q_out", j + 1) for j in range(NQ)] + ([("sq_out", 1)] if own else [])
    LEFT = TPB * (AT + 1)
    CREDIT = 1
    first_left = len(uses)
    uses += [("left", j + 1) for j in range(LEFT)]
    spare = lambda use: psum[:, 6 + use % 2, :]

    def count(b, o, per, k):
        if isinstance(b, int):
            return max((b + o) * per + k, 0)
        assert o * per + k >= 0
        return b * per + (o * per + k)

    def at_spare(pe, b, o, use, last):
        kind = uses[use - 2][0] if use >= 2 else None
        if kind == "left" and uses[use][0] == "left":
            pe.wait_ge(sems["left"], count(b, o, LEFT, uses[use - 2][1] + CREDIT))
        elif use < 2 or (last and uses[use][0] == "left"):
            pe.wait_ge(sems["left"], count(b, 0, LEFT, CREDIT))
            pe.wait_ge(sems["q_out"], count(b, 0, NQ, NQ if o or last else 0))
            if own:
                pe.wait_ge(sems["sq_out"], count(b, 0, 1, 1 if o or last else 0))
        else:
            per = NQ if kind == "q_out" else 1
            ahead = 1 if uses[use][0] == "left" else o
            pe.wait_ge(sems[kind], count(b, ahead, per, uses[use - 2][1]))
        return spare(use)

    def stream(engine, prepare, slot, step=None):
        prepare(0, 0)
        for s in range(-SCORES, 0):
            slot(0, s, False)
        if step:
            step.filled()
        with engine.Fori(0, NBATCH - 1) as bi:
            if step:
                step.round(bi)
            for s in range(STEPS):
                slot(bi, s, False)
            if step:
                step.check()
        if step:
            step.round(NBATCH - 1)
        for s in range(STEPS):
            slot(NBATCH - 1, s, True)

    def item(fn, b, s, lead, last):
        g = s + lead
        if 0 <= g < STEPS:
            fn(b, 0, g)
        elif g >= STEPS and not last:
            fn(b, 1, g - STEPS)

    with nc.Block() as block:
        @block.sync
        def _(sp):
            for dst, src in loads:
                sp.dma_start(dst, src).then_inc(sems["loaded"], 16)

        @block.tensor
        def _(pe):
            def queries(b, o, j):
                w = wqr if rope and j >= NQ // 2 else wq
                bank = at_spare(pe, b, o, j, False)
                for s in range(2):
                    c = (2 * j + s) % NC
                    for k in range(DC):
                        last = nc.tensor.matmul(bank[:, s * SEQ:(s + 1) * SEQ], w[:, k, c * P:(c + 1) * P],
                                                xT[:, k, bass.ds((b + o) * SEQ, SEQ)],
                                                start=(k == 0), stop=(k == DC - 1))
                last.then_inc(sems["q_ready"], 1)

            def query_squares(b, o):
                pe.wait_ge(sems["q_out"], count(b, o, NQ, NQ))
                bank = at_spare(pe, b, o, NQ, False)
                for tile in range(TPB):
                    for c in range(NC):
                        col = tile * HEADS + 2 * c
                        last = nc.tensor.matmul(bank[:, col:col + 2], q2[:, c, tile * P:(tile + 1) * P],
                                                of_head[:], start=True, stop=True)
                last.then_inc(sems["sq_ready"], 1)

            def scores(b, o, g):
                tile, quad = divmod(g, GROUPS)
                if g < GROUPS:
                    if rope:
                        pe.wait_ge(sems["q_done"], count(b, o, 2, quad // 2 + 1))
                    else:
                        pe.wait_ge(sems["q_out"], count(b, o, NQ, min(quad + 1, NQ)))
                pe.wait_ge(sems["s_free" if own or mask else "shift"], count(b, o, STEPS, g - 1))
                rows = slice(tile * P, (tile + 1) * P)
                if hd == 16:
                    first = (quad % 2) * GROUP
                    last = nc.tensor.matmul(psum[:, g % 2, 0:GROUP * keys], qT[:, quad // 2, rows],
                                            keysT[:, quad // 2, b + o, first:first + GROUP, :], start=True, stop=True)
                else:
                    for s in range(2):
                        c = 2 * quad + s
                        last = nc.tensor.matmul(psum[:, g % 2, s * 2 * keys:(s + 1) * 2 * keys], qT[:, c, rows],
                                                keysT[:, c, b + o, :, :], start=True, stop=True)
                last.then_inc(sems["scored"], 1)

            def turn(b, o, g):
                pe.wait_ge(sems["probs"], count(b, o, STEPS, g + 1))
                pe.wait_ge(sems["pt_out"], count(b, o, STEPS, g - 1))
                for h in range(GROUP):
                    last = nc.tensor.transpose(psum[0:keys, 2 + g % 2, h * P:(h + 1) * P],
                                               probs[g % 2][:, h, :], ident[:])
                last.then_inc(sems["turned"], 1)

            def sums(b, o, g):
                quad = g % GROUPS
                pe.wait_ge(sems["pt_out"], count(b, o, STEPS, g + 1))
                pe.wait_ge(sems["normed"], count(b, o, STEPS, g - 1))
                for h in range(GROUP):
                    last = nc.tensor.matmul(psum[:, 4 + g % 2, h * (hd + 1):(h + 1) * (hd + 1)],
                                            probsT[g % 2][:, h * P:(h + 1) * P],
                                            values[:, b + o, quad * GROUP + h, :], start=True, stop=True)
                last.then_inc(sems["summed"], 1)

            def turn_sums(b, tile, end):
                pe.wait_ge(sems["normed"], count(b, 0, STEPS, (tile + 1) * GROUPS))
                for j in range(AT):
                    bank = at_spare(pe, b, 0, first_left + tile * (AT + 1) + j, end)
                    per = NC // AT
                    for q in range(per):
                        c = j * per + q
                        last = nc.tensor.transpose(
                            bank[:, q * P:(q + 1) * P],
                            att[tile][:].rearrange("p h d -> p (h d)")[:, c * P:(c + 1) * P], ident[:])
                    last.then_inc(sems["att_turned"], 1)

            def output(b, tile, end):
                pe.wait_ge(sems["left"], count(b, 0, LEFT, tile * (AT + 1) + AT + CREDIT))
                bank = at_spare(pe, b, 0, first_left + tile * (AT + 1) + AT, end)
                for c in range(NC):
                    last = nc.tensor.matmul(bank[:, 0:D], attT[tile][:, c, :], wo[:, c, :],
                                            start=(c == 0), stop=(c == NC - 1))
                last.then_inc(sems["y_ready"], 1)

            def prepare(b, o):
                for j in range(NQ):
                    queries(b, o, j)
                if own:
                    query_squares(b, o)

            def slot(b, s, end):
                item(scores, b, s, SCORES, end)
                if 0 <= s < len(Q_SLOTS) and not end:
                    for j in Q_SLOTS[s]:
                        queries(b, 1, j)
                if own and s == SQ_SLOT and not end:
                    query_squares(b, 1)
                item(turn, b, s, TURN, end)
                item(sums, b, s, SUMS, end)
                for tile in range(TPB):
                    if s == TURN_SLOT[tile]:
                        turn_sums(b, tile, end)
                    if s == OUT_SLOT[tile]:
                        output(b, tile, end)

            pe.sem_inc(sems["att_turned"], CREDIT)
            pe.wait_ge(sems["loaded"], 16 * len(loads))
            stream(pe, prepare, slot)

        @block.scalar
        def _(act):
            def queries_out(b, o, j):
                act.wait_ge(sems["q_ready"], count(b, o, NQ, j + 1))
                if own:
                    act.wait_ge(sems["scored"], count(b, o, STEPS, j + 1 - GROUPS))
                    both = spare(j).rearrange("p (c s) -> p c s", c=2)
                    nc.scalar.activation(q2[:, 2 * j:2 * j + 2, :], both, ACT.Square)
                    nc.scalar.activation(qT[:, 2 * j:2 * j + 2, :], both, ACT.Copy,
                                         scale=q_scale[:]).then_inc(sems["q_out"], 1)
                    return
                if rope:
                    act.wait_ge(sems["q_done"], count(b, o, 2, 0))
                for s in range(2):
                    c = (2 * j + s) % NC
                    if not rope:
                        read = GROUPS // NC * (s + 1) if hd == 16 else j + 1
                        act.wait_ge(sems["scored"], count(b, o, STEPS, read - GROUPS))
                    turned = rope and j >= NQ // 2
                    dst = (qr if turned else q_raw) if rope else qT
                    last = nc.scalar.activation(dst[:, c, :], spare(j)[:, s * SEQ:(s + 1) * SEQ], ACT.Identity,
                                                bias=(bqr if turned else bq)[:, c:c + 1])
                last.then_inc(sems["q_out"], 1)

            def exps(b, o, g):
                act.wait_ge(sems["shift"], count(b, o, STEPS, g + 1))
                act.wait_ge(sems["turned"], count(b, o, STEPS, g - 1))
                nc.scalar.activation(probs[g % 2][:], shifted[g % 2][:], ACT.Exp,
                                     scale=cfg["scale"]).then_inc(sems["probs"], 1)

            def turned_out(b, o, g):
                act.wait_ge(sems["turned"], count(b, o, STEPS, g + 1))
                act.wait_ge(sems["summed"], count(b, o, STEPS, g - 1))
                nc.scalar.activation(probsT[g % 2][:], psum[0:keys, 2 + g % 2, :], ACT.Copy).then_inc(
                    sems["pt_out"], 1)

            def prepare(b, o):
                for j in range(NQ):
                    queries_out(b, o, j)

            queries_late = hd == 16 and not rope

            def slot(b, s, end):
                item(exps, b, s, EXPS, end)
                if queries_late:
                    item(turned_out, b, s, TURN, end)
                if 0 <= s < len(Q_SLOTS) and not end:
                    for j in Q_SLOTS[s]:
                        queries_out(b, 1, j)
                if not queries_late:
                    item(turned_out, b, s, TURN, end)

            act.wait_ge(sems["loaded"], 16 * len(loads))
            stream(act, prepare, slot)
            if own:
                act.wait_ge(sems["shift_done"], 1)
                for q in range(QUADS):
                    for tile in range(4 * q, 4 * q + 4):
                        last = nc.scalar.activation(y_all[:, tile, :], y_all[:, tile, :], ACT.Identity,
                                                    scale=env["rstd"][:, tile:tile + 1],
                                                    bias=shift_by[:, tile:tile + 1])
                    last.then_inc(sems["applied"], 1)

        if own:
            @block.gpsimd
            def _(pool):
                with pool.Fori(0, NBATCH) as bi:
                    pool.wait_ge(sems["sq_out"], bi + 1)
                    nc.gpsimd.tensor_tensor(qrn[:].rearrange("p t h -> p (t h)"), qss[:].rearrange("p t h -> p (t h)"),
                                            env["half32"][:], ALU.pow).then_inc(sems["q_inverted"], 1)
                pool.wait_ge(sems["var_done"], 1)
                nc.gpsimd.tensor_tensor(env["rstd"][:], env["var"][:], env["half"][:], ALU.pow).then_inc(
                    sems["rstd_done"], 1)
                for q in range(QUADS):
                    tiles = slice(4 * q, 4 * q + 4)
                    pool.wait_ge(sems["applied"], q + 1)
                    nc.gpsimd.tensor_tensor(y_all[:, tiles, :], y_all[:, tiles, :],
                                            t["gain"][:].unsqueeze(1).to_broadcast([P, 4, D]), ALU.mult).then_inc(
                                                sems["gained"], 1)

        @block.vector
        def _(dve):
            dve.sem_inc(sems["left"], CREDIT)
            step = Step(dve, sems["chain"], per=STEPS * (3 if mask else 2) + (2 if rope else 0))
            dve.wait_ge(sems["loaded"], 16 * len(loads))

            def soft(b, o, g):
                tile, quad = divmod(g, GROUPS)
                s3 = psum[:, g % 2, 0:GROUP * keys].rearrange("p (h k) -> p h k", k=keys)
                dst, mx = shifted[g % 2], top[g % 2]
                if own and g == 0:
                    dve.wait_ge(sems["q_inverted"], count(b, o, 1, 1))
                dve.wait_ge(sems["scored"], count(b, o, STEPS, g + 1))
                dve.wait_ge(sems["probs"], count(b, o, STEPS, g - 1))
                source = dst[:]
                if own:
                    ins = nc.vector.tensor_tensor(
                        dst[:], s3, qrn[:, tile, quad * GROUP:(quad + 1) * GROUP].unsqueeze(2).to_broadcast(wide),
                        ALU.mult)
                elif mask == "given":
                    row = t["mask_mul"][:, bass.ds((b + o) * TPB + tile, 1), :].to_broadcast(wide)
                    ins = nc.vector.tensor_tensor(dst[:], s3, row, ALU.mult)
                elif mask == "window":
                    ins = nc.vector.tensor_tensor(dst[:], s3, window[:, tile, :].unsqueeze(1).to_broadcast(wide),
                                                  ALU.add)
                else:
                    ins, source = None, s3
                if ins is not None:
                    ins.then_inc(sems["s_free"], 1)
                    dve.wait_ge(sems["s_free"], count(b, o, STEPS, g + 1))
                if mask == "given":
                    row = t["mask_add"][:, bass.ds((b + o) * TPB + tile, 1), :].to_broadcast(wide)
                    step.then(nc.vector.tensor_tensor(dst[:], dst[:], row, ALU.add))
                step.then(nc.vector.tensor_reduce(mx[:], source, AX.X, ALU.max))
                nc.vector.tensor_tensor(dst[:], source, mx[:].unsqueeze(2).to_broadcast(wide),
                                        ALU.subtract).then_inc(sems["shift"], 1)

            def norm(b, o, g):
                tile, quad = divmod(g, GROUPS)
                dve.wait_ge(sems["summed"], count(b, o, STEPS, g + 1))
                if quad == 0:
                    dve.wait_ge(sems["att_turned"], count(b, o, TPB * AT, (tile + 1 - TPB) * AT + CREDIT))
                o3 = psum[:, 4 + g % 2, 0:GROUP * (hd + 1)].rearrange("p (h d) -> p h d", d=hd + 1)
                step.then(nc.vector.reciprocal(inv[g % 2][:], o3[:, :, hd]))
                if mask == "window":
                    step.then(nc.vector.tensor_scalar(inv[g % 2][:], inv[g % 2][:], seen[:, tile:tile + 1], None,
                                                      ALU.mult))
                nc.vector.tensor_tensor(att[tile][:, quad * GROUP:(quad + 1) * GROUP, :], o3[:, :, 0:hd],
                                        inv[g % 2][:].unsqueeze(2).to_broadcast([P, GROUP, hd]),
                                        ALU.mult).then_inc(sems["normed"], 1)

            def copy_turned(b, tile):
                per = NC // AT
                for j in range(AT):
                    dve.wait_ge(sems["att_turned"], count(b, 0, TPB * AT, tile * AT + j + 1 + CREDIT))
                    nc.vector.tensor_copy(attT[tile][:, j * per:(j + 1) * per, :],
                                          spare(first_left + tile * (AT + 1) + j)[:, 0:per * P].rearrange(
                                              "p (c s) -> p c s", s=P)).then_inc(sems["left"], 1)

            def add_output(b, tile):
                dve.wait_ge(sems["y_ready"], count(b, 0, TPB, tile + 1))
                y = spare(first_left + tile * (AT + 1) + AT)[:, 0:D]
                where = bass.ds(b * TPB + tile, 1)
                if own:
                    nc.vector.tensor_scalar(y_all[:, where, :], y.unsqueeze(1), 1.0, None, ALU.mult)
                    nc.vector.bn_stats(env["stats"][:, where, :].rearrange("p o c -> p (o c)"), y).then_inc(
                        sems["left"], 1)
                else:
                    nc.vector.scalar_tensor_tensor(x[:, where, :], y.unsqueeze(1), gate, x[:, where, :],
                                                   ALU.mult, ALU.add).then_inc(sems["left"], 1)

            def turn_positions(b, o):
                table = lambda v: v[:].unsqueeze(1).to_broadcast([P, NC, SEQ])
                dve.wait_ge(sems["q_out"], count(b, o, NQ, NQ))
                step.did(nc.vector.tensor_tensor(q_raw[:], q_raw[:], table(cos), ALU.mult))
                step.then(nc.vector.tensor_tensor(qr[:], qr[:], table(sin), ALU.mult))
                for c in range(NC):
                    dve.wait_ge(sems["scored"], count(b, o, STEPS, GROUPS // NC * (c + 1) - GROUPS))
                    nc.vector.tensor_tensor(qT[:, c, :], q_raw[:, c, :], qr[:, c, :], ALU.add).then_inc(
                        sems["q_done"], 1)

            def sum_squares(b, o):
                dve.wait_ge(sems["sq_ready"], count(b, o, 1, 1))
                nc.vector.tensor_scalar(qss[:].rearrange("p t h -> p (t h)"), spare(NQ)[:, 0:TPB * HEADS], 1e-24,
                                        None, ALU.max).then_inc(sems["sq_out"], 1)

            def prepare(b, o):
                if rope:
                    turn_positions(b, o)
                if own:
                    sum_squares(b, o)

            def slot(b, s, end):
                if own and s == SQ_SLOT and not end:
                    sum_squares(b, 1)
                item(soft, b, s, SCORES, end)
                if rope and s == 0 and not end:
                    turn_positions(b, 1)
                done = [tile for tile in range(TPB) if s == STATS_SLOT[tile] and not own]
                for tile in done:
                    dve.wait_ge(sems["left"], count(b, 0, LEFT, (tile + 1) * (AT + 1) + CREDIT))
                item(norm, b, s, SUMS, end)
                for tile in done:
                    where = bass.ds(b * TPB + tile, 1)
                    nc.vector.bn_stats(env["stats"][:, where, :].rearrange("p o c -> p (o c)"),
                                       x[:, where, :].rearrange("p o d -> p (o d)"))
                for tile in range(TPB):
                    if s == TURN_SLOT[tile]:
                        copy_turned(b, tile)
                    if s == OUT_SLOT[tile]:
                        add_output(b, tile)

            stream(dve, prepare, slot, step)
            if own:
                dve.wait_ge(sems["left"], NBATCH * LEFT + CREDIT)
                emit_statistics(nc, dve, y_all, env, sems["stats"], sems["var_done"], ready=True)
                dve.wait_ge(sems["rstd_done"], 1)
                nc.vector.scalar_tensor_tensor(shift_by[:], env["mv"][:, :, 0], -1.0, env["rstd"][:], ALU.mult,
                                               ALU.mult).then_inc(sems["shift_done"], 1)
                for q in range(QUADS):
                    tiles = slice(4 * q, 4 * q + 4)
                    dve.wait_ge(sems["gained"], q + 1)
                    nc.vector.tensor_tensor(x[:, tiles, :], x[:, tiles, :], y_all[:, tiles, :], ALU.add).then_inc(
                        sems["added"], 1)
                    dve.wait_ge(sems["added"], q + 1)
                    for tile in range(4 * q, 4 * q + 4):
                        nc.vector.bn_stats(env["stats"][:, tile, :], x[:, tile, :])


def _chunks(w):
    r, c = w.shape
    return np.ascontiguousarray(w.reshape(r // P, P, c).transpose(1, 0, 2))


def _units(w1, w2, b1=None):
    out = [np.stack([_chunks(w) for w in w1]), np.stack([_chunks(w) for w in w2])]
    if b1 is not None:
        out.append(np.ascontiguousarray(np.stack([b.reshape(UNIT // P, P).T for b in b1], axis=1)))
    return out


def layout(inputs):
    a = {k: np.asarray(v) for k, v in inputs.items()}
    out = {"x": a["x"], "g_xattn": a["g_xattn"], "g_ffn": a["g_ffn"]}
    ctx = a["ctx_1024"]
    out["ctxT"] = _chunks(np.ascontiguousarray(ctx.reshape(-1, D).T))
    out["ctx"] = np.ascontiguousarray(ctx.transpose(1, 0, 2))
    out["mask"] = np.ascontiguousarray(
        a["mask_BxSxS2_bf1"].view(np.uint8).reshape(TILES, P, CTX).transpose(1, 0, 2))
    out["ident"] = np.eye(P, dtype=np.float32)
    out["rank"] = np.ascontiguousarray(np.broadcast_to((8 - np.arange(8)).astype(np.float32), (P, TILES, 8)))
    w1 = [*a["L0_ffn_rw1"], a["L0_ffn_sw1"]]
    w2 = [*a["L0_ffn_rw2"], a["L0_ffn_sw2"]]
    out["f0_w1"], out["f0_w2"], out["f0_b1"] = _units(w1, w2, [*a["L0_ffn_rb1"], a["L0_ffn_sb1"]])
    out["f0_b2"] = np.concatenate([a["L0_ffn_rb2"], a["L0_ffn_sb2"][None]])
    out["f0_wr"], out["f0_rb"] = _chunks(a["L0_ffn_router_w"]), a["L0_ffn_router_b"]
    halves = [slice(0, UNIT), slice(UNIT, 2 * UNIT)]
    out["f1_w1"], out["f1_w2"], out["f1_b1"] = _units(
        [w[:, h] for w in a["L1_ffn_W1"] for h in halves], [w[h] for w in a["L1_ffn_W2"] for h in halves],
        [b[h] for b in a["L1_ffn_b1"] for h in halves])
    out["f1_b2"], out["f1_wr"], out["f1_rb"] = a["L1_ffn_b2"], _chunks(a["L1_ffn_Wr"]), a["L1_ffn_br"]
    wi, wo = a["L2_ffn_wi_W"].T, a["L2_ffn_wo_W"].T
    out["f2_w1"], out["f2_w2"], out["f2_b1"] = _units(
        [wi[:, h] for h in halves], [wo[h] for h in halves], [a["L2_ffn_wi_b"][h] for h in halves])
    out["f2_b2"], out["f2_rb"] = a["L2_ffn_wo_b"][None], a["L2_ffn_gate_b"]
    out["f2_wr"] = _chunks(np.concatenate([a["L2_ffn_gate_W"], a["L2_ffn_lora_A"].reshape(-1, D)]).T)
    lb = a["L2_ffn_lora_B"].transpose(0, 2, 1).reshape(32, 2, UNIT)
    out["f2_lb"] = np.ascontiguousarray(lb)
    w1 = [np.concatenate([p, q]).T for p, q in zip(a["L3_ffn_w1"], a["L3_ffn_w3"])]
    w2 = [w.T for w in a["L3_ffn_w2"]]
    for h in (slice(0, D), slice(D, 2 * D)):
        w1.append(np.concatenate([a["L3_ffn_sw1"][h], a["L3_ffn_sw3"][h]]).T)
        w2.append(a["L3_ffn_sw2"][:, h].T)
    out["f3_w1"], out["f3_w2"] = _units(w1, w2)
    out["f3_wr"], out["f3_rb"] = _chunks(a["L3_ffn_gate_w"].T), a["L3_ffn_gate_bias"]
    for n in range(4):
        c, pre = ATTN[n], f"L{n}_xattn_"
        w = {k: a[pre + k] for k in ("Wq", "Wk", "Wv", "Wo") if pre + k in a}
        if n == 1:
            w["Wk"], w["Wv"] = a[pre + "Wkv"][:, :HEADS * c["hd"]], a[pre + "Wkv"][:, HEADS * c["hd"]:]
        if n in (0, 3):
            w = {k: v.T for k, v in w.items()}
        for k, v in w.items():
            out[f"a{n}_w{k[1]}"] = _chunks(v)
        if n != 1:
            for k in ("bq", "bk"):
                out[f"a{n}_{k}"] = np.ascontiguousarray(a[pre + k].reshape(-1, P).T)
            out[f"a{n}_bv"], out[f"a{n}_bo"] = a[pre + "bv"], a[pre + "bo"]
    per_feature = lambda g, b: np.ascontiguousarray(np.stack([g, b]).reshape(2, DC, P).transpose(2, 0, 1))
    out["a1_ln_in"] = per_feature(a["L1_xattn_ln_in_g"], a["L1_xattn_ln_in_b"])
    out["a1_ln_ctx"] = per_feature(a["L1_xattn_ln_ctx_g"], a["L1_xattn_ln_ctx_b"])
    out["a1_ln_out"] = np.stack([a["L1_xattn_ln_out_g"], a["L1_xattn_ln_out_b"]])
    out["a1_k_scale"] = np.ascontiguousarray(np.tile(a["L1_xattn_k_scale"], 2)[:, None])
    out["a1_q_scale"] = np.ascontiguousarray(np.tile(a["L1_xattn_q_scale"], 2)[:, None])
    null = a["L1_xattn_null_kv"]
    out["a1_null"] = np.ascontiguousarray(np.broadcast_to(null[0], (1, 1, HEADS, 64)))
    out["a1_null_v"] = np.ascontiguousarray(np.broadcast_to(null[1], (1, NBATCH, HEADS, 64)))
    partner = (np.arange(D) // 16) * 16 + (np.arange(D) + 8) % 16
    for k in "qk":
        out[f"a3_w{k}r"] = _chunks(a[f"L3_xattn_W{k}"][partner].T)
        out[f"a3_b{k}r"] = np.ascontiguousarray(a[f"L3_xattn_b{k}"][partner].reshape(-1, P).T)
    k = np.arange(P)
    out["before"] = (k[:, None] < k[None, :]).astype(np.float32)
    out["ones"] = np.ones((P, P), np.float32)
    out["thresholds"] = np.ascontiguousarray(np.broadcast_to((BLOCK * k[:8]).astype(np.float32), (P, 8, 8)))
    out["up_to"] = np.ascontiguousarray(np.broadcast_to(
        (k[:8, None] >= k[None, :8]).astype(np.float32), (P, 8, 8)))
    out["block_index"] = np.ascontiguousarray(np.broadcast_to(
        k[:BLOCKS, None].astype(np.float32), (P, BLOCKS, 8)))
    f = np.arange(P)
    out["own_rows"] = (f[:, None] // 16 == np.arange(8)[None]).astype(np.float32)
    out["of_head"] = (f[:, None] // 64 == np.arange(2)[None]).astype(np.float32)
    freq = (1.0 / np.float32(10000.0) ** (np.arange(8, dtype=np.float32) / np.float32(8))).astype(np.float32)
    angle = np.arange(SEQ, dtype=np.float32)[None, :] * freq[f % 8][:, None]
    out["cos"] = np.cos(angle).astype(np.float32)
    out["sin"] = (np.sin(angle) * np.where(f % 16 < 8, -1.0, 1.0)[:, None]).astype(np.float32)
    tok, key = np.arange(SEQ).reshape(TPB, P).T[:, :, None], np.arange(CTX)[None, None]
    hidden = (key > tok) | (key < tok - 128)
    out["window"] = np.where(hidden, np.float32(MASKED), np.float32(0))
    out["seen"] = (~hidden.all(-1)).astype(np.float32)
    return {k: np.ascontiguousarray(v) for k, v in out.items()}


STAGES = [("a", 0), ("f", 0), ("a", 1), ("f", 1), ("a", 2), ("f", 2), ("a", 3), ("f", 3)]


def kernel(**inputs):
    import concourse.bacc as bacc
    from concourse.bass_utils import run_bass_kernel_spmd

    nc = bacc.Bacc("TRN2", target_bir_lowering=False, num_devices=1)
    arrays, dram = {}, {}
    for name, v in layout(inputs).items():
        arrays[f"in_{name}"] = v
        dram[name] = nc.dram_tensor(f"in_{name}", v.shape, mybir.dt.from_np(v.dtype), kind="ExternalInput").ap()
    out = nc.dram_tensor("out", (NBATCH, SEQ, D), F32, kind="ExternalOutput").ap()
    build(nc, dram, out, STAGES)
    return run_bass_kernel_spmd(nc, [arrays], core_ids=[0]).results[0]["out"]
```
